# Optimizing a Trainium2 kernel written in Bass

```python
import numpy as np
import jax
import jax.numpy as jnp

def _softmax(x, axis=-1):
    return jax.nn.softmax(x, axis=axis)

def _gelu(x):
    return jax.nn.gelu(x, approximate=True)

def _silu(x):
    return jax.nn.silu(x)

def _sigmoid(x):
    return jax.nn.sigmoid(x)

def _layernorm(x, axis=-1, eps=1e-05):
    m = jnp.mean(x, axis=axis, keepdims=True)
    v = jnp.var(x, axis=axis, keepdims=True)
    return (x - m) / jnp.sqrt(v + eps)

def _scatter_add(tgt, idx, src, axis=0):
    return tgt.at[idx].add(src)

def _segment_sum(src, seg, n):
    return jax.ops.segment_sum(src, seg, n)
kernel_name = 'mk_flamingo_gated_d2_seqx_r8_6f0e6f'

def setup_inputs(seed: int=0):
    np.random.seed(seed)
    _w = jnp.asarray

    def _rec_inputs():
        import jax
        import jax.numpy as jnp
        _rk = jax.random.key(seed)
        x = -0.0002928 + 1 * jax.random.normal(jax.random.fold_in(_rk, 1), (16, 128, 256), jnp.float32)
        _lenS = 128 - jax.random.randint(jax.random.fold_in(_rk, 7), (16,), 0, max(1, 128 // 4) + 1, jnp.int32)
        _lenS2 = 128 - jax.random.randint(jax.random.fold_in(_rk, 8), (16,), 0, max(1, 128 // 4) + 1, jnp.int32)
        _ctx_2048P = jax.random.normal(jax.random.fold_in(_rk, 11), (16, 16, 256), jnp.float32)
        _ctx_2048c = jax.random.dirichlet(jax.random.fold_in(_rk, 511), 0.3 * jnp.ones((16,), jnp.float32), (16, 128))
        _ctx_2048t = jnp.einsum('bsk,bkd->bsd', _ctx_2048c, _ctx_2048P)
        _ctx_2048t = _ctx_2048t * jax.lax.rsqrt(jnp.mean(jnp.square(_ctx_2048t)) + 1e-12) * 0.953939
        ctx_2048 = -1.39393e-06 + 0.999914 * (_ctx_2048t + 0.3 * jax.random.normal(jax.random.fold_in(_rk, 611), (16, 128, 256), jnp.float32))
        _validS = jnp.arange(128)[None, :] < _lenS[:, None]
        _validS2 = jnp.arange(128)[None, :] < _lenS2[:, None]
        _causal = jnp.tril(jnp.ones((128, 128), dtype=bool))
        mask_Bx1x2048_fk1 = jnp.where(jnp.ones((16, 1, 256), dtype=bool), 1.0, 0.0).astype(jnp.float32)
        _g = jax.random.normal(jax.random.fold_in(_rk, 9001), (2, 2), jnp.float32)
        _g = jnp.sign(_g) * jnp.maximum(jnp.abs(_g), 1.0) + (_g == 0) * 1.0
        g_xattn = _g[0]
        g_ffn = _g[1]
        return (x, ctx_2048, mask_Bx1x2048_fk1, g_xattn, g_ffn)
    x, ctx_2048, mask_Bx1x2048_fk1, g_xattn, g_ffn = _rec_inputs()

    def _L0_xattn_setup():
        import math
        import jax, jax.numpy as jnp
        import numpy as np
        SIZE = 128
        HEADS = 16
        HEAD_DIM = SIZE // HEADS
        B, T, S = (2, 256, 256)
        NEG = 1000000.0
        key = jax.random.key(seed)
        ks = jax.random.split(key, 10)
        target = jax.random.normal(ks[0], (B, SIZE, T), dtype=jnp.float32)
        source = jax.random.normal(ks[1], (B, SIZE, S), dtype=jnp.float32)
        target_mask = (jax.random.uniform(ks[2], (B, 1, T)) > 0.1).astype(jnp.float32)
        source_mask = (jax.random.uniform(ks[3], (B, 1, S)) > 0.1).astype(jnp.float32)
        scale = 1.0 / math.sqrt(SIZE)
        Wq = jax.random.normal(ks[4], (SIZE, SIZE), dtype=jnp.float32) * scale
        Wk = jax.random.normal(ks[5], (SIZE, SIZE), dtype=jnp.float32) * scale
        Wv = jax.random.normal(ks[6], (SIZE, SIZE), dtype=jnp.float32) * scale
        bq = jax.random.normal(ks[7], (SIZE,), dtype=jnp.float32) * 0.01
        bk = jax.random.normal(ks[8], (SIZE,), dtype=jnp.float32) * 0.01
        bv = jax.random.normal(ks[9], (SIZE,), dtype=jnp.float32) * 0.01
        return {'target': target, 'source': source, 'target_mask': target_mask, 'source_mask': source_mask, 'Wq': Wq, 'bq': bq, 'Wk': Wk, 'bk': bk, 'Wv': Wv, 'bv': bv}
    _L0_xattn_all = _L0_xattn_setup()
    _L0_xattn_in = {k: v for k, v in _L0_xattn_all.items() if k in ('Wq', 'bq', 'Wk', 'bk', 'Wv', 'bv')}
    del _L0_xattn_all

    def _L0_ffn_setup():
        import jax, jax.numpy as jnp
        import numpy as np
        E = 8
        TOP_K = 2
        H = 256
        I_MOE = 176
        I_SH = 704
        B, S = (2, 256)

        def _moe_forward(hidden_states, router_weight, gate_up_proj, down_proj, sh_gate_w, sh_up_w, sh_down_w, shared_gate_w):
            b, s, h = hidden_states.shape
            x = hidden_states.reshape(-1, h)
            shared = jnp.einsum('ti,hi->th', jax.nn.silu(x @ sh_gate_w.T) * (x @ sh_up_w.T), sh_down_w)
            logits = x @ router_weight.T
            probs = jax.nn.softmax(logits.astype(jnp.float32), axis=-1)
            top_v, top_i = jax.lax.top_k(probs, TOP_K)
            top_v = top_v / top_v.sum(axis=-1, keepdims=True)
            combine = (jax.nn.one_hot(top_i, E, dtype=top_v.dtype) * top_v[..., None]).sum(axis=1)
            out = jnp.zeros_like(x)
            for e in range(E):
                gu = x @ gate_up_proj[e].T
                gate, up = (gu[:, :I_MOE], gu[:, I_MOE:])
                cur = jax.nn.silu(gate) * up @ down_proj[e].T
                out = out + cur * combine[:, e:e + 1]
            out = out + jax.nn.sigmoid(x @ shared_gate_w.T) * shared
            return out.reshape(b, s, h)
        key = jax.random.key(seed)
        ks = jax.random.split(key, 8)
        scale = 0.02
        return {'hidden_states': jax.random.normal(ks[0], (B, S, H), dtype=jnp.float32), 'router_weight': jax.random.normal(ks[1], (E, H), dtype=jnp.float32) * scale, 'gate_up_proj': jax.random.normal(ks[2], (E, 2 * I_MOE, H), dtype=jnp.float32) * scale, 'down_proj': jax.random.normal(ks[3], (E, H, I_MOE), dtype=jnp.float32) * scale, 'sh_gate_w': jax.random.normal(ks[4], (I_SH, H), dtype=jnp.float32) * scale, 'sh_up_w': jax.random.normal(ks[5], (I_SH, H), dtype=jnp.float32) * scale, 'sh_down_w': jax.random.normal(ks[6], (H, I_SH), dtype=jnp.float32) * scale, 'shared_gate_w': jax.random.normal(ks[7], (1, H), dtype=jnp.float32) * scale}
    _L0_ffn_all = _L0_ffn_setup()
    _L0_ffn_in = {k: v for k, v in _L0_ffn_all.items() if k in ('router_weight', 'gate_up_proj', 'down_proj', 'sh_gate_w', 'sh_up_w', 'sh_down_w', 'shared_gate_w')}
    del _L0_ffn_all

    def _L1_xattn_setup():
        import jax, jax.numpy as jnp
        import numpy as np
        HIDDEN = 256
        N_HEADS = 16
        N_KV_HEADS = 4
        HEAD_DIM = 128
        EPS = 1e-06

        def rms_norm(x, w, eps=EPS):
            xf = x.astype(jnp.float32)
            var = jnp.mean(xf * xf, axis=-1, keepdims=True)
            return w * (xf * jax.lax.rsqrt(var + eps)).astype(x.dtype)
        key = jax.random.key(seed)
        ks = jax.random.split(key, 8)
        B, S, S_ENC = (4, 256, 128)
        inner = N_HEADS * HEAD_DIM
        kv_dim = N_KV_HEADS * HEAD_DIM
        s = 0.02
        return {'hidden_states': jax.random.normal(ks[0], (B, S, HIDDEN), jnp.float32), 'encoder_hidden_states': jax.random.normal(ks[1], (B, S_ENC, HIDDEN), jnp.float32), 'Wq': jax.random.normal(ks[2], (HIDDEN, inner), jnp.float32) * s, 'Wk': jax.random.normal(ks[3], (HIDDEN, kv_dim), jnp.float32) * s, 'Wv': jax.random.normal(ks[4], (HIDDEN, kv_dim), jnp.float32) * s, 'Wo': jax.random.normal(ks[5], (inner, HIDDEN), jnp.float32) * s, 'q_norm_w': jnp.ones((HEAD_DIM,), jnp.float32), 'k_norm_w': jnp.ones((HEAD_DIM,), jnp.float32)}
    _L1_xattn_all = _L1_xattn_setup()
    _L1_xattn_in = {k: v for k, v in _L1_xattn_all.items() if k in ('Wq', 'Wk', 'Wv', 'Wo', 'q_norm_w', 'k_norm_w')}
    del _L1_xattn_all

    def _L1_ffn_setup():
        import jax, jax.numpy as jnp
        import numpy as np
        EPS = 1e-05
        RMS_EPS = 1e-06

        def _rmsnorm(x):
            return x * jax.lax.rsqrt(jnp.mean(x * x, axis=-1, keepdims=True) + RMS_EPS)

        def _act_quant(x):
            scale = 127.0 / jnp.clip(jnp.max(jnp.abs(x), axis=-1, keepdims=True), EPS)
            q = jnp.round(jnp.clip(x * scale, -128.0, 127.0)) / scale
            return x + jax.lax.stop_gradient(q - x)

        def _weight_quant(w):
            scale = 1.0 / jnp.clip(jnp.mean(jnp.abs(w)), EPS)
            q = jnp.round(jnp.clip(w * scale, -1.0, 1.0)) / scale
            return w + jax.lax.stop_gradient(q - w)

        def _bitlinear(x, w):
            xq = _act_quant(_rmsnorm(x))
            wq = _weight_quant(w)
            return jnp.einsum('bsi,oi->bso', xq, wq)
        key = jax.random.key(seed)
        k1, k2, k3, k4 = jax.random.split(key, 4)
        B, S, D, F = (2, 256, 256, 1024)
        x = jax.random.normal(k1, (B, S, D), dtype=jnp.float32)
        w_gate = jax.random.normal(k2, (F, D), dtype=jnp.float32) * 0.02
        w_up = jax.random.normal(k3, (F, D), dtype=jnp.float32) * 0.02
        w_down = jax.random.normal(k4, (D, F), dtype=jnp.float32) * 0.02
        return {'x': x, 'w_gate': w_gate, 'w_up': w_up, 'w_down': w_down}
    _L1_ffn_all = _L1_ffn_setup()
    _L1_ffn_in = {k: v for k, v in _L1_ffn_all.items() if k in ('w_gate', 'w_up', 'w_down')}
    del _L1_ffn_all
    return {'x': x, 'ctx_2048': ctx_2048, 'mask_Bx1x2048_fk1': mask_Bx1x2048_fk1, 'g_xattn': g_xattn, 'g_ffn': g_ffn, 'L0_xattn_Wq': _L0_xattn_in['Wq'], 'L0_xattn_bq': _L0_xattn_in['bq'], 'L0_xattn_Wk': _L0_xattn_in['Wk'], 'L0_xattn_bk': _L0_xattn_in['bk'], 'L0_xattn_Wv': _L0_xattn_in['Wv'], 'L0_xattn_bv': _L0_xattn_in['bv'], 'L0_ffn_router_weight': _L0_ffn_in['router_weight'], 'L0_ffn_gate_up_proj': _L0_ffn_in['gate_up_proj'], 'L0_ffn_down_proj': _L0_ffn_in['down_proj'], 'L0_ffn_sh_gate_w': _L0_ffn_in['sh_gate_w'], 'L0_ffn_sh_up_w': _L0_ffn_in['sh_up_w'], 'L0_ffn_sh_down_w': _L0_ffn_in['sh_down_w'], 'L0_ffn_shared_gate_w': _L0_ffn_in['shared_gate_w'], 'L1_xattn_Wq': _L1_xattn_in['Wq'], 'L1_xattn_Wk': _L1_xattn_in['Wk'], 'L1_xattn_Wv': _L1_xattn_in['Wv'], 'L1_xattn_Wo': _L1_xattn_in['Wo'], 'L1_xattn_q_norm_w': _L1_xattn_in['q_norm_w'], 'L1_xattn_k_norm_w': _L1_xattn_in['k_norm_w'], 'L1_ffn_w_gate': _L1_ffn_in['w_gate'], 'L1_ffn_w_up': _L1_ffn_in['w_up'], 'L1_ffn_w_down': _L1_ffn_in['w_down']}

def reference(x, ctx_2048, mask_Bx1x2048_fk1, g_xattn, g_ffn, L0_xattn_Wq, L0_xattn_bq, L0_xattn_Wk, L0_xattn_bk, L0_xattn_Wv, L0_xattn_bv, L0_ffn_router_weight, L0_ffn_gate_up_proj, L0_ffn_down_proj, L0_ffn_sh_gate_w, L0_ffn_sh_up_w, L0_ffn_sh_down_w, L0_ffn_shared_gate_w, L1_xattn_Wq, L1_xattn_Wk, L1_xattn_Wv, L1_xattn_Wo, L1_xattn_q_norm_w, L1_xattn_k_norm_w, L1_ffn_w_gate, L1_ffn_w_up, L1_ffn_w_down):
    import jax
    import jax.numpy as jnp

    def _L0_xattn_ref(target, source, target_mask, source_mask, Wq, bq, Wk, bk, Wv, bv):
        import math
        import jax, jax.numpy as jnp
        import numpy as np
        SIZE = 128
        HEADS = 16
        HEAD_DIM = SIZE // HEADS
        B, T, S = (2, 256, 256)
        NEG = 1000000.0
        b, _, t = target.shape
        s = source.shape[-1]
        q = jnp.einsum('oc,bct->bot', Wq, target) + bq[None, :, None]
        k = jnp.einsum('oc,bcs->bos', Wk, source) + bk[None, :, None]
        v = jnp.einsum('oc,bcs->bos', Wv, source) + bv[None, :, None]
        q = q.reshape(b, HEADS, HEAD_DIM, t)
        k = k.reshape(b, HEADS, HEAD_DIM, s)
        v = v.reshape(b, HEADS, HEAD_DIM, s)
        dot = jnp.einsum('bhdt,bhds->bhts', q, k) / math.sqrt(HEAD_DIM)
        mask = target_mask[:, :, :, None] * source_mask[:, :, None, :]
        dot = mask * dot - (1.0 - mask) * NEG
        amap = jax.nn.softmax(dot, axis=-1) * mask
        out = jnp.einsum('bhts,bhds->bhdt', amap, v)
        return out.reshape(b, HEADS * HEAD_DIM, t)

    def _L0_ffn_ref(hidden_states, router_weight, gate_up_proj, down_proj, sh_gate_w, sh_up_w, sh_down_w, shared_gate_w):
        import jax, jax.numpy as jnp
        import numpy as np
        E = 8
        TOP_K = 2
        H = 256
        I_MOE = 176
        I_SH = 704
        B, S = (2, 256)

        def _moe_forward(hidden_states, router_weight, gate_up_proj, down_proj, sh_gate_w, sh_up_w, sh_down_w, shared_gate_w):
            b, s, h = hidden_states.shape
            x = hidden_states.reshape(-1, h)
            shared = jnp.einsum('ti,hi->th', jax.nn.silu(x @ sh_gate_w.T) * (x @ sh_up_w.T), sh_down_w)
            logits = x @ router_weight.T
            probs = jax.nn.softmax(logits.astype(jnp.float32), axis=-1)
            top_v, top_i = jax.lax.top_k(probs, TOP_K)
            top_v = top_v / top_v.sum(axis=-1, keepdims=True)
            combine = (jax.nn.one_hot(top_i, E, dtype=top_v.dtype) * top_v[..., None]).sum(axis=1)
            out = jnp.zeros_like(x)
            for e in range(E):
                gu = x @ gate_up_proj[e].T
                gate, up = (gu[:, :I_MOE], gu[:, I_MOE:])
                cur = jax.nn.silu(gate) * up @ down_proj[e].T
                out = out + cur * combine[:, e:e + 1]
            out = out + jax.nn.sigmoid(x @ shared_gate_w.T) * shared
            return out.reshape(b, s, h)
        return _moe_forward(hidden_states, router_weight, gate_up_proj, down_proj, sh_gate_w, sh_up_w, sh_down_w, shared_gate_w)

    def _L1_xattn_ref(hidden_states, encoder_hidden_states, Wq, Wk, Wv, Wo, q_norm_w, k_norm_w):
        import jax, jax.numpy as jnp
        import numpy as np
        HIDDEN = 256
        N_HEADS = 16
        N_KV_HEADS = 4
        HEAD_DIM = 128
        EPS = 1e-06

        def rms_norm(x, w, eps=EPS):
            xf = x.astype(jnp.float32)
            var = jnp.mean(xf * xf, axis=-1, keepdims=True)
            return w * (xf * jax.lax.rsqrt(var + eps)).astype(x.dtype)
        B, S, _ = hidden_states.shape
        S_enc = encoder_hidden_states.shape[1]
        groups = N_HEADS // N_KV_HEADS
        scale = 1.0 / HEAD_DIM ** 0.5
        q = (hidden_states @ Wq).reshape(B, S, N_HEADS, HEAD_DIM)
        k = (encoder_hidden_states @ Wk).reshape(B, S_enc, N_KV_HEADS, HEAD_DIM)
        v = (encoder_hidden_states @ Wv).reshape(B, S_enc, N_KV_HEADS, HEAD_DIM)
        q = rms_norm(q, q_norm_w)
        k = rms_norm(k, k_norm_w)
        k = jnp.repeat(k, groups, axis=2)
        v = jnp.repeat(v, groups, axis=2)
        scores = jnp.einsum('bqhd,bkhd->bhqk', q, k) * scale
        probs = jax.nn.softmax(scores, axis=-1)
        out = jnp.einsum('bhqk,bkhd->bqhd', probs, v)
        out = out.reshape(B, S, N_HEADS * HEAD_DIM)
        return out @ Wo

    def _L1_ffn_ref(x, w_gate, w_up, w_down):
        import jax, jax.numpy as jnp
        import numpy as np
        EPS = 1e-05
        RMS_EPS = 1e-06

        def _rmsnorm(x):
            return x * jax.lax.rsqrt(jnp.mean(x * x, axis=-1, keepdims=True) + RMS_EPS)

        def _act_quant(x):
            scale = 127.0 / jnp.clip(jnp.max(jnp.abs(x), axis=-1, keepdims=True), EPS)
            q = jnp.round(jnp.clip(x * scale, -128.0, 127.0)) / scale
            return x + jax.lax.stop_gradient(q - x)

        def _weight_quant(w):
            scale = 1.0 / jnp.clip(jnp.mean(jnp.abs(w)), EPS)
            q = jnp.round(jnp.clip(w * scale, -1.0, 1.0)) / scale
            return w + jax.lax.stop_gradient(q - w)

        def _bitlinear(x, w):
            xq = _act_quant(_rmsnorm(x))
            wq = _weight_quant(w)
            return jnp.einsum('bsi,oi->bso', xq, wq)
        gate = jax.nn.silu(_bitlinear(x, w_gate))
        up = _bitlinear(x, w_up)
        return _bitlinear(gate * up, w_down)
    x = x + jnp.tanh(g_xattn[0]) * _L0_xattn_ref(_layernorm(x, axis=-1), ctx_2048, mask_Bx1x2048_fk1, mask_Bx1x2048_fk1, L0_xattn_Wq, L0_xattn_bq, L0_xattn_Wk, L0_xattn_bk, L0_xattn_Wv, L0_xattn_bv)
    x = x + jnp.tanh(g_ffn[0]) * _L0_ffn_ref(_layernorm(x, axis=-1), L0_ffn_router_weight, L0_ffn_gate_up_proj, L0_ffn_down_proj, L0_ffn_sh_gate_w, L0_ffn_sh_up_w, L0_ffn_sh_down_w, L0_ffn_shared_gate_w)
    x = x + jnp.tanh(g_xattn[1]) * _L1_xattn_ref(_layernorm(x, axis=-1), ctx_2048, L1_xattn_Wq, L1_xattn_Wk, L1_xattn_Wv, L1_xattn_Wo, L1_xattn_q_norm_w, L1_xattn_k_norm_w)
    x = x + jnp.tanh(g_ffn[1]) * _L1_ffn_ref(_layernorm(x, axis=-1), L1_ffn_w_gate, L1_ffn_w_up, L1_ffn_w_down)
    return x

_drawn_inputs = setup_inputs


def setup_inputs(seed=0):
    import zlib

    import numpy as np

    out = dict(_drawn_inputs(seed))
    spreads = {'g_ffn': (-1.0, 0.6), 'L1_xattn_q_norm_w': (1.0, 0.6), 'L1_xattn_k_norm_w': (1.0, 0.6)}
    factors = {'L0_xattn_bq': 8.0,
     'L0_xattn_bk': 8.0,
     'L0_xattn_bv': 7.287,
     'L0_ffn_router_weight': 6.028,
     'L0_ffn_gate_up_proj': 5.51,
     'L0_ffn_down_proj': 5.512,
     'L0_ffn_sh_gate_w': 4.395,
     'L0_ffn_sh_up_w': 4.367,
     'L0_ffn_sh_down_w': 4.381,
     'L0_ffn_shared_gate_w': 8.0}
    for name, (base, spread) in spreads.items():
        noise = np.random.default_rng([zlib.crc32(name.encode()), seed]).standard_normal(out[name].shape)
        drawn = base * np.exp(spread * noise) if base else spread * noise
        out[name] = jnp.asarray(drawn.astype(out[name].dtype))
    for name, factor in factors.items():
        out[name] = (out[name] * factor).astype(out[name].dtype)
    return out
```

```python
from contextlib import ExitStack

import numpy as np

import concourse.bass as bass
from concourse import mybir

F32 = mybir.dt.float32
F32R = mybir.dt.float32r
BF16 = mybir.dt.bfloat16
ALU = mybir.AluOpType
ACT = mybir.ActivationFunctionType
AX = mybir.AxisListType

B, S, D = 16, 128, 256
P = 128
HEADS0, HD0 = 16, 8
GROUPS, GH = 4, 4
NEG_HI, NEG_LO = 999936.0, 64.0
LN_EPS = 1e-5
CONST_COLS = 11
N_CONST_DMAS = 11


class Batch:

    def __init__(self, number, half, parity):
        self.number, self.half, self.parity = number, half, parity

    def plus(self, n):
        parity = self.parity + n
        return Batch(self.number + n, self.half + parity // 2, parity % 2)


def fixed(n):
    return Batch(n, n // 2, n % 2)


def wait(engine, semaphore, value):
    if isinstance(value, int) and value <= 0:
        return
    engine.wait_ge(semaphore, value)


def paired_loop(engine, first, last, step):
    with engine.Fori(first // 2, last // 2) as half:
        for parity in range(2):
            step(Batch(half * 2 + parity, half, parity))


def attention0(nc, ctx_mem, shared, x, ctx, mask, wq, wk, wv, bq, bk, bv, consts):
    xres, ident, gates = shared["x"], shared["ident"], shared["gates"]

    def sb(name, shape, dt=F32):
        return ctx_mem.enter_context(nc.sbuf_tensor(name, shape, dt))

    def sem(name):
        return shared["semaphores"].enter_context(nc.semaphore(name))

    def ps(name, cols):
        return ctx_mem.enter_context(nc.psum_tensor(name, [P, cols], F32))

    w_sb = sb("a_w", [P, 3, P])
    bias = sb("a_bias", [P, 2])
    bv_row = sb("a_bv_row", [P, P])
    cst = sb("a_consts", [P, CONST_COLS])
    maskb = sb("a_maskb", [P, B, D])
    mask_col = sb("a_mask_col", [P, B, 2])
    stats = sb("a_stats", [P, B, 6])
    mv = sb("a_mv", [P, B, 2])
    rstd = sb("a_rstd", [P, B])
    eps = sb("a_eps", [P, 1])
    cbuf = [sb(f"a_ctx{i}", [P, D]) for i in range(2)]
    mrow = [sb(f"a_mrow{i}", [P, D]) for i in range(2)]
    xn = sb("a_xn", [P, D])
    full = [sb(f"a_full{i}", [P, D]) for i in range(2)]
    split = [sb(f"a_split{i}", [P, 2, D], F32R) for i in range(2)]
    qst = [sb(f"a_qst{i}", [P, GROUPS, D], F32R) for i in range(2)]
    krep = sb("a_krep", [P, GROUPS, D], F32R)
    kst = [sb(f"a_kst{i}", [P, GROUPS, GH, D], F32R) for i in range(2)]
    vt = sb("a_vt", [P, 2, P])
    mcb = sb("a_mcb", [P, 2])
    vst = [sb(f"a_vst{i}", [P, 2, HEADS0, P]) for i in range(2)]
    mx = sb("a_mx", [P, 2, HEADS0])
    probs = [sb(f"a_probs{i}", [P, 2, 2, D]) for i in range(2)]
    sums = sb("a_sums", [P, D])
    outs = sb("a_outs", [P, D])
    rinv = sb("a_rinv", [P, D])
    tmp = sb("a_tmp", [P, D])

    p1 = ps("a_p1", 1024)
    p2 = [ps(f"a_p2{i}", 1024) for i in range(2)]
    pv = ps("a_pv", 512)
    misc = ps("a_misc", 512)

    names = """consts_in stats_done rstd_in rstd_done w_scaled zeroed ones_done ctx_in0 ctx_in1 mrow_in0 mrow_in1
        tanh_done mcb_done xn_ready qk_psum full_done hi_done split_done dist_q0 dist_q1 dist_k q3_krep q3_qst
        kst_dve kst_pool v_psum vt_ready vst_ready p1_ready mx_done mt_ready shift_done p2_ready
        exp_done pv_done evac_done fin_done rin_done tmp_done x_done sums_done""".split()
    s = {n: sem("a_" + n) for n in names}
    x_in = [sem(f"a_x_in{i}") for i in range(4)]

    C_SEL, C_QA, C_QB, C_KA, C_KB = 0, 4, 5, 6, 7

    with nc.Block() as block:

        @block.sync
        def _(sp):
            for i in range(4):
                sp.dma_start(xres[:, 4 * i:4 * i + 4, :],
                             x[4 * i:4 * i + 4].rearrange("b s d -> s b d")).then_inc(x_in[i], 16)
            for dst, src in ((w_sb[:, 0, :], wq), (w_sb[:, 1, :], wk), (w_sb[:, 2, :], wv),
                             (bias[:, 0:1], bq), (bias[:, 1:2], bk), (cst[:], consts),
                             (ident[:], shared["ident_dram"]),
                             (bv_row[:].unsqueeze(1), bv.partition_broadcast(P)),
                             (gates[:].unsqueeze(1), shared["gates_dram"].partition_broadcast(P)),
                             (maskb[:], mask.rearrange("b o t -> (b o) t").partition_broadcast(P)),
                             (mask_col[:], shared["mask_col_dram"])):
                sp.dma_start(dst, src).then_inc(s["consts_in"], 16)

            def load(b):
                wait(sp, s["v_psum"], b.number - 1)
                wait(sp, s["qk_psum"], b.number - 1)
                sp.dma_start(cbuf[b.parity][:], ctx[b.number]).then_inc(s[f"ctx_in{b.parity}"], 16)
                wait(sp, s["q3_krep"], 4 * (b.number - 1))
                wait(sp, s["q3_qst"], b.number - 1)
                sp.dma_start(mrow[b.parity][96:128, :].unsqueeze(1),
                             mask[b.number].partition_broadcast(32)).then_inc(s[f"mrow_in{b.parity}"], 16)

            def distribute(b):
                wait(sp, s["split_done"], 2 * b.number + 2)
                wait(sp, s["kst_dve"], 2 * b.number)
                wait(sp, s["kst_pool"], 2 * b.number)
                for quadrant, part in enumerate((0, 1, 0)):
                    for g in range(GROUPS):
                        sp.dma_start(krep[32 * quadrant:32 * quadrant + 32, g, :].bitcast(F32),
                                     split[1][32 * g:32 * g + 32, part, :].bitcast(F32)).then_inc(s["dist_k"], 16)
                wait(sp, s["p2_ready"], 8 * (b.number - 1))
                for quadrant, part in enumerate((0, 0, 1)):
                    for g in range(GROUPS):
                        sp.dma_start(qst[b.parity][32 * quadrant:32 * quadrant + 32, g, :].bitcast(F32),
                                     split[0][32 * g:32 * g + 32, part, :].bitcast(F32)).then_inc(s[f"dist_q{b.parity}"], 16)

            load(fixed(0))
            load(fixed(1))
            distribute(fixed(0))

            def step(b):
                load(b.plus(2))
                distribute(b.plus(1))
            for n in range(2):
                step(fixed(n))
            paired_loop(sp, 2, B - 2, step)
            distribute(fixed(B - 1))

        @block.tensor
        def _(pe):
            def project_qk(b):
                wait(pe, s[f"ctx_in{b.parity}"], 16 * (b.half + 1))
                wait(pe, s["xn_ready"], b.number + 1)
                wait(pe, s["vt_ready"], b.number)
                nc.tensor.matmul(misc[:, 0:D], w_sb[:, 0, :], xn[:], start=True, stop=True)
                nc.tensor.matmul(misc[:, D:2 * D], w_sb[:, 1, :], cbuf[b.parity][:],
                                 start=True, stop=True).then_inc(s["qk_psum"], 1)

            def project_v(b):
                wait(pe, s["shift_done"], b.number)
                wait(pe, s["full_done"], 2 * b.number + 2)
                for c in range(2):
                    last = nc.tensor.matmul(misc[:, c * P:(c + 1) * P], cbuf[b.parity][:, c * P:(c + 1) * P],
                                            w_sb[:, 2, :], start=True, stop=True)
                last.then_inc(s["v_psum"], 1)

            def pass1(b, tile):
                tc, g = tile // GROUPS, tile % GROUPS
                if tile == 0:
                    wait(pe, s[f"dist_q{b.parity}"], 16 * 12 * (b.half + 1))
                    wait(pe, s["q3_qst"], b.number + 1)
                    wait(pe, s["kst_dve"], 2 * b.number + 2)
                    wait(pe, s["kst_pool"], 2 * b.number + 2)
                wait(pe, s["mx_done"], 8 * b.number + tile)
                for pair in range(2):
                    last = nc.tensor.matmul(p1[:, pair * 512:(pair + 1) * 512],
                                            qst[b.parity][:, g, tc * P:(tc + 1) * P],
                                            kst[b.parity][:, g, 2 * pair:2 * pair + 2, :],
                                            start=True, stop=True)
                last.then_inc(s["p1_ready"], 1)

            def transpose_max(b):
                wait(pe, s["mx_done"], 8 * b.number + 8)
                wait(pe, s["full_done"], 2 * min(b.number + 1, B - 1) + 2 if isinstance(b.number, int) else 2 * b.number + 4)
                wait(pe, s["vt_ready"], b.number + 1)
                for tc in range(2):
                    last = nc.tensor.transpose(misc[0:HEADS0, tc * P:(tc + 1) * P], mx[:, tc, :], ident[:])
                last.then_inc(s["mt_ready"], 1)

            def pass2(b, tile):
                if tile == 0:
                    wait(pe, s["shift_done"], b.number + 1)
                wait(pe, s["exp_done"], 8 * b.number + tile - 1)
                for k in range(2):
                    head = 2 * tile + k
                    for c in range(2):
                        last = nc.tensor.matmul(p2[tile % 2][:, (2 * k + c) * D:(2 * k + c + 1) * D],
                                                kst[b.parity][:, head // GH, head % GH, c * P:(c + 1) * P],
                                                qst[b.parity][:, head // GH, :], start=True, stop=True)
                last.then_inc(s["p2_ready"], 1)

            def weigh(b, tile):
                if tile == 0:
                    wait(pe, s["vst_ready"], 4 * b.number + 4)
                    wait(pe, s["evac_done"], 4 * b.number)
                wait(pe, s["exp_done"], 8 * b.number + tile + 1)
                half = tile // 4
                for k in range(2):
                    for c in range(2):
                        last = nc.tensor.matmul(pv[:, half * D:(half + 1) * D],
                                                vst[b.parity][:, c, 2 * tile + k, :],
                                                probs[tile % 2][:, k, c, :],
                                                start=(tile % 4 == 0 and k == 0 and c == 0),
                                                stop=(tile % 4 == 3 and k == 1 and c == 1))
                last.then_inc(s["pv_done"], 1)

            wait(pe, s["w_scaled"], 2)
            wait(pe, s["consts_in"], 16 * N_CONST_DMAS)
            wait(pe, s["zeroed"], 6)
            project_qk(fixed(0))
            project_v(fixed(0))
            project_qk(fixed(1))
            for tile in range(8):
                pass1(fixed(0), tile)
            transpose_max(fixed(0))

            def step(b, one=True, two=True):
                pass2(b, 0)
                if one:
                    project_v(b.plus(1))
                pass2(b, 1)
                weigh(b, 0)
                pass2(b, 2)
                weigh(b, 1)
                done = 0
                for tile in range(3, 8):
                    if two and tile == 4:
                        project_qk(b.plus(2))
                    if one:
                        for _ in range(2 if tile >= 5 else 1):
                            pass1(b.plus(1), done)
                            done += 1
                    pass2(b, tile)
                    weigh(b, tile - 1)
                if one:
                    while done < 8:
                        pass1(b.plus(1), done)
                        done += 1
                    transpose_max(b.plus(1))
                weigh(b, 7)
            for n in range(2):
                step(fixed(n))
            paired_loop(pe, 2, B - 2, step)
            step(fixed(B - 2), two=False)
            step(fixed(B - 1), one=False, two=False)

        @block.vector
        def _(dve):
            nc.vector.memset(eps[:], LN_EPS).then_inc(s["zeroed"], 1)
            for i in range(2):
                nc.vector.memset(vst[i][:], 0.0).then_inc(s["zeroed"], 1)
            dve.wait_ge(s["zeroed"], 3)
            for i in range(2):
                for half in range(2):
                    view = vst[i][:, :, 8 * half:8 * half + 8, :]
                    for h in range(8):
                        col = (64 if half == 0 else 0) + 8 * h
                        last = nc.vector.memset(view[:, :, h, col:col + 8], 1.0)
                last.then_inc(s["zeroed"], 1)
            nc.vector.memset(mx[:], 0.0).then_inc(s["zeroed"], 1)
            for b in range(B):
                if b % 4 == 0:
                    dve.wait_ge(x_in[b // 4], 16)
                last = nc.vector.bn_stats(stats[:, b, :], xres[:, b, :])
            last.then_inc(s["stats_done"], 1)
            dve.wait_ge(s["stats_done"], 1)
            for b in range(B):
                last = nc.vector.bn_aggr(mv[:, b, :], stats[:, b, :])
            last.then_inc(s["stats_done"], 1)
            dve.wait_ge(s["consts_in"], 16 * N_CONST_DMAS)
            nc.vector.tensor_scalar(w_sb[:, 0, :], w_sb[:, 0, :], HD0 ** -0.5, None, ALU.mult).then_inc(s["w_scaled"], 1)
            nc.vector.tensor_scalar(bias[:, 0:1], bias[:, 0:1], HD0 ** -0.5, None, ALU.mult).then_inc(s["w_scaled"], 1)
            dve.wait_ge(s["rstd_in"], 1)
            nc.vector.reciprocal(rstd[:], rstd[:]).then_inc(s["rstd_done"], 1)
            dve.wait_ge(s["rstd_done"], 1)

            def normalise(b):
                wait(dve, s["qk_psum"], b.number)
                nc.vector.tensor_scalar(xn[:], xres[:, b.number, :], mv[:, b.number, 0:1],
                                        rstd[:, bass.ds(b.number, 1)],
                                        ALU.subtract, ALU.mult).then_inc(s["xn_ready"], 1)

            def split_qk(b):
                wait(dve, s["qk_psum"], b.number + 1)
                wait(dve, s["dist_k"], 16 * 12 * b.number)
                wait(dve, s[f"dist_q{1 - b.parity}"], 16 * 12 * (b.half + b.parity))
                for i in range(2):
                    nc.vector.scalar_tensor_tensor(full[i][:], misc[:, i * D:(i + 1) * D], bias[:, i:i + 1],
                                                   maskb[:, b.number, :], ALU.add, ALU.mult).then_inc(s["full_done"], 1)
                for i in range(2):
                    dve.wait_ge(s["full_done"], 2 * b.number + i + 1)
                    nc.vector.tensor_copy(split[i][:, 0, :], full[i][:]).then_inc(s["hi_done"], 1)
                for i in range(2):
                    dve.wait_ge(s["hi_done"], 2 * b.number + i + 1)
                    nc.vector.tensor_tensor(split[i][:, 1, :], full[i][:], split[i][:, 0, :].bitcast(F32),
                                            ALU.subtract).then_inc(s["split_done"], 1)

            def stack_k(b):
                wait(dve, s["dist_k"], 16 * 12 * (b.number + 1))
                wait(dve, s["q3_krep"], 4 * (b.number + 1))
                wait(dve, s["p2_ready"], 8 * (b.number - 1))
                for j in range(2):
                    nc.vector.tensor_scalar(kst[b.parity][:, :, j, :], krep[:].bitcast(F32), cst[:, C_SEL + j:C_SEL + j + 1],
                                            None, ALU.mult).then_inc(s["kst_dve"], 1)

            def value_bias(b):
                wait(dve, s["v_psum"], b.number + 1)
                wait(dve, s["vst_ready"], 4 * b.number)
                nc.vector.tensor_tensor(vt[:], misc[:, 0:D].rearrange("p (c n) -> p c n", c=2),
                                        bv_row[:].unsqueeze(1).broadcast_to([P, 2, P]), ALU.add).then_inc(s["vt_ready"], 1)
                nc.vector.tensor_copy(mcb[:], mask_col[:, b.number, :]).then_inc(s["mcb_done"], 1)

            def reduce_max(b, tile):
                tc, g = tile // GROUPS, tile % GROUPS
                if tile == 0:
                    wait(dve, s["mt_ready"], b.number)
                wait(dve, s["p1_ready"], 8 * b.number + tile + 1)
                nc.vector.tensor_reduce(mx[:, tc, GH * g:GH * (g + 1)], p1[:].rearrange("p (h s) -> p h s", h=GH),
                                        AX.X, ALU.max).then_inc(s["mx_done"], 1)

            def finish(b):
                wait(dve, s["evac_done"], 4 * b.number + 4)
                nc.vector.reciprocal(rinv[:], sums[:]).then_inc(s["rin_done"], 1)
                nc.vector.scalar_tensor_tensor(tmp[:], outs[:], gates[:, 0:1], maskb[:, b.number, :],
                                               ALU.mult, ALU.mult).then_inc(s["tmp_done"], 1)
                dve.wait_ge(s["rin_done"], b.number + 1)
                dve.wait_ge(s["tmp_done"], 2 * b.number + 1)
                nc.vector.tensor_tensor(tmp[:], tmp[:], rinv[:], ALU.mult).then_inc(s["tmp_done"], 1)
                dve.wait_ge(s["tmp_done"], 2 * b.number + 2)
                nc.vector.tensor_tensor(xres[:, b.number, :], xres[:, b.number, :], tmp[:], ALU.add).then_inc(s["fin_done"], 1)
                dve.wait_ge(s["fin_done"], b.number + 1)
                nc.vector.bn_stats(shared["stats"][:, b.number, :], xres[:, b.number, :])

            dve.wait_ge(s["tanh_done"], 1)
            normalise(fixed(0))
            split_qk(fixed(0))
            normalise(fixed(1))
            value_bias(fixed(0))
            stack_k(fixed(0))
            split_qk(fixed(1))
            for tile in range(8):
                reduce_max(fixed(0), tile)

            def step(b, one=True, two=True, before=True):
                if one:
                    stack_k(b.plus(1))
                if two:
                    normalise(b.plus(2))
                if one:
                    value_bias(b.plus(1))
                    for tile in range(1):
                        reduce_max(b.plus(1), tile)
                if two:
                    split_qk(b.plus(2))
                if one:
                    for tile in range(1, 4):
                        reduce_max(b.plus(1), tile)
                if before:
                    finish(b.plus(-1))
                if one:
                    for tile in range(4, 8):
                        reduce_max(b.plus(1), tile)
            step(fixed(0), before=False)
            step(fixed(1))
            paired_loop(dve, 2, B - 2, step)
            step(fixed(B - 2), two=False)
            step(fixed(B - 1), one=False, two=False)
            finish(fixed(B - 1))

        @block.scalar
        def _(act):
            act.wait_ge(s["stats_done"], 2)
            act.wait_ge(s["zeroed"], 1)
            nc.scalar.activation(rstd[:], mv[:, :, 1], ACT.Sqrt, bias=eps[:, 0:1]).then_inc(s["rstd_in"], 1)
            act.wait_ge(s["consts_in"], 16 * N_CONST_DMAS)
            nc.scalar.activation(gates[:], gates[:], ACT.Tanh).then_inc(s["tanh_done"], 1)

            def shift(b):
                wait(act, s["mt_ready"], b.number + 1)
                nc.scalar.activation(qst[b.parity][96:96 + HEADS0, :, :],
                                     misc[0:HEADS0, 0:D].unsqueeze(1).broadcast_to([HEADS0, GROUPS, D]),
                                     ACT.Copy, scale=-1.0).then_inc(s["shift_done"], 1)

            def exps(b, tile):
                wait(act, s["p2_ready"], 8 * b.number + tile + 1)
                wait(act, s["pv_done"], 8 * b.number + tile - 1)
                nc.scalar.activation(probs[tile % 2][:].rearrange("p k c t -> p (k c t)"), p2[tile % 2][:],
                                     ACT.Exp).then_inc(s["exp_done"], 1)

            def evacuate(b):
                wait(act, s["pv_done"], 8 * b.number + 8)
                wait(act, s["fin_done"], b.number)
                for dst, rows, part in ((sums[0:64, :], slice(64, 128), 0), (sums[64:128, :], slice(0, 64), 1),
                                        (outs[0:64, :], slice(0, 64), 0), (outs[64:128, :], slice(64, 128), 1)):
                    nc.scalar.activation(dst, pv[rows, part * D:(part + 1) * D], ACT.Copy).then_inc(s["evac_done"], 1)

            shift(fixed(0))

            def step(b, one=True):
                for tile in range(8):
                    exps(b, tile)
                if one:
                    shift(b.plus(1))
                evacuate(b)
            for n in range(2):
                step(fixed(n))
            paired_loop(act, 2, B - 2, step)
            step(fixed(B - 2))
            step(fixed(B - 1), one=False)

        @block.gpsimd
        def _(pool):
            pool.wait_ge(s["consts_in"], 16 * N_CONST_DMAS)
            pool.wait_ge(s["zeroed"], 5)

            def settle():
                pool.nop(nofuse=True)

            def mask_rows(b):
                wait(pool, s[f"mrow_in{b.parity}"], 16 * (b.half + 1))
                wait(pool, s["kst_dve"], 2 * b.number)
                wait(pool, s["kst_pool"], 2 * b.number)
                wait(pool, s["vst_ready"], 4 * b.number)
                settle()
                for g in range(GROUPS):
                    nc.gpsimd.tensor_scalar(krep[96:128, g, :], mrow[b.parity][96:128, :],
                                            cst[96:128, C_KA:C_KA + 1], cst[96:128, C_KB + g:C_KB + g + 1],
                                            ALU.mult, ALU.add).then_inc(s["q3_krep"], 1)
                wait(pool, s["p2_ready"], 8 * (b.number - 1))
                wait(pool, s["q3_krep"], 4 * (b.number + 1))
                settle()
                nc.gpsimd.tensor_scalar(qst[b.parity][96:128, :, :],
                                        mrow[b.parity][96:128, :].unsqueeze(1).broadcast_to([32, GROUPS, D]),
                                        cst[96:128, C_QA:C_QA + 1], cst[96:128, C_QB:C_QB + 1],
                                        ALU.mult, ALU.add).then_inc(s["q3_qst"], 1)

            def stack_k(b):
                wait(pool, s["dist_k"], 16 * 12 * (b.number + 1))
                wait(pool, s["q3_qst"], b.number + 1)
                settle()
                for j in range(2, 4):
                    nc.gpsimd.tensor_scalar(kst[b.parity][:, :, j, :], krep[:].bitcast(F32), cst[:, C_SEL + j:C_SEL + j + 1],
                                            1.0, ALU.mult, ALU.mult).then_inc(s["kst_pool"], 1)

            def place_v(b):
                wait(pool, s["vt_ready"], b.number + 1)
                wait(pool, s["mcb_done"], b.number + 1)
                wait(pool, s["pv_done"], 8 * (b.number - 1))
                wait(pool, s["kst_pool"], 2 * (b.number + 1))
                settle()
                for c in range(2):
                    for half in range(2):
                        first = vst[b.parity][:, c, 8 * half:8 * half + 8, :]
                        flat = first.rearrange("p h n -> p (h n)")
                        out = bass.AP(flat.tensor, flat.offset + 64 * half, [list(flat.ap[0]), [P + 8, 8], [1, 8]])
                        nc.gpsimd.tensor_scalar(out, vt[:, c, 64 * half:64 * half + 64].rearrange("p (h n) -> p h n", h=8),
                                                mcb[:, c:c + 1],
                                                1.0, ALU.mult, ALU.mult).then_inc(s["vst_ready"], 1)

            mask_rows(fixed(0))
            stack_k(fixed(0))
            place_v(fixed(0))

            def step(b):
                mask_rows(b.plus(1))
                stack_k(b.plus(1))
                place_v(b.plus(1))
            for n in range(2):
                step(fixed(n))
            paired_loop(pool, 2, B - 2, step)
            step(fixed(B - 2))


TILES, GROUPS_OF_TILES = 4, 4
TOK = TILES * S
EXPERTS = 8
CHUNKS = 17
W_COLS = 6 * P
SEL_ROWS = 32


def mixture(nc, mem, shared, weights, router, select, rank):
    xres, ident, gates, stats = shared["x"], shared["ident"], shared["gates"], shared["stats"]

    def sb(name, shape, dt=F32):
        return mem.enter_context(nc.sbuf_tensor("m_" + name, shape, dt))

    def ps(name, cols):
        return mem.enter_context(nc.psum_tensor("m_" + name, [P, cols], F32))

    stage = [sb(f"stage{i}", [P, W_COLS]) for i in range(4)]
    w_hi = sb("w_hi", [P, CHUNKS, W_COLS], F32R)
    w_lo = sb("w_lo", [P, CHUNKS, W_COLS], F32R)
    router_sb = sb("router", [P, 2, EXPERTS + 1])
    select_f = sb("select_f", [SEL_ROWS, CHUNKS * P])
    select_r = sb("select_r", [SEL_ROWS, CHUNKS * P], F32R)
    rank_sb = sb("rank", [P, TILES, EXPERTS])
    mv = sb("mv", [P, B, 2])
    rstd = sb("rstd", [P, B])
    eps = sb("eps", [P, 1])
    xn = sb("xn", [P, TILES, D])
    xt = sb("xt", [P, 2, TOK])
    x_hi = sb("x_hi", [P, 2, TOK], F32R)
    x_lo = sb("x_lo", [P, 2, TOK], F32R)
    logit_t = sb("logit_t", [EXPERTS + 1, TOK])
    e = sb("e", [P, TILES, EXPERTS + 1])
    r1 = sb("r1", [P, TILES])
    w1 = sb("w1", [P, TILES, EXPERTS])
    w2 = sb("w2", [P, TILES, EXPERTS])
    comb = sb("comb", [P, TILES, SEL_ROWS])
    comb_hi = sb("comb_hi", [P, TILES, EXPERTS + 1], F32R)
    comb_f = sb("comb_f", [P, TILES, EXPERTS + 1])
    comb_t = sb("comb_t", [SEL_ROWS, TOK], F32R)
    sg = [sb(f"sg{i}", [P, TOK]) for i in range(2)]
    hid = [sb(f"hid{i}", [P, TOK]) for i in range(2)]
    h_hi = [sb(f"h_hi{i}", [P, TOK], F32R) for i in range(3)]
    h_lo = [sb(f"h_lo{i}", [P, TOK], F32R) for i in range(3)]
    yt = sb("yt", [P, 2, TOK])

    g_ps = [ps(f"g{i}", TOK) for i in range(2)]
    u_ps = [ps(f"u{i}", TOK) for i in range(2)]
    c_ps = ps("c", TOK)
    acc = [ps(f"acc{i}", TOK) for i in range(2)]
    misc = ps("misc", TOK)

    names = """in0 stage0 stage1 stage2 stage3 eps_done aggr sqrt_done rstd_done sel_done hi_w lo_w
        xn_done tr_ready tr_read split_hi split_lo router_ready logit_read nat_ready nat_read
        route exp_done comb_done combt_ready combt_done comb_chain g_ready u_ready c_ready silu_done
        mul_done hid_done h_hi h_lo down_done yt_done y_ready y_read""".split()
    s = {n: shared["semaphores"].enter_context(nc.semaphore("m_" + n)) for n in names}
    last_chunk = CHUNKS - 1

    with nc.Block() as block:

        @block.sync
        def _(sp):
            for dst, src in ((router_sb[:], router), (select_f[:], select), (rank_sb[:], rank)):
                sp.dma_start(dst, src).then_inc(s["in0"], 16)
            for j in range(CHUNKS):
                wait(sp, s["hi_w"], j - 3)
                wait(sp, s["lo_w"], j - 3)
                sp.dma_start(stage[j % 4][:], weights[j]).then_inc(s[f"stage{j % 4}"], 16)

        @block.tensor
        def _(pe):
            def transpose_x(n, kc):
                wait(pe, s["xn_done"], TILES * (n + 1))
                if kc == 0:
                    wait(pe, s["combt_done"], n)
                    wait(pe, s["y_read"], 2 * (n - 1))
                else:
                    wait(pe, s["tr_read"], 2 * n + 1)
                for t in range(TILES):
                    last = nc.tensor.transpose(misc[:, t * S:(t + 1) * S], xn[:, t, kc * P:(kc + 1) * P], ident[:])
                last.then_inc(s["tr_ready"], 1)

            def route_logits(n):
                wait(pe, s["tr_read"], 2 * n + 2)
                for kc in range(2):
                    last = nc.tensor.matmul(misc[0:EXPERTS + 1, :], router_sb[:, kc, :], xt[:, kc, :],
                                            start=kc == 0, stop=kc == 1)
                last.then_inc(s["router_ready"], 1)

            def transpose_logits(n):
                wait(pe, s["logit_read"], n + 1)
                pe.nop(nofuse=True)
                for t in range(TILES):
                    last = nc.tensor.transpose(misc[:, 16 * t:16 * t + EXPERTS + 1], logit_t[:, t * S:(t + 1) * S],
                                               ident[0:EXPERTS + 1, 0:EXPERTS + 1])
                last.then_inc(s["nat_ready"], 1)

            def transpose_comb(n):
                wait(pe, s["comb_done"], 2 * (n + 1))
                for t in range(TILES):
                    last = nc.tensor.transpose(misc[0:SEL_ROWS, t * S:(t + 1) * S], comb[:, t, :], ident[:])
                last.then_inc(s["combt_ready"], 1)

            def three(out, j, col, hi, lo, first, final):
                cols = slice(col, col + P)
                nc.tensor.matmul(out, w_hi[:, j, cols], hi, start=first, stop=False)
                nc.tensor.matmul(out, w_lo[:, j, cols], hi, start=False, stop=False)
                return nc.tensor.matmul(out, w_hi[:, j, cols], lo, start=False, stop=final)

            def up(n, j, group0):
                m = CHUNKS * n + j
                if group0:
                    wait(pe, s["hi_w"], j + 1)
                    wait(pe, s["lo_w"], j + 1)
                if j == 0:
                    wait(pe, s["split_hi"], n + 1)
                    wait(pe, s["split_lo"], n + 1)
                wait(pe, s["silu_done"], m - 1 if j else m)
                for kc in range(2):
                    last = three(g_ps[j % 2][:], j, kc * P, x_hi[:, kc, :], x_lo[:, kc, :], kc == 0, kc == 1)
                last.then_inc(s["g_ready"], 1)
                wait(pe, s["mul_done"], m - 1 if j else m)
                for kc in range(2):
                    last = three(u_ps[j % 2][:], j, (2 + kc) * P, x_hi[:, kc, :], x_lo[:, kc, :], kc == 0, kc == 1)
                last.then_inc(s["u_ready"], 1)
                if j == 0:
                    wait(pe, s["combt_done"], n + 1)
                wait(pe, s["hid_done"], m)
                nc.tensor.matmul(c_ps[:], select_r[:, j * P:(j + 1) * P], comb_t[:],
                                 start=True, stop=True).then_inc(s["c_ready"], 1)

            def down(n, j):
                m = CHUNKS * n + j
                wait(pe, s["h_hi"], m + 1)
                wait(pe, s["h_lo"], m + 1)
                if j == 0:
                    wait(pe, s["yt_done"], 2 * n)
                for fh in range(2):
                    last = three(acc[fh][:], j, (4 + fh) * P, h_hi[j % 3][:], h_lo[j % 3][:], j == 0, j == last_chunk)
                last.then_inc(s["down_done"], 1)

            def transpose_y(n, half, after):
                wait(pe, s["yt_done"], 2 * n + 2)
                if half == 0:
                    wait(pe, s["combt_done"], after)
                else:
                    wait(pe, s["y_read"], 2 * n + 1)
                for t in range(2):
                    for fh in range(2):
                        last = nc.tensor.transpose(misc[:, t * D + fh * P:t * D + (fh + 1) * P],
                                                   yt[:, fh, (2 * half + t) * S:(2 * half + t + 1) * S], ident[:])
                last.then_inc(s["y_ready"], 1)

            def group(n, first, final):
                for j in range(CHUNKS):
                    up(n, j, first)
                    if j < 2:
                        if not first:
                            down(n - 1, CHUNKS - 2 + j)
                    else:
                        down(n, j - 2)
                    if not first and j in (3, 4):
                        transpose_y(n - 1, j - 3, n + 1)
                    if not final:
                        if j in (6, 7):
                            transpose_x(n + 1, j - 6)
                        if j == 8:
                            route_logits(n + 1)
                        if j == 9:
                            transpose_logits(n + 1)
                        if j == 14:
                            transpose_comb(n + 1)

            wait(pe, s["in0"], 48)
            wait(pe, s["sel_done"], 2)
            transpose_x(0, 0)
            transpose_x(0, 1)
            route_logits(0)
            transpose_logits(0)
            transpose_comb(0)
            group(0, True, False)
            with pe.Fori(1, GROUPS_OF_TILES - 1) as n:
                group(n, False, False)
            group(GROUPS_OF_TILES - 1, False, True)
            for j in (CHUNKS - 2, CHUNKS - 1):
                down(GROUPS_OF_TILES - 1, j)
            for half in range(2):
                transpose_y(GROUPS_OF_TILES - 1, half, GROUPS_OF_TILES)

        @block.vector
        def _(dve):
            def normalise(n):
                wait(dve, s["tr_ready"], 2 * n)
                for t in range(TILES):
                    b = TILES * n + t
                    nc.vector.tensor_scalar(xn[:, t, :], xres[:, b, :], mv[:, b, 0:1], rstd[:, bass.ds(b, 1)],
                                            ALU.subtract, ALU.mult).then_inc(s["xn_done"], 1)

            def split_x(n):
                wait(dve, s["u_ready"], CHUNKS * n)
                wait(dve, s["tr_read"], 2 * n + 2)
                nc.vector.tensor_copy(x_hi[:], xt[:]).then_inc(s["split_hi"], 1)
                dve.wait_ge(s["split_hi"], n + 1)
                nc.vector.tensor_tensor(x_lo[:], xt[:], x_hi[:].bitcast(F32), ALU.subtract).then_inc(s["split_lo"], 1)

            def chain(ins, k):
                ins.then_inc(s["route"], 1)
                dve.wait_ge(s["route"], k)

            ROUTE = 15

            def route_a(n):
                base = ROUTE * n
                wait(dve, s["nat_ready"], n + 1)
                logits = misc[:, 0:64].rearrange("p (t c) -> p t c", c=16)
                chain(nc.vector.tensor_reduce(r1[:], logits[:, :, 0:EXPERTS], AX.X, ALU.max), base + 1)
                chain(nc.vector.tensor_tensor(e[:, :, 0:EXPERTS], logits[:, :, 0:EXPERTS],
                                              r1[:].unsqueeze(2).broadcast_to([P, TILES, EXPERTS]), ALU.subtract), base + 2)
                chain(nc.vector.tensor_scalar(e[:, :, EXPERTS:], logits[:, :, EXPERTS:EXPERTS + 1], -1.0, None, ALU.mult), base + 3)

            def pick(base, src, w):
                wide = [P, TILES, EXPERTS]
                chain(nc.vector.tensor_reduce(r1[:], src, AX.X, ALU.max), base + 1)
                chain(nc.vector.tensor_tensor(w[:], src, r1[:].unsqueeze(2).broadcast_to(wide), ALU.is_equal), base + 2)
                chain(nc.vector.tensor_tensor(w[:], w[:], rank_sb[:], ALU.mult), base + 3)
                chain(nc.vector.tensor_reduce(r1[:], w[:], AX.X, ALU.max), base + 4)
                chain(nc.vector.tensor_tensor(w[:], w[:], r1[:].unsqueeze(2).broadcast_to(wide), ALU.is_equal), base + 5)

            def route_b(n):
                base = ROUTE * n
                wait(dve, s["exp_done"], n + 1)
                wait(dve, s["combt_ready"], n)
                probs = e[:, :, 0:EXPERTS]
                pick(base + 3, probs, w1)
                ins = nc.vector.scalar_tensor_tensor(w2[:], w1[:], -4.0, probs, ALU.mult, ALU.add)
                chain(ins, base + 9)
                wide = [P, TILES, EXPERTS]
                chain(nc.vector.tensor_reduce(r1[:], w2[:], AX.X, ALU.max), base + 10)
                chain(nc.vector.tensor_tensor(w2[:], w2[:], r1[:].unsqueeze(2).broadcast_to(wide), ALU.is_equal), base + 11)
                chain(nc.vector.tensor_tensor(w2[:], w2[:], rank_sb[:], ALU.mult), base + 12)
                chain(nc.vector.tensor_reduce(r1[:], w2[:], AX.X, ALU.max), base + 13)
                chain(nc.vector.tensor_tensor(w2[:], w2[:], r1[:].unsqueeze(2).broadcast_to(wide), ALU.is_equal), base + 14)
                chain(nc.vector.tensor_tensor(w1[:], w1[:], w2[:], ALU.add), base + 15)

            COMB = 7

            def chain2(ins, k):
                ins.then_inc(s["comb_chain"], 1)
                dve.wait_ge(s["comb_chain"], k)

            def route_c(n):
                base = COMB * n
                wide = [P, TILES, EXPERTS]
                probs = e[:, :, 0:EXPERTS]
                chain2(nc.vector.tensor_tensor(w1[:], w1[:], probs, ALU.mult), base + 1)
                chain2(nc.vector.tensor_reduce(r1[:], w1[:], AX.X, ALU.add), base + 2)
                chain2(nc.vector.reciprocal(r1[:], r1[:]), base + 3)
                chain2(nc.vector.tensor_tensor(comb_f[:, :, 0:EXPERTS], w1[:],
                                               r1[:].unsqueeze(2).broadcast_to(wide), ALU.mult), base + 4)
                chain2(nc.vector.tensor_scalar(e[:, :, EXPERTS:], e[:, :, EXPERTS:], 1.0, None, ALU.add), base + 5)
                chain2(nc.vector.reciprocal(comb_f[:, :, EXPERTS:], e[:, :, EXPERTS:]), base + 6)
                chain2(nc.vector.tensor_copy(comb_hi[:], comb_f[:]), base + 7)
                nc.vector.tensor_copy(comb[:, :, 0:EXPERTS + 1], comb_hi[:].bitcast(F32)).then_inc(s["comb_done"], 1)
                nc.vector.tensor_tensor(comb[:, :, 16:17 + EXPERTS], comb_f[:], comb_hi[:].bitcast(F32),
                                        ALU.subtract).then_inc(s["comb_done"], 1)

            def split_weights(j):
                wait(dve, s["hi_w"], j + 1)
                nc.vector.tensor_tensor(w_lo[:, j, :], stage[j % 4][:], w_hi[:, j, :].bitcast(F32),
                                        ALU.subtract).then_inc(s["lo_w"], 1)

            def hidden(n, j):
                m = CHUNKS * n + j
                wait(dve, s["silu_done"], m + 1)
                wait(dve, s["u_ready"], m + 1)
                wait(dve, s["h_lo"], m - 1 if j else m)
                wait(dve, s["h_hi"], m - 1 if j else m)
                nc.vector.tensor_tensor(sg[j % 2][:], sg[j % 2][:], u_ps[j % 2][:], ALU.mult).then_inc(s["mul_done"], 1)
                wait(dve, s["mul_done"], m + 1)
                wait(dve, s["c_ready"], m + 1)
                nc.vector.tensor_tensor(hid[j % 2][:], sg[j % 2][:], c_ps[:], ALU.mult).then_inc(s["hid_done"], 1)

            def hidden_low(n, j):
                m = CHUNKS * n + j
                wait(dve, s["h_hi"], m + 1)
                nc.vector.tensor_tensor(h_lo[j % 3][:], hid[j % 2][:], h_hi[j % 3][:].bitcast(F32),
                                        ALU.subtract).then_inc(s["h_lo"], 1)

            def add_y(n, half):
                wait(dve, s["y_ready"], 2 * n + half + 1)
                tiles = xres[:, bass.ds(TILES * n + 2 * half, 2), :].rearrange("p t d -> p (t d)")
                nc.vector.scalar_tensor_tensor(tiles, misc[:], gates[:, 2:3], tiles, ALU.mult,
                                               ALU.add).then_inc(s["y_read"], 1)
                wait(dve, s["y_read"], 2 * n + half + 1)
                for t in range(2):
                    at = TILES * n + 2 * half + t
                    nc.vector.bn_stats(stats[:, at, :], xres[:, at, :])

            def group(n, first, final):
                for j in range(CHUNKS):
                    if first and j + 2 < CHUNKS:
                        split_weights(j + 2)
                    if j == 0 and not first:
                        hidden_low(n - 1, last_chunk)
                    hidden(n, j)
                    if j > 0:
                        hidden_low(n, j - 1)
                    if not first and j in (3, 4):
                        add_y(n - 1, j - 3)
                    if not final:
                        if j == 5:
                            normalise(n + 1)
                        if j == 10:
                            route_a(n + 1)
                        if j == 12:
                            route_b(n + 1)
                            route_c(n + 1)
                        if j == last_chunk:
                            split_x(n + 1)

            nc.vector.memset(eps[:], LN_EPS).then_inc(s["eps_done"], 1)
            nc.vector.memset(comb[:], 0.0).then_inc(s["sel_done"], 1)
            for b in range(B):
                last = nc.vector.bn_aggr(mv[:, b, :], stats[:, b, :])
            last.then_inc(s["aggr"], 1)
            dve.wait_ge(s["in0"], 48)
            nc.vector.tensor_copy(select_r[:], select_f[:]).then_inc(s["sel_done"], 1)
            dve.wait_ge(s["sqrt_done"], 1)
            nc.vector.reciprocal(rstd[:], rstd[:]).then_inc(s["rstd_done"], 1)
            dve.wait_ge(s["rstd_done"], 1)
            normalise(0)
            split_x(0)
            route_a(0)
            for j in range(2):
                split_weights(j)
            route_b(0)
            route_c(0)
            group(0, True, False)
            with dve.Fori(1, GROUPS_OF_TILES - 1) as n:
                group(n, False, False)
            group(GROUPS_OF_TILES - 1, False, True)
            hidden_low(GROUPS_OF_TILES - 1, last_chunk)
            for half in range(2):
                add_y(GROUPS_OF_TILES - 1, half)

        @block.scalar
        def _(act):
            def evacuate_x(n):
                for kc in range(2):
                    wait(act, s["tr_ready"], 2 * n + kc + 1)
                    if kc == 0:
                        wait(act, s["split_lo"], n)
                    nc.scalar.activation(xt[:, kc, :], misc[:], ACT.Copy).then_inc(s["tr_read"], 1)

            def evacuate_logits(n):
                wait(act, s["router_ready"], n + 1)
                nc.scalar.activation(logit_t[:], misc[0:EXPERTS + 1, :], ACT.Copy).then_inc(s["logit_read"], 1)

            def exp(n):
                wait(act, s["route"], 15 * n + 3)
                nc.scalar.activation(e[:], e[:], ACT.Exp).then_inc(s["exp_done"], 1)

            def evacuate_comb(n):
                wait(act, s["combt_ready"], n + 1)
                wait(act, s["c_ready"], CHUNKS * n)
                nc.scalar.activation(comb_t[:], misc[0:SEL_ROWS, :], ACT.Copy).then_inc(s["combt_done"], 1)

            def split_weights(j):
                wait(act, s[f"stage{j % 4}"], 16 * (j // 4 + 1))
                nc.scalar.activation(w_hi[:, j, :], stage[j % 4][:], ACT.Copy).then_inc(s["hi_w"], 1)

            def silu(n, j):
                m = CHUNKS * n + j
                wait(act, s["g_ready"], m + 1)
                wait(act, s["hid_done"], m - 1 if j else m)
                nc.scalar.activation(sg[j % 2][:], g_ps[j % 2][:], ACT.Silu).then_inc(s["silu_done"], 1)

            def hidden_high(n, j):
                m = CHUNKS * n + j
                wait(act, s["hid_done"], m + 1)
                wait(act, s["down_done"], m - 1 if j < 2 else m - 2)
                nc.scalar.activation(h_hi[j % 3][:], hid[j % 2][:], ACT.Copy).then_inc(s["h_hi"], 1)

            def evacuate_y(n):
                wait(act, s["down_done"], CHUNKS * (n + 1))
                for fh in range(2):
                    nc.scalar.activation(yt[:, fh, :], acc[fh][:], ACT.Copy).then_inc(s["yt_done"], 1)

            def group(n, first, final):
                for j in range(CHUNKS):
                    silu(n, j)
                    if j > 0:
                        hidden_high(n, j - 1)
                    elif not first:
                        hidden_high(n - 1, last_chunk)
                    if first and j + 3 < CHUNKS:
                        split_weights(j + 3)
                    if not first and j == 2:
                        evacuate_y(n - 1)
                    if not final:
                        if j == 7:
                            evacuate_x(n + 1)
                        if j == 8:
                            evacuate_logits(n + 1)
                        if j == 11:
                            exp(n + 1)
                        if j == last_chunk:
                            evacuate_comb(n + 1)

            act.wait_ge(s["aggr"], 1)
            act.wait_ge(s["eps_done"], 1)
            nc.scalar.activation(rstd[:], mv[:, :, 1], ACT.Sqrt, bias=eps[:, 0:1]).then_inc(s["sqrt_done"], 1)
            evacuate_x(0)
            evacuate_logits(0)
            for j in range(2):
                split_weights(j)
            exp(0)
            evacuate_comb(0)
            split_weights(2)
            group(0, True, False)
            with act.Fori(1, GROUPS_OF_TILES - 1) as n:
                group(n, False, False)
            group(GROUPS_OF_TILES - 1, False, True)
            hidden_high(GROUPS_OF_TILES - 1, last_chunk)
            evacuate_y(GROUPS_OF_TILES - 1)


KV, HPK = 4, 4
HD1 = 128
RMS_EPS = 1e-6
PIECES = 10


def attention1(nc, mem, shared, weights, norm_w, ctx):
    xres, ident, gates, stats = shared["x"], shared["ident"], shared["gates"], shared["stats"]

    def sb(name, shape, dt=F32):
        return mem.enter_context(nc.sbuf_tensor("c_" + name, shape, dt))

    def ps(name):
        return mem.enter_context(nc.psum_tensor("c_" + name, [P, 512], F32))

    stage = [sb(f"stage{i}", [P, 1024]) for i in range(2)]
    w_hi = sb("w_hi", [P, PIECES, 1024], F32R)
    w_lo = sb("w_lo", [P, PIECES, 1024], F32R)
    norm_sb = sb("norm", [P, 2])
    wqk = sb("wqk", [P, 1])
    mv = sb("mv", [P, B, 2])
    rstd = sb("rstd", [P, B])
    eps = sb("eps", [P, 1])
    half_neg = sb("half_neg", [P, KV])
    cbuf = [sb(f"ctx{i}", [P, D]) for i in range(2)]
    xn = sb("xn", [P, D])
    in_hi = sb("in_hi", [P, 4, P], F32R)
    in_lo = sb("in_lo", [P, 4, P], F32R)
    sq = [sb(f"sq{i}", [P, 512]) for i in range(2)]
    ssq = sb("ssq", [P, 5 * KV])
    ms = sb("ms", [P, 5 * KV])
    rms = sb("rms", [P, 5 * KV])
    kn = sb("kn", [P, 512])
    qn = [sb(f"qn{i}", [P, 512]) for i in range(2)]
    k_t = [sb(f"k_t{i}", [P, KV, P]) for i in range(2)]
    q_t = [sb(f"q_t{i}", [P, KV, 512]) for i in range(2)]
    v_sb = [sb(f"v{i}", [P, KV, HD1]) for i in range(2)]
    probs = [sb(f"probs{i}", [P, 512]) for i in range(4)]
    top = sb("top", [P, 4 * HPK])
    tot = sb("tot", [P, 4 * HPK])
    inv = sb("inv", [P, 4 * HPK])
    p_t = [sb(f"p_t{i}", [P, 512]) for i in range(2)]
    o_hi = [sb(f"o_hi{i}", [P, 512], F32R) for i in range(2)]
    o_lo = [sb(f"o_lo{i}", [P, 512], F32R) for i in range(2)]

    pj = [ps(f"pj{i}") for i in range(2)]
    tr = [ps(f"tr{i}") for i in range(2)]
    sc = [ps(f"sc{i}") for i in range(2)]
    pv = ps("pv")
    out = ps("out")

    names = """in0 stage0 stage1 hi_w lo_w eps_done aggr sqrt_done rstd_done wqk_done ctx_in0 ctx_in1 xn_done
        x_tr x_hi x_lo pj_ready sq_done ssq_done ms_done rms_done mul_done v_read kt_tr kt_read qt_tr qt_read
        sc_ready max_done sub_done exp_done sum_done inv_done norm_done pt_tr pt_read pv_ready o_hi o_lo
        out_ready x_done""".split()
    s = {n: shared["semaphores"].enter_context(nc.semaphore("c_" + n)) for n in names}

    def heads(ap):
        return ap.rearrange("p (h n) -> p h n", h=4)

    def spread(ap):
        return ap.unsqueeze(2).broadcast_to([P, 4, 128])

    with nc.Block() as block:

        @block.sync
        def _(sp):
            def step(b):
                wait(sp, s["x_tr"], b.number - 1)
                sp.dma_start(cbuf[b.parity][:], ctx[b.number]).then_inc(s[f"ctx_in{b.parity}"], 16)
            sp.dma_start(norm_sb[:], norm_w).then_inc(s["in0"], 16)
            for n in range(2):
                step(fixed(n))
            for j in range(PIECES):
                wait(sp, s["hi_w"], j - 1)
                wait(sp, s["lo_w"], j - 1)
                sp.dma_start(stage[j % 2][:], weights[j]).then_inc(s[f"stage{j % 2}"], 16)
            paired_loop(sp, 2, B, step)

        @block.tensor
        def _(pe):
            def transpose_in(b):
                wait(pe, s["xn_done"], b.number + 1)
                wait(pe, s[f"ctx_in{b.parity}"], 16 * (b.half + 1))
                wait(pe, s["kt_read"], b.number)
                wait(pe, s["pt_read"], 4 * (b.number - 1))
                for src, at in ((xn, 0), (cbuf[b.parity], 2)):
                    for kc in range(2):
                        last = nc.tensor.transpose(tr[0][:, (at + kc) * P:(at + kc + 1) * P],
                                                   src[:, kc * P:(kc + 1) * P], ident[:])
                last.then_inc(s["x_tr"], 1)

            def project(a, c):
                n = a.number
                if c == 0:
                    wait(pe, s["x_hi"], n + 1)
                    wait(pe, s["x_lo"], n + 1)
                if c == 3:
                    wait(pe, s["v_read"], n + 1)
                else:
                    wait(pe, s["mul_done"], 5 * n + {0: -1, 1: 0, 2: 1, 4: 2, 5: 3}[c])
                for kc in range(2):
                    row = kc + (2 if c < 2 else 0)
                    if c < 2:
                        w = (kc, c * 512)
                    else:
                        w = (2 + 2 * kc + (c - 2) // 2, (c % 2) * 512)
                    wh, wl = (t[:, w[0], w[1]:w[1] + 512] for t in (w_hi, w_lo))
                    nc.tensor.matmul(pj[c % 2][:], in_hi[:, row, :], wh, start=kc == 0, stop=False)
                    nc.tensor.matmul(pj[c % 2][:], in_hi[:, row, :], wl, start=False, stop=False)
                    last = nc.tensor.matmul(pj[c % 2][:], in_lo[:, row, :], wh, start=False, stop=kc == 1)
                last.then_inc(s["pj_ready"], 1)

            def transpose_k(a):
                wait(pe, s["mul_done"], 5 * a.number + 1)
                wait(pe, s["x_lo"], a.number + 1)
                wait(pe, s["x_hi"], a.number + 1)
                for i in range(KV):
                    last = nc.tensor.transpose(tr[0][:, i * P:(i + 1) * P], kn[:, i * P:(i + 1) * P], ident[:])
                last.then_inc(s["kt_tr"], 1)

            def transpose_q(a, i):
                wait(pe, s["mul_done"], 5 * a.number + 2 + i)
                if i == 0:
                    wait(pe, s["pt_read"], 4 * (a.number - 1) + 1)
                else:
                    wait(pe, s["qt_read"], 4 * a.number + i)
                for h in range(HPK):
                    last = nc.tensor.transpose(tr[1][:, h * P:(h + 1) * P], qn[i % 2][:, h * P:(h + 1) * P], ident[:])
                last.then_inc(s["qt_tr"], 1)

            def transpose_p(b, i, a_runs):
                wait(pe, s["norm_done"], 4 * b.number + i + 1)
                if i == 0:
                    wait(pe, s["qt_read"], 4 * (b.number + 1))
                elif i == 1:
                    wait(pe, s["pt_read"], 4 * b.number)
                    if a_runs:
                        wait(pe, s["kt_read"], b.number + 2)
                else:
                    wait(pe, s["pt_read"], 4 * b.number + i)
                for h in range(HPK):
                    last = nc.tensor.transpose(tr[0 if i else 1][:, h * P:(h + 1) * P],
                                               probs[i][:, h * P:(h + 1) * P], ident[:])
                last.then_inc(s["pt_tr"], 1)

            def score(b, i):
                if i == 0:
                    wait(pe, s["kt_read"], b.number + 1)
                wait(pe, s["qt_read"], 4 * b.number + i + 1)
                wait(pe, s["sub_done"], 4 * b.number + i - 1)
                for h in range(HPK):
                    last = nc.tensor.matmul(sc[i % 2][:, h * P:(h + 1) * P], q_t[b.parity][:, i, h * P:(h + 1) * P],
                                            k_t[b.parity][:, i, :], start=True, stop=True)
                last.then_inc(s["sc_ready"], 1)

            def weigh(b, i):
                if i == 0:
                    wait(pe, s["v_read"], b.number + 1)
                wait(pe, s["pt_read"], 4 * b.number + i + 1)
                wait(pe, s["o_hi"], 4 * b.number + i)
                wait(pe, s["o_lo"], 4 * b.number + i)
                nc.tensor.matmul(pv[:], v_sb[b.parity][:, i, :], p_t[i % 2][:], start=True, stop=True).then_inc(s["pv_ready"], 1)

            def project_out(b, i):
                wait(pe, s["o_hi"], 4 * b.number + i + 1)
                wait(pe, s["o_lo"], 4 * b.number + i + 1)
                if i == 0:
                    wait(pe, s["x_done"], b.number)
                for h in range(HPK):
                    wh, wl = (t[:, 6 + i, h * D:(h + 1) * D] for t in (w_hi, w_lo))
                    oh, ol = (t[i % 2][:, h * P:(h + 1) * P] for t in (o_hi, o_lo))
                    nc.tensor.matmul(out[:, 0:D], oh, wh, start=i == 0 and h == 0, stop=False)
                    nc.tensor.matmul(out[:, 0:D], oh, wl, start=False, stop=False)
                    last = nc.tensor.matmul(out[:, 0:D], ol, wh, start=False, stop=i == 3 and h == 3)
                last.then_inc(s["out_ready"], 1)

            def step(b, do_b=True, do_a=True, do_x=True):
                a = b.plus(1)
                if do_a:
                    project(a, 0)
                if do_b:
                    score(b, 0)
                if do_a:
                    project(a, 1)
                if do_b:
                    score(b, 1)
                if do_a:
                    project(a, 2)
                    transpose_k(a)
                if do_b:
                    transpose_p(b, 0, do_a)
                    score(b, 2)
                if do_a:
                    project(a, 3)
                if do_b:
                    transpose_p(b, 1, do_a)
                    weigh(b, 0)
                if do_a:
                    transpose_q(a, 0)
                    project(a, 4)
                if do_b:
                    score(b, 3)
                    weigh(b, 1)
                    project_out(b, 0)
                    transpose_p(b, 2, do_a)
                if do_a:
                    transpose_q(a, 1)
                    project(a, 5)
                if do_b:
                    weigh(b, 2)
                    project_out(b, 1)
                    transpose_p(b, 3, do_a)
                if do_a:
                    transpose_q(a, 2)
                if do_x:
                    transpose_in(b.plus(2))
                if do_b:
                    project_out(b, 2)
                    weigh(b, 3)
                if do_a:
                    transpose_q(a, 3)
                if do_b:
                    project_out(b, 3)

            step(fixed(-2), do_b=False, do_a=False)
            wait(pe, s["hi_w"], PIECES)
            wait(pe, s["lo_w"], PIECES)
            step(fixed(-1), do_b=False)
            for n in range(2):
                step(fixed(n))
            paired_loop(pe, 2, B - 2, step)
            step(fixed(B - 2), do_x=False)
            step(fixed(B - 1), do_a=False, do_x=False)

        @block.vector
        def _(dve):
            def normalise(b):
                wait(dve, s["x_tr"], b.number)
                nc.vector.tensor_scalar(xn[:], xres[:, b.number, :], mv[:, b.number, 0:1], rstd[:, bass.ds(b.number, 1)],
                                        ALU.subtract, ALU.mult).then_inc(s["xn_done"], 1)

            def split_in(b):
                wait(dve, s["x_hi"], b.number + 1)
                wait(dve, s["pj_ready"], 6 * b.number)
                nc.vector.tensor_tensor(in_lo[:].rearrange("p a n -> p (a n)"), tr[0][:],
                                        in_hi[:].bitcast(F32).rearrange("p a n -> p (a n)"), ALU.subtract).then_inc(s["x_lo"], 1)

            def sum_squares(a, k):
                wait(dve, s["sq_done"], 5 * a.number + k + 1)
                nc.vector.tensor_reduce(ssq[:, 4 * k:4 * k + 4], heads(sq[k % 2][:]),
                                        AX.X, ALU.add).then_inc(s["ssq_done"], 1)

            def scale(a, k):
                wait(dve, s["rms_done"], 5 * a.number + k + 1)
                if k == 0:
                    wait(dve, s["kt_tr"], a.number)
                    dst = kn
                else:
                    wait(dve, s["qt_tr"], 4 * a.number + k - 2)
                    dst = qn[(k - 1) % 2]
                bank = 0 if k == 0 else (k + 1) % 2
                nc.vector.tensor_tensor(heads(dst[:]), heads(pj[bank][:]), spread(rms[:, 4 * k:4 * k + 4]),
                                        ALU.mult).then_inc(s["mul_done"], 1)

            def evacuate_k(a):
                wait(dve, s["kt_tr"], a.number + 1)
                wait(dve, s["sc_ready"], 4 * (a.number - 1))
                nc.vector.tensor_scalar(k_t[a.parity][:].rearrange("p a n -> p (a n)"), tr[0][:], wqk[:, 0:1], None,
                                        ALU.mult).then_inc(s["kt_read"], 1)

            def shift(b, i):
                wait(dve, s["sc_ready"], 4 * b.number + i + 1)
                nc.vector.tensor_reduce(top[:, 4 * i:4 * i + 4], heads(sc[i % 2][:]), AX.X, ALU.max).then_inc(s["max_done"], 1)
                wait(dve, s["max_done"], 4 * b.number + i + 1)
                wait(dve, s["pt_tr"], 4 * (b.number - 1) + i + 1)
                nc.vector.tensor_tensor(heads(probs[i][:]), heads(sc[i % 2][:]), spread(top[:, 4 * i:4 * i + 4]),
                                        ALU.subtract).then_inc(s["sub_done"], 1)

            def total(b, i):
                wait(dve, s["exp_done"], 4 * b.number + i + 1)
                nc.vector.tensor_reduce(tot[:, 4 * i:4 * i + 4], heads(probs[i][:]), AX.X, ALU.add).then_inc(s["sum_done"], 1)
                wait(dve, s["sum_done"], 4 * b.number + i + 1)
                nc.vector.reciprocal(inv[:, 4 * i:4 * i + 4], tot[:, 4 * i:4 * i + 4]).then_inc(s["inv_done"], 1)

            def split_out(b, i):
                wait(dve, s["o_hi"], 4 * b.number + i + 1)
                wait(dve, s["out_ready"], 4 * b.number + i - 1)
                nc.vector.tensor_tensor(o_lo[i % 2][:], pv[:], o_hi[i % 2][:].bitcast(F32), ALU.subtract).then_inc(s["o_lo"], 1)

            def add_out(b):
                wait(dve, s["out_ready"], 4 * b.number + 4)
                nc.vector.scalar_tensor_tensor(xres[:, b.number, :], out[:, 0:D], gates[:, 1:2], xres[:, b.number, :],
                                               ALU.mult, ALU.add).then_inc(s["x_done"], 1)
                wait(dve, s["x_done"], b.number + 1)
                nc.vector.bn_stats(stats[:, b.number, :], xres[:, b.number, :])

            def step(b, do_b=True, do_a=True, do_x=True):
                a = b.plus(1)
                if do_a:
                    sum_squares(a, 0)
                if do_b:
                    shift(b, 0)
                if do_a:
                    scale(a, 0)
                if do_b:
                    total(b, 0)
                    shift(b, 1)
                if do_a:
                    evacuate_k(a)
                    sum_squares(a, 1)
                if do_b:
                    total(b, 1)
                    shift(b, 2)
                if do_a:
                    scale(a, 1)
                    sum_squares(a, 2)
                if do_b:
                    total(b, 2)
                    split_out(b, 0)
                if do_a:
                    scale(a, 2)
                    sum_squares(a, 3)
                if do_b:
                    shift(b, 3)
                    split_out(b, 1)
                    total(b, 3)
                if do_a:
                    scale(a, 3)
                    sum_squares(a, 4)
                if do_b:
                    split_out(b, 2)
                if do_x:
                    normalise(b.plus(2))
                if do_a:
                    scale(a, 4)
                if do_x:
                    split_in(b.plus(2))
                if do_b:
                    split_out(b, 3)
                    add_out(b)

            nc.vector.memset(eps[:], LN_EPS).then_inc(s["eps_done"], 1)
            nc.vector.memset(half_neg[:], -0.5).then_inc(s["eps_done"], 1)
            for b in range(B):
                last = nc.vector.bn_aggr(mv[:, b, :], stats[:, b, :])
            last.then_inc(s["aggr"], 1)
            dve.wait_ge(s["in0"], 16)
            nc.vector.scalar_tensor_tensor(wqk[:], norm_sb[:, 0:1], HD1 ** -0.5, norm_sb[:, 1:2],
                                           ALU.mult, ALU.mult).then_inc(s["wqk_done"], 1)
            dve.wait_ge(s["sqrt_done"], 1)
            nc.vector.reciprocal(rstd[:], rstd[:]).then_inc(s["rstd_done"], 1)
            dve.wait_ge(s["rstd_done"], 1)
            dve.wait_ge(s["wqk_done"], 1)
            step(fixed(-2), do_b=False, do_a=False)
            for j in range(PIECES):
                wait(dve, s["hi_w"], j + 1)
                nc.vector.tensor_tensor(w_lo[:, j, :], stage[j % 2][:], w_hi[:, j, :].bitcast(F32),
                                        ALU.subtract).then_inc(s["lo_w"], 1)
            step(fixed(-1), do_b=False)
            for n in range(2):
                step(fixed(n))
            paired_loop(dve, 2, B - 2, step)
            step(fixed(B - 2), do_x=False)
            step(fixed(B - 1), do_a=False, do_x=False)

        @block.scalar
        def _(act):
            def copy(dst, src):
                return nc.scalar.activation(dst, src, ACT.Copy)

            def square(a, k):
                c = 0 if k == 0 else k + 1
                wait(act, s["pj_ready"], 6 * a.number + c + 1)
                wait(act, s["ssq_done"], 5 * a.number + k - (1 if k else 0))
                nc.scalar.activation(sq[k % 2][:], pj[c % 2][:], ACT.Square).then_inc(s["sq_done"], 1)

            def values(a):
                wait(act, s["pj_ready"], 6 * a.number + 2)
                wait(act, s["pv_ready"], 4 * (a.number - 1))
                copy(v_sb[a.parity][:].rearrange("p a n -> p (a n)"), pj[1][:]).then_inc(s["v_read"], 1)

            def exp(b, i):
                wait(act, s["sub_done"], 4 * b.number + i + 1)
                nc.scalar.activation(probs[i][:], probs[i][:], ACT.Exp).then_inc(s["exp_done"], 1)

            def evacuate_p(b, i):
                wait(act, s["pt_tr"], 4 * b.number + i + 1)
                wait(act, s["pv_ready"], 4 * b.number + i - 1)
                copy(p_t[i % 2][:], tr[0 if i else 1][:]).then_inc(s["pt_read"], 1)

            def evacuate_q(a, i):
                wait(act, s["qt_tr"], 4 * a.number + i + 1)
                wait(act, s["sc_ready"], 4 * (a.number - 1))
                copy(q_t[a.parity][:, i, :], tr[1][:]).then_inc(s["qt_read"], 1)

            def split_out(b, i):
                wait(act, s["pv_ready"], 4 * b.number + i + 1)
                wait(act, s["out_ready"], 4 * b.number + i - 1)
                copy(o_hi[i % 2][:], pv[:]).then_inc(s["o_hi"], 1)

            def split_in(b):
                wait(act, s["x_tr"], b.number + 1)
                wait(act, s["pj_ready"], 6 * b.number)
                copy(in_hi[:].rearrange("p a n -> p (a n)"), tr[0][:]).then_inc(s["x_hi"], 1)

            def step(b, do_b=True, do_a=True, do_x=True):
                a = b.plus(1)
                if do_a:
                    square(a, 0)
                if do_b:
                    exp(b, 0)
                if do_a:
                    values(a)
                if do_b:
                    exp(b, 1)
                if do_a:
                    square(a, 1)
                if do_b:
                    evacuate_p(b, 0)
                if do_a:
                    square(a, 2)
                if do_b:
                    exp(b, 2)
                    evacuate_p(b, 1)
                    split_out(b, 0)
                if do_a:
                    evacuate_q(a, 0)
                    square(a, 3)
                if do_b:
                    exp(b, 3)
                    split_out(b, 1)
                    evacuate_p(b, 2)
                if do_a:
                    evacuate_q(a, 1)
                    square(a, 4)
                if do_b:
                    split_out(b, 2)
                    evacuate_p(b, 3)
                if do_a:
                    evacuate_q(a, 2)
                if do_x:
                    split_in(b.plus(2))
                if do_b:
                    split_out(b, 3)
                if do_a:
                    evacuate_q(a, 3)

            act.wait_ge(s["aggr"], 1)
            act.wait_ge(s["eps_done"], 1)
            nc.scalar.activation(rstd[:], mv[:, :, 1], ACT.Sqrt, bias=eps[:, 0:1]).then_inc(s["sqrt_done"], 1)
            step(fixed(-2), do_b=False, do_a=False)
            for j in range(PIECES):
                wait(act, s[f"stage{j % 2}"], 16 * (j // 2 + 1))
                copy(w_hi[:, j, :], stage[j % 2][:]).then_inc(s["hi_w"], 1)
            step(fixed(-1), do_b=False)
            for n in range(2):
                step(fixed(n))
            paired_loop(act, 2, B - 2, step)
            step(fixed(B - 2), do_x=False)
            step(fixed(B - 1), do_a=False, do_x=False)

        @block.gpsimd
        def _(pool):
            def settle():
                pool.nop(nofuse=True)

            def root(a, k):
                n = 5 * a.number + k
                cols = slice(4 * k, 4 * k + 4)
                wait(pool, s["ssq_done"], n + 1)
                settle()
                nc.gpsimd.tensor_scalar(ms[:, cols], ssq[:, cols], 1.0 / HD1, RMS_EPS, ALU.mult, ALU.add).then_inc(s["ms_done"], 1)
                wait(pool, s["ms_done"], n + 1)
                settle()
                nc.gpsimd.tensor_tensor(rms[:, cols], ms[:, cols], half_neg[:], ALU.pow).then_inc(s["rms_done"], 1)

            def norm(b, i):
                wait(pool, s["inv_done"], 4 * b.number + i + 1)
                settle()
                nc.gpsimd.tensor_tensor(heads(probs[i][:]), heads(probs[i][:]), spread(inv[:, 4 * i:4 * i + 4]),
                                        ALU.mult).then_inc(s["norm_done"], 1)

            def step(b, do_b=True, do_a=True):
                for i in range(4):
                    if do_a:
                        root(b.plus(1), i)
                    if do_b:
                        norm(b, i)
                if do_a:
                    root(b.plus(1), 4)

            pool.wait_ge(s["eps_done"], 2)
            step(fixed(-1), do_b=False)
            for n in range(2):
                step(fixed(n))
            paired_loop(pool, 2, B - 2, step)
            step(fixed(B - 2))
            step(fixed(B - 1), do_a=False)


FF = 1024
Q_EPS = 1e-5
ROUND = 12582912.0
HCH = FF // P


def bitlinear(nc, mem, shared, weights, out):
    xres, gates, stats = shared["x"], shared["gates"], shared["stats"]
    ident_f = shared["ident"]

    def sb(name, shape, dt=F32):
        return mem.enter_context(nc.sbuf_tensor("d_" + name, shape, dt))

    def ps(name, cols, dt=F32):
        return mem.enter_context(nc.psum_tensor("d_" + name, [P, cols], dt))

    wf = [sb(f"wf{i}", [P, 2 * FF]) for i in range(3)]
    wq = [sb(f"wq{i}", [P, 2 * FF], BF16) for i in range(3)]
    part = sb("part", [P, 3])
    ones = sb("ones", [P, P])
    wmean = sb("wmean", [P, 3])
    wscale = sb("wscale", [P, 3])
    ident = sb("ident", [P, P], BF16)
    eps = sb("eps", [P, 1])
    half_neg = sb("half_neg", [P, B])
    mv = sb("mv", [P, B, 2])
    rstd = sb("rstd", [P, B])
    rms = sb("rms", [P, B])
    xn = sb("xn", [P, B, D])
    amax = sb("amax", [P, B])
    qs = sb("qs", [P, B])
    unit = sb("unit", [P, B])
    gate_a = sb("gate_a", [P, B])
    up_a = sb("up_a", [P, B])
    down_a = sb("down_a", [P, B])
    xq = sb("xq", [P, B, D], BF16)
    xq_t = [sb(f"xq_t{i}", [P, 2, P], BF16) for i in range(2)]
    sg = [sb(f"sg{i}", [P, FF]) for i in range(2)]
    h = [sb(f"h{i}", [P, FF]) for i in range(2)]
    hs = sb("hs", [P, FF])
    sq = sb("sq", [P, FF])
    ssq = sb("ssq", [P, 2])
    hms = sb("hms", [P, 2])
    hr = sb("hr", [P, 2])
    hmax = sb("hmax", [P, B])
    hunit = sb("hunit", [P, B])
    hqs = sb("hqs", [P, B])
    hq = [sb(f"hq{i}", [P, FF], BF16) for i in range(2)]
    hq_t = [sb(f"hq_t{i}", [P, FF], BF16) for i in range(2)]

    g_ps = ps("g", FF)
    u_ps = ps("u", FF)
    h_tr = ps("h_tr", FF, BF16)
    x_tr = ps("x_tr", 2 * P, BF16)
    y_ps = ps("y", 512)

    names = """set_done aggr sqrt_done x_chain rms_done xq_done part_done mean_ready w_chain wq_done xt_ready xt_read
        g_ready u_ready silu_done h_done sq_done max_done ms_done pow_done h_chain hs_done hq_done
        ht_ready ht_read y_ready x_done stored""".split()
    s = {n: shared["semaphores"].enter_context(nc.semaphore("d_" + n)) for n in names}
    w_in = [shared["semaphores"].enter_context(nc.semaphore(f"d_w_in{i}")) for i in range(3)]

    with nc.Block() as block:

        @block.sync
        def _(sp):
            for i in range(3):
                sp.dma_start(wf[i][:], weights[i]).then_inc(w_in[i], 16)

            def store(b):
                wait(sp, s["x_done"], b.number + 1)
                sp.dma_start(out[b.number], xres[:, b.number, :]).then_inc(s["stored"], 16)
            for n in range(2):
                store(fixed(n))
            paired_loop(sp, 2, B, store)
            sp.wait_ge(s["stored"], 16 * B)

        @block.tensor
        def _(pe):
            def transpose_x(b):
                wait(pe, s["xt_read"], b.number)
                for kc in range(2):
                    last = nc.tensor.transpose(x_tr[:, kc * P:(kc + 1) * P], xq[:, b.number, kc * P:(kc + 1) * P], ident[:])
                last.then_inc(s["xt_ready"], 1)

            def gate_up(b):
                wait(pe, s["xt_read"], b.number + 1)
                for i, (bank, free, ready) in enumerate(((g_ps, "silu_done", "g_ready"), (u_ps, "h_done", "u_ready"))):
                    wait(pe, s[free], b.number)
                    for half in range(2):
                        for kc in range(2):
                            last = nc.tensor.matmul(bank[:, half * 512:(half + 1) * 512], xq_t[b.parity][:, kc, :],
                                                    wq[i][:, kc * FF + half * 512:kc * FF + (half + 1) * 512],
                                                    start=kc == 0, stop=kc == 1)
                    last.then_inc(s[ready], 1)

            def transpose_h(b):
                wait(pe, s["hq_done"], b.number + 1)
                wait(pe, s["ht_read"], b.number)
                for c in range(HCH):
                    last = nc.tensor.transpose(h_tr[:, c * P:(c + 1) * P], hq[b.parity][:, c * P:(c + 1) * P], ident[:])
                last.then_inc(s["ht_ready"], 1)

            def down(b):
                wait(pe, s["ht_read"], b.number + 1)
                wait(pe, s["x_done"], b.number)
                for c in range(HCH):
                    last = nc.tensor.matmul(y_ps[:, 0:D], hq_t[b.parity][:, c * P:(c + 1) * P], wq[2][:, c * D:(c + 1) * D],
                                            start=c == 0, stop=c == HCH - 1)
                last.then_inc(s["y_ready"], 1)

            def step(b, one=True, two=True):
                if one:
                    gate_up(b.plus(1))
                if two:
                    transpose_x(b.plus(2))
                transpose_h(b)
                down(b)

            pe.wait_ge(s["set_done"], 4)
            pe.wait_ge(s["part_done"], 3)
            nc.tensor.matmul(y_ps[:, 0:3], ones[:], part[:], start=True, stop=True).then_inc(s["mean_ready"], 1)
            pe.wait_ge(s["xq_done"], B)
            transpose_x(fixed(0))
            pe.wait_ge(s["wq_done"], 3)
            gate_up(fixed(0))
            transpose_x(fixed(1))
            for n in range(2):
                step(fixed(n))
            paired_loop(pe, 2, B - 2, step)
            step(fixed(B - 2), two=False)
            step(fixed(B - 1), one=False, two=False)

        @block.vector
        def _(dve):
            col = lambda t, b: t[:, bass.ds(b.number, 1)]

            nc.vector.memset(eps[:], LN_EPS).then_inc(s["set_done"], 1)
            nc.vector.memset(half_neg[:], -0.5).then_inc(s["set_done"], 1)
            nc.vector.memset(ones[:], 1.0).then_inc(s["set_done"], 1)
            nc.vector.tensor_copy(ident[:], ident_f[:]).then_inc(s["set_done"], 1)
            for b in range(B):
                last = nc.vector.bn_aggr(mv[:, b, :], stats[:, b, :])
            last.then_inc(s["aggr"], 1)
            dve.wait_ge(s["sqrt_done"], 1)
            nc.vector.reciprocal(rstd[:], rstd[:]).then_inc(s["x_chain"], 1)
            dve.wait_ge(s["x_chain"], 1)
            for b in range(B):
                last = nc.vector.tensor_scalar(xn[:, b, :], xres[:, b, :], mv[:, b, 0:1], rstd[:, b:b + 1],
                                               ALU.subtract, ALU.mult)
            nc.vector.tensor_tensor(rms[:], rstd[:], rstd[:], ALU.mult).then_inc(s["x_chain"], 1)
            dve.wait_ge(s["x_chain"], 2)
            nc.vector.tensor_tensor(rms[:], rms[:], mv[:, :, 1], ALU.mult).then_inc(s["x_chain"], 1)
            dve.wait_ge(s["x_chain"], 3)
            nc.vector.tensor_scalar(rms[:], rms[:], RMS_EPS, None, ALU.add).then_inc(s["x_chain"], 1)
            nc.vector.tensor_reduce(amax[:], xn[:], AX.X, ALU.max, apply_absolute_value=True).then_inc(s["x_chain"], 1)
            dve.wait_ge(s["rms_done"], 1)
            dve.wait_ge(s["x_chain"], 5)
            nc.vector.tensor_tensor(amax[:], amax[:], rms[:], ALU.mult).then_inc(s["x_chain"], 1)
            dve.wait_ge(s["x_chain"], 6)
            nc.vector.tensor_scalar(unit[:], amax[:], Q_EPS, 1.0 / 127, ALU.max, ALU.mult).then_inc(s["x_chain"], 1)
            dve.wait_ge(s["x_chain"], 7)
            nc.vector.reciprocal(qs[:], unit[:]).then_inc(s["x_chain"], 1)
            dve.wait_ge(s["x_chain"], 8)
            for i in range(3):
                dve.wait_ge(w_in[i], 16)
                nc.vector.tensor_reduce(part[:, i:i + 1], wf[i][:], AX.X, ALU.add,
                                        apply_absolute_value=True).then_inc(s["part_done"], 1)
            dve.wait_ge(s["mean_ready"], 1)
            nc.vector.tensor_scalar(wmean[:], y_ps[:, 0:3], 1.0 / (D * FF), Q_EPS, ALU.mult, ALU.max).then_inc(s["w_chain"], 1)
            dve.wait_ge(s["w_chain"], 1)
            nc.vector.reciprocal(wscale[:], wmean[:]).then_inc(s["w_chain"], 1)
            nc.vector.tensor_scalar(gate_a[:], unit[:], wmean[:, 0:1], None, ALU.mult).then_inc(s["w_chain"], 1)
            nc.vector.tensor_scalar(up_a[:], unit[:], wmean[:, 1:2], None, ALU.mult).then_inc(s["w_chain"], 1)
            dve.wait_ge(s["w_chain"], 4)
            for i in range(3):
                nc.vector.tensor_scalar(wf[i][:], wf[i][:], wscale[:, i:i + 1], 1.0, ALU.mult, ALU.min).then_inc(s["w_chain"], 1)
                dve.wait_ge(s["w_chain"], 3 * i + 5)
                nc.vector.tensor_scalar(wf[i][:], wf[i][:], -1.0, ROUND, ALU.max, ALU.add).then_inc(s["w_chain"], 1)
                dve.wait_ge(s["w_chain"], 3 * i + 6)
                nc.vector.tensor_scalar(wq[i][:], wf[i][:], ROUND, None, ALU.subtract).then_inc(s["wq_done"], 1)
                nc.vector.memset(part[:, i:i + 1], 0.0).then_inc(s["w_chain"], 1)

            def product(b):
                wait(dve, s["silu_done"], b.number + 1)
                wait(dve, s["u_ready"], b.number + 1)
                wait(dve, s["sq_done"], b.number - 1)
                nc.vector.scalar_tensor_tensor(h[b.parity][:], u_ps[:], col(up_a, b), sg[b.parity][:],
                                               ALU.mult, ALU.mult).then_inc(s["h_done"], 1)

            def largest(b):
                wait(dve, s["h_done"], b.number + 1)
                nc.vector.tensor_reduce(col(hmax, b), h[b.parity][:], AX.X, ALU.max,
                                        apply_absolute_value=True).then_inc(s["max_done"], 1)

            def scales(b):
                n = b.number
                wait(dve, s["pow_done"], n + 1)
                wait(dve, s["max_done"], n + 1)
                nc.vector.tensor_scalar(col(hmax, b), col(hmax, b), hr[:, b.parity:b.parity + 1], Q_EPS, ALU.mult, ALU.max).then_inc(s["h_chain"], 1)
                wait(dve, s["h_chain"], 4 * n + 1)
                nc.vector.tensor_scalar(col(hunit, b), col(hmax, b), 1.0 / 127, None, ALU.mult).then_inc(s["h_chain"], 1)
                wait(dve, s["h_chain"], 4 * n + 2)
                nc.vector.reciprocal(col(hqs, b), col(hunit, b)).then_inc(s["h_chain"], 1)
                nc.vector.tensor_scalar(col(down_a, b), col(hunit, b), wmean[:, 2:3], gates[:, 3:4],
                                        ALU.mult, ALU.mult).then_inc(s["h_chain"], 1)

            def quantise(b):
                wait(dve, s["h_chain"], 4 * b.number + 4)
                wait(dve, s["hq_done"], b.number)
                nc.vector.tensor_scalar(hs[:], h[b.parity][:], hr[:, b.parity:b.parity + 1], col(hqs, b),
                                        ALU.mult, ALU.mult).then_inc(s["hs_done"], 1)
                wait(dve, s["hs_done"], b.number + 1)
                wait(dve, s["ht_ready"], b.number - 1)
                nc.vector.tensor_scalar(hq[b.parity][:], hs[:], ROUND, ROUND, ALU.add, ALU.subtract).then_inc(s["hq_done"], 1)

            def add_y(b):
                wait(dve, s["y_ready"], b.number + 1)
                nc.vector.scalar_tensor_tensor(xres[:, b.number, :], y_ps[:, 0:D], col(down_a, b), xres[:, b.number, :],
                                               ALU.mult, ALU.add).then_inc(s["x_done"], 1)

            def step(b, one=True, before=True):
                quantise(b)
                if one:
                    product(b.plus(1))
                    largest(b.plus(1))
                if before:
                    add_y(b.plus(-1))
                if one:
                    scales(b.plus(1))

            product(fixed(0))
            largest(fixed(0))
            scales(fixed(0))
            step(fixed(0), before=False)
            step(fixed(1))
            paired_loop(dve, 2, B - 2, step)
            step(fixed(B - 2))
            step(fixed(B - 1), one=False)
            add_y(fixed(B - 1))

        @block.scalar
        def _(act):
            def evacuate_x(b):
                wait(act, s["xt_ready"], b.number + 1)
                wait(act, s["u_ready"], b.number - 1)
                nc.scalar.activation(xq_t[b.parity][:].rearrange("p a n -> p (a n)"), x_tr[:],
                                     ACT.Copy).then_inc(s["xt_read"], 1)

            def silu(b):
                wait(act, s["g_ready"], b.number + 1)
                wait(act, s["h_done"], b.number - 1)
                nc.scalar.activation(sg[b.parity][:], g_ps[:], ACT.Silu,
                                     scale=gate_a[:, bass.ds(b.number, 1)]).then_inc(s["silu_done"], 1)

            def square(b):
                wait(act, s["h_done"], b.number + 1)
                wait(act, s["sq_done"], b.number)
                nc.scalar.activation(sq[:], h[b.parity][:], ACT.Square,
                                     accum_out=ssq[:, b.parity:b.parity + 1]).then_inc(s["sq_done"], 1)

            def evacuate_h(b):
                wait(act, s["ht_ready"], b.number + 1)
                wait(act, s["y_ready"], b.number - 1)
                nc.scalar.activation(hq_t[b.parity][:], h_tr[:], ACT.Copy).then_inc(s["ht_read"], 1)

            act.wait_ge(s["aggr"], 1)
            act.wait_ge(s["set_done"], 1)
            nc.scalar.activation(rstd[:], mv[:, :, 1], ACT.Sqrt, bias=eps[:, 0:1]).then_inc(s["sqrt_done"], 1)
            evacuate_x(fixed(0))
            act.wait_ge(s["w_chain"], 4)
            silu(fixed(0))
            evacuate_x(fixed(1))
            square(fixed(0))

            def step(b, one=True, two=True):
                if one:
                    silu(b.plus(1))
                evacuate_h(b)
                if two:
                    evacuate_x(b.plus(2))
                if one:
                    square(b.plus(1))
            for n in range(2):
                step(fixed(n))
            paired_loop(act, 2, B - 2, step)
            step(fixed(B - 2), two=False)
            step(fixed(B - 1), one=False, two=False)

        @block.gpsimd
        def _(pool):
            pool.wait_ge(s["set_done"], 2)
            pool.wait_ge(s["x_chain"], 4)
            nc.gpsimd.tensor_tensor(rms[:], rms[:], half_neg[:], ALU.pow).then_inc(s["rms_done"], 1)
            pool.wait_ge(s["x_chain"], 8)
            for b in range(B):
                nc.gpsimd.tensor_scalar(xn[:, b, :], xn[:, b, :], rms[:, b:b + 1], qs[:, b:b + 1], ALU.mult,
                                        ALU.mult).then_inc(s["rms_done"], 1)
            for b in range(B):
                pool.wait_ge(s["rms_done"], b + 2)
                nc.gpsimd.tensor_scalar(xq[:, b, :], xn[:, b, :], ROUND, ROUND, ALU.add,
                                        ALU.subtract).then_inc(s["xq_done"], 1)

            def inverse_root(b):
                wait(pool, s["sq_done"], b.number + 1)
                pool.nop(nofuse=True)
                at = slice(b.parity, b.parity + 1)
                nc.gpsimd.tensor_scalar(hms[:, at], ssq[:, at], 1.0 / FF, RMS_EPS, ALU.mult, ALU.add).then_inc(s["ms_done"], 1)
                wait(pool, s["ms_done"], b.number + 1)
                pool.nop(nofuse=True)
                nc.gpsimd.tensor_tensor(hr[:, at], hms[:, at], half_neg[:, 0:1], ALU.pow).then_inc(s["pow_done"], 1)
            for n in range(2):
                inverse_root(fixed(n))
            paired_loop(pool, 2, B, inverse_root)


def program(nc, x, ctx, mask, mask_col, gates, wq0, wk0, wv0, bq0, bk0, bv0, consts, ident,
            mix_w, router, select, rank, att_w, norm_w, bit_w, out):
    with ExitStack() as kept:
        def sb(name, shape):
            return kept.enter_context(nc.sbuf_tensor(name, shape, F32))

        shared = {"x": sb("x", [S, B, D]),
                  "stats": sb("stats", [S, B, 6]),
                  "ident": sb("ident", [P, P]), "gates": sb("gates", [P, 4]), "ident_dram": ident,
                  "gates_dram": gates, "mask_col_dram": mask_col, "semaphores": kept}
        with ExitStack() as mem:
            attention0(nc, mem, shared, x, ctx, mask, wq0, wk0, wv0, bq0, bk0, bv0, consts)
        with ExitStack() as mem:
            mixture(nc, mem, shared, mix_w, router, select, rank)
        with ExitStack() as mem:
            attention1(nc, mem, shared, att_w, norm_w, ctx)
        with ExitStack() as mem:
            bitlinear(nc, mem, shared, bit_w, out)


def attention0_consts():
    c = np.zeros((P, CONST_COLS), np.float32)
    for head in range(GH):
        for quadrant in range(3):
            c[32 * quadrant + HD0 * head:32 * quadrant + HD0 * (head + 1), head] = 1
        c[96 + head:96 + HEADS0:GH, head] = 1
        c[112:116, head] = 1
    c[112:114, 4], c[112:116, 5] = -1, 1
    c[114, 6], c[115, 6] = NEG_HI, NEG_LO
    for group in range(GROUPS):
        c[96 + GH * group:96 + GH * (group + 1), 7 + group] = 1
        c[[112, 114], 7 + group], c[[113, 115], 7 + group] = -NEG_HI, -NEG_LO
    return c


def expert_rows(expert, shared_expert):
    rows = np.zeros((CHUNKS * P, D), np.float32)
    n = expert.shape[0] * expert.shape[1]
    rows[:n] = expert.reshape(n, D)
    rows[n:n + shared_expert.shape[0]] = shared_expert
    return rows


def pack_mixture(gate_up, down, sh_gate, sh_up, sh_down):
    inner = gate_up.shape[1] // 2
    parts = []
    for expert, one in ((gate_up[:, :inner], sh_gate), (gate_up[:, inner:], sh_up)):
        rows = expert_rows(expert, one)
        parts.append(rows.reshape(CHUNKS, P, 2, P).transpose(0, 3, 2, 1).reshape(CHUNKS, P, D))
    parts.append(expert_rows(down.transpose(0, 2, 1), sh_down.T).reshape(CHUNKS, P, D))
    return np.concatenate(parts, axis=2)


def select_matrix(inner, shared_inner):
    owner = np.concatenate([np.repeat(np.arange(EXPERTS), inner), np.full(shared_inner, EXPERTS)])
    select = np.zeros((SEL_ROWS, CHUNKS * P), np.float32)
    rows = np.arange(owner.size)
    select[owner, rows] = 1
    select[SEL_ROWS // 2 + owner, rows] = 1
    return select


def pack_attention1(wk, wv, wq, wo):
    halves = slice(0, P), slice(P, D)
    pieces = [np.concatenate([wk[h], wv[h]], axis=1) for h in halves]
    pieces += [wq[h][:, c * 1024:(c + 1) * 1024] for h in halves for c in range(2)]
    pieces += list(wo.reshape(KV, HPK, HD1, D).transpose(0, 2, 1, 3).reshape(KV, HD1, HPK * D))
    return np.stack(pieces)


def pack_bitlinear(*weights):
    return np.stack([w.T.reshape(w.shape[1] // P, P, w.shape[0]).transpose(1, 0, 2).reshape(P, -1) for w in weights])


def kernel(**inputs):
    import concourse.bacc as bacc
    from concourse.bass_utils import run_bass_kernel_spmd

    a = {name: np.asarray(value) for name, value in inputs.items()}
    mask = a["mask_Bx1x2048_fk1"]
    l0 = {n: a["L0_ffn_" + n] for n in ("gate_up_proj", "down_proj", "sh_gate_w", "sh_up_w", "sh_down_w")}
    router = np.concatenate([a["L0_ffn_router_weight"], a["L0_ffn_shared_gate_w"]])
    layout = {
        "x": a["x"], "ctx": a["ctx_2048"], "mask": mask,
        "mask_col": mask.reshape(B, 2, P).transpose(2, 0, 1),
        "gates": np.concatenate([a["g_xattn"], a["g_ffn"]]).reshape(1, 4),
        "wq0": a["L0_xattn_Wq"].T, "wk0": a["L0_xattn_Wk"].T, "wv0": a["L0_xattn_Wv"].T,
        "bq0": a["L0_xattn_bq"].reshape(P, 1), "bk0": a["L0_xattn_bk"].reshape(P, 1),
        "bv0": a["L0_xattn_bv"].reshape(1, P),
        "consts": attention0_consts(), "ident": np.eye(P, dtype=np.float32),
        "mix_w": pack_mixture(*l0.values()),
        "router": router.T.reshape(2, P, EXPERTS + 1).transpose(1, 0, 2),
        "select": select_matrix(l0["gate_up_proj"].shape[1] // 2, l0["sh_gate_w"].shape[0]),
        "rank": np.tile(np.arange(EXPERTS, 0, -1, dtype=np.float32), (P, TILES, 1)),
        "att_w": pack_attention1(*(a["L1_xattn_" + n] for n in ("Wk", "Wv", "Wq", "Wo"))),
        "norm_w": np.stack([a["L1_xattn_q_norm_w"], a["L1_xattn_k_norm_w"]], axis=1),
        "bit_w": pack_bitlinear(*(a["L1_ffn_" + n] for n in ("w_gate", "w_up", "w_down"))),
    }
    nc = bacc.Bacc("TRN2", target_bir_lowering=False, num_devices=1)
    arrays, args = {}, []
    for name, value in layout.items():
        value = np.ascontiguousarray(value)
        arrays[f"in_{name}_dram"] = value
        args.append(nc.dram_tensor(f"in_{name}_dram", value.shape, mybir.dt.from_np(value.dtype),
                                   kind="ExternalInput").ap())
    args.append(nc.dram_tensor("out_0_dram", (B, S, D), F32, kind="ExternalOutput").ap())
    program(nc, *args)
    r = run_bass_kernel_spmd(nc, [arrays], core_ids=[0])
    return r.results[0]["out_0_dram"]
```

```python
from contextlib import ExitStack

import numpy as np

import concourse.bass as bass
from concourse import mybir

F32 = mybir.dt.float32
F32R = mybir.dt.float32r
BF16 = mybir.dt.bfloat16
ALU = mybir.AluOpType
ACT = mybir.ActivationFunctionType
AX = mybir.AxisListType

B, S, D = 16, 128, 256
P = 128
HEADS0, HD0 = 16, 8
GROUPS, GH = 4, 4
NEG_HI, NEG_LO = 999936.0, 64.0
LN_EPS = 1e-5
CONST_COLS = 11
N_WEIGHT_DMAS, N_CONST_DMAS = 6, 5
STAGE_COLS = 3072
FF = 1024
Q_EPS = 1e-5
ROUND = 12582912.0


class Batch:

    def __init__(self, number, half, parity):
        self.number, self.half, self.parity = number, half, parity

    def plus(self, n):
        parity = self.parity + n
        return Batch(self.number + n, self.half + parity // 2, parity % 2)


def fixed(n):
    return Batch(n, n // 2, n % 2)


def wait(engine, semaphore, value):
    if isinstance(value, int) and value <= 0:
        return
    engine.wait_ge(semaphore, value)


def paired_loop(engine, first, last, step):
    with engine.Fori(first // 2, last // 2) as half:
        for parity in range(2):
            step(Batch(half * 2 + parity, half, parity))


def attention0(nc, ctx_mem, shared, x, ctx, mask, wq, wk, wv, bq, bk, bv, consts):
    xres, ident, gates = shared["x"], shared["ident"], shared["gates"]

    def sb(name, shape, dt=F32):
        return ctx_mem.enter_context(nc.sbuf_tensor(name, shape, dt))

    def sem(name):
        return shared["semaphores"].enter_context(nc.semaphore(name))

    def ps(name, cols):
        return ctx_mem.enter_context(nc.psum_tensor(name, [P, cols], F32))

    w_sb = sb("a_w", [P, 3, P])
    bias = sb("a_bias", [P, 2])
    bv_row = sb("a_bv_row", [P, P])
    cst = sb("a_consts", [P, CONST_COLS])
    maskb = sb("a_maskb", [P, B, D])
    mask_col = sb("a_mask_col", [P, B, 2])
    stats = sb("a_stats", [P, B, 6])
    mv = sb("a_mv", [P, B, 2])
    rstd = sb("a_rstd", [P, B])
    eps = sb("a_eps", [P, 1])
    cbuf = [sb(f"a_ctx{i}", [P, D]) for i in range(2)]
    mrow = [sb(f"a_mrow{i}", [P, D]) for i in range(2)]
    xn = sb("a_xn", [P, D])
    full = [sb(f"a_full{i}", [P, D]) for i in range(2)]
    split = [sb(f"a_split{i}", [P, 2, D], F32R) for i in range(2)]
    qst = [sb(f"a_qst{i}", [P, GROUPS, D], F32R) for i in range(2)]
    krep = sb("a_krep", [P, GROUPS, D], F32R)
    qrep = sb("a_qrep", [P, GROUPS, D], F32R)
    kst = [sb(f"a_kst{i}", [P, GROUPS, GH, D], F32R) for i in range(2)]
    vt = sb("a_vt", [P, 2, P])
    mcb = sb("a_mcb", [P, 2])
    vst = [sb(f"a_vst{i}", [P, 2, HEADS0, P]) for i in range(2)]
    mx = sb("a_mx", [P, 2, HEADS0])
    probs = [sb(f"a_probs{i}", [P, 2, 2, D]) for i in range(2)]
    sums = sb("a_sums", [P, D])
    outs = sb("a_outs", [P, D])
    rinv = sb("a_rinv", [P, D])
    tmp = sb("a_tmp", [P, D])

    bit_f = sb("a_bit_f", [P, 3, 2 * FF])
    bit_sum = sb("a_bit_sum", [P, 3])
    ones = sb("a_ones", [P, P])
    bit_scale = sb("a_bit_scale", [P, 3])

    p1 = [ps(f"a_p1{i}", 512) for i in range(2)]
    p2 = [ps(f"a_p2{i}", 1024) for i in range(2)]
    pv = ps("a_pv", 512)
    misc = ps("a_misc", 512)

    names = """weights_in consts_in small_done vst_zero ones_done stats_done rstd_in rstd_done w_scaled zeroed ctx_in0 ctx_in1 mrow_in0 mrow_in1
        tanh_done mcb_done xn_ready qk_psum full_done hi_done split_done dist_q dist_k q3_krep q3_qrep q_stacked
        kst_dve kst_pool v_psum vt_ready vst_ready p1_ready mx_done mt_ready shift_done p2_ready
        exp_done pv_done evac_done fin_done rin_done bit_in bit_sums bit_mean bit_chain tmp_done """.split()
    s = {n: sem("a_" + n) for n in names}
    x_in = [sem(f"a_x_in{i}") for i in range(4)]

    C_SEL, C_QA, C_QB, C_KA, C_KB = 0, 4, 5, 6, 7

    with nc.Block() as block:

        @block.sync
        def _(sp):
            def load_x(i):
                sp.dma_start(xres[:, 4 * i:4 * i + 4, :],
                             x[4 * i:4 * i + 4].rearrange("b s d -> s b d")).then_inc(x_in[i], 16)

            def load(b):
                wait(sp, s["v_psum"], b.number - 1)
                wait(sp, s["qk_psum"], b.number - 1)
                sp.dma_start(cbuf[b.parity][:], ctx[b.number]).then_inc(s[f"ctx_in{b.parity}"], 16)
                wait(sp, s["q3_krep"], 4 * (b.number - 1))
                wait(sp, s["q3_qrep"], b.number - 1)
                sp.dma_start(mrow[b.parity][96:128, :].unsqueeze(1),
                             mask[b.number].partition_broadcast(32)).then_inc(s[f"mrow_in{b.parity}"], 16)

            def distribute(b):
                wait(sp, s["split_done"], 2 * b.number + 2)
                wait(sp, s["kst_dve"], 2 * b.number)
                wait(sp, s["kst_pool"], 2 * b.number)
                for quadrant, part in enumerate((0, 1, 0)):
                    for g in range(GROUPS):
                        sp.dma_start(krep[32 * quadrant:32 * quadrant + 32, g, :].bitcast(F32),
                                     split[1][32 * g:32 * g + 32, part, :].bitcast(F32)).then_inc(s["dist_k"], 16)
                wait(sp, s["q_stacked"], b.number)
                for quadrant, part in enumerate((0, 0, 1)):
                    for g in range(GROUPS):
                        sp.dma_start(qrep[32 * quadrant:32 * quadrant + 32, g, :].bitcast(F32),
                                     split[0][32 * g:32 * g + 32, part, :].bitcast(F32)).then_inc(s["dist_q"], 16)

            load_x(0)
            for dst, src in ((w_sb[:, 0, :], wq), (w_sb[:, 1, :], wk), (bias[:, 0:1], bq), (bias[:, 1:2], bk),
                             (maskb[:], mask.rearrange("b o t -> (b o) t").partition_broadcast(P)),
                             (cst[:], consts)):
                sp.dma_start(dst, src).then_inc(s["weights_in"], 16)
            load(fixed(0))
            for dst, src in ((w_sb[:, 2, :], wv), (ident[:], shared["ident_dram"]),
                             (bv_row[:].unsqueeze(1), bv.partition_broadcast(P)),
                             (gates[:].unsqueeze(1), shared["gates_dram"].partition_broadcast(P)),
                             (mask_col[:], shared["mask_col_dram"])):
                sp.dma_start(dst, src).then_inc(s["consts_in"], 16)
            load(fixed(1))
            distribute(fixed(0))
            for i in range(1, 4):
                load_x(i)
            sp.dma_start(bit_f[:], shared["bit_dram"].rearrange("i p n -> p i n")).then_inc(s["bit_in"], 16)

            def step(b):
                load(b.plus(2))
                distribute(b.plus(1))
            for n in range(2):
                step(fixed(n))
            paired_loop(sp, 2, B - 2, step)
            distribute(fixed(B - 1))
            for j in range(M_STAGES):
                sp.dma_start(shared["stage"][:, W_COLS * j:W_COLS * (j + 1)], shared["mix_dram"][j]).then_inc(shared["mix_staged"][j], 16)

        @block.tensor
        def _(pe):
            def project_qk(b):
                wait(pe, s[f"ctx_in{b.parity}"], 16 * (b.half + 1))
                wait(pe, s["xn_ready"], b.number + 1)
                wait(pe, s["vt_ready"], b.number - 1)
                wait(pe, s["shift_done"], b.number - 1)
                nc.tensor.matmul(misc[:, 0:D], w_sb[:, 0, :], xn[:], start=True, stop=True)
                nc.tensor.matmul(misc[:, D:2 * D], w_sb[:, 1, :], cbuf[b.parity][:],
                                 start=True, stop=True).then_inc(s["qk_psum"], 1)

            def project_v(b, ahead):
                wait(pe, s["shift_done"], b.number)
                wait(pe, s["full_done"], 2 * (b.number + ahead) + 2)
                for c in range(2):
                    last = nc.tensor.matmul(misc[:, c * P:(c + 1) * P], cbuf[b.parity][:, c * P:(c + 1) * P],
                                            w_sb[:, 2, :], start=True, stop=True)
                last.then_inc(s["v_psum"], 1)

            def pass1(b, half):
                tc, g, pair = half // (2 * GROUPS), half // 2 % GROUPS, half % 2
                if half == 0:
                    wait(pe, s["q_stacked"], b.number + 1)
                    wait(pe, s["kst_dve"], 2 * b.number + 2)
                    wait(pe, s["kst_pool"], 2 * b.number + 2)
                wait(pe, s["mx_done"], 16 * b.number + half - 1)
                nc.tensor.matmul(p1[pair][:], qst[b.parity][:, g, tc * P:(tc + 1) * P],
                                 kst[b.parity][:, g, 2 * pair:2 * pair + 2, :],
                                 start=True, stop=True).then_inc(s["p1_ready"], 1)

            def transpose_max(b, ahead):
                wait(pe, s["mx_done"], 16 * b.number + 16)
                wait(pe, s["full_done"], 2 * (b.number + ahead) + 2)
                wait(pe, s["vt_ready"], b.number + 1)
                for tc in range(2):
                    last = nc.tensor.transpose(misc[0:HEADS0, tc * P:(tc + 1) * P], mx[:, tc, :], ident[:])
                last.then_inc(s["mt_ready"], 1)

            def pass2(b, tile):
                if tile == 0:
                    wait(pe, s["shift_done"], b.number + 1)
                wait(pe, s["exp_done"], 8 * b.number + tile - 1)
                for k in range(2):
                    head = 2 * tile + k
                    for c in range(2):
                        last = nc.tensor.matmul(p2[tile % 2][:, (2 * k + c) * D:(2 * k + c + 1) * D],
                                                kst[b.parity][:, head // GH, head % GH, c * P:(c + 1) * P],
                                                qst[b.parity][:, head // GH, :], start=True, stop=True)
                last.then_inc(s["p2_ready"], 1)

            def weigh(b, tile, k):
                if tile == 0 and k == 0:
                    wait(pe, s["vst_ready"], 4 * b.number + 4)
                    wait(pe, s["evac_done"], 4 * b.number)
                if k == 0:
                    wait(pe, s["exp_done"], 8 * b.number + tile + 1)
                half = tile // 4
                for c in range(2):
                    last = nc.tensor.matmul(pv[:, half * D:(half + 1) * D],
                                            vst[b.parity][:, c, 2 * tile + k, :],
                                            probs[tile % 2][:, k, c, :],
                                            start=(tile % 4 == 0 and k == 0 and c == 0),
                                            stop=(tile % 4 == 3 and k == 1 and c == 1))
                if k == 1:
                    last.then_inc(s["pv_done"], 1)

            wait(pe, s["w_scaled"], 2)
            wait(pe, s["weights_in"], 16 * N_WEIGHT_DMAS)
            project_qk(fixed(0))
            wait(pe, s["consts_in"], 16 * N_CONST_DMAS)
            project_v(fixed(0), 0)
            wait(pe, s["vt_ready"], 1)
            project_qk(fixed(1))
            wait(pe, s["zeroed"], 1)
            for half in range(16):
                pass1(fixed(0), half)
            transpose_max(fixed(0), 1)
            pass2(fixed(0), 0)
            wait(pe, s["ones_done"], 2)

            def step(b, one=True, two=True):
                done = 0
                for tile, halves in zip(range(1, 7), (0, 3, 3, 3, 3, 4)):
                    turn = [halves // 3, halves // 3, halves - halves // 3 * 2] if one else [0] * 3
                    pass2(b, tile)
                    if two and tile == 1:
                        project_qk(b.plus(2))
                    if not one and tile == 5:
                        wait(pe, s["bit_sums"], 4)
                        nc.tensor.matmul(misc[:, 0:3], ones[:], bit_sum[:], start=True, stop=True).then_inc(s["bit_mean"], 1)
                    if one and tile == 2:
                        project_v(b.plus(1), int(two))
                    for part in range(3):
                        for _ in range(turn[part]):
                            pass1(b.plus(1), done)
                            done += 1
                        if part < 2:
                            weigh(b, tile - 1, part)
                pass2(b, 7)
                for k in range(2):
                    weigh(b, 6, k)
                    if one and k == 0:
                        transpose_max(b.plus(1), int(two))
                if one:
                    pass2(b.plus(1), 0)
                for k in range(2):
                    weigh(b, 7, k)
            for n in range(2):
                step(fixed(n))
            paired_loop(pe, 2, B - 2, step)
            step(fixed(B - 2), two=False)
            step(fixed(B - 1), one=False, two=False)

        @block.vector
        def _(dve):
            def row_statistics(group):
                n, cols = group, slice(4 * group, 4 * group + 4)
                dve.wait_ge(x_in[group], 16)
                for b in range(4 * group, 4 * group + 4):
                    last = nc.vector.bn_stats(stats[:, b, :], xres[:, b, :])
                last.then_inc(s["stats_done"], 1)
                dve.wait_ge(s["stats_done"], 2 * n + 1)
                for b in range(4 * group, 4 * group + 4):
                    last = nc.vector.bn_aggr(mv[:, b, :], stats[:, b, :])
                last.then_inc(s["stats_done"], 1)
                dve.wait_ge(s["rstd_in"], n + 1)
                nc.vector.reciprocal(rstd[:, cols], rstd[:, cols]).then_inc(s["rstd_done"], 1)
                dve.wait_ge(s["rstd_done"], n + 1)

            nc.vector.memset(eps[:], LN_EPS).then_inc(s["small_done"], 1)
            nc.vector.memset(mx[:], 0.0).then_inc(s["zeroed"], 1)
            row_statistics(0)
            dve.wait_ge(s["weights_in"], 16 * N_WEIGHT_DMAS)
            nc.vector.tensor_scalar(w_sb[:, 0, :], w_sb[:, 0, :], HD0 ** -0.5, None, ALU.mult).then_inc(s["w_scaled"], 1)
            nc.vector.tensor_scalar(bias[:, 0:1], bias[:, 0:1], HD0 ** -0.5, None, ALU.mult).then_inc(s["w_scaled"], 1)

            def normalise(b):
                wait(dve, s["qk_psum"], b.number)
                nc.vector.tensor_scalar(xn[:], xres[:, b.number, :], mv[:, b.number, 0:1],
                                        rstd[:, bass.ds(b.number, 1)],
                                        ALU.subtract, ALU.mult).then_inc(s["xn_ready"], 1)

            def full_qk(b):
                wait(dve, s["qk_psum"], b.number + 1)
                wait(dve, s["split_done"], 2 * b.number)
                for i in range(2):
                    nc.vector.scalar_tensor_tensor(full[i][:], misc[:, i * D:(i + 1) * D], bias[:, i:i + 1],
                                                   maskb[:, b.number, :], ALU.add, ALU.mult).then_inc(s["full_done"], 1)

            def split_qk(b):
                wait(dve, s["dist_k"], 16 * 12 * b.number)
                wait(dve, s["dist_q"], 16 * 12 * b.number)
                for i in range(2):
                    wait(dve, s["full_done"], 2 * b.number + i + 1)
                    nc.vector.tensor_copy(split[i][:, 0, :], full[i][:]).then_inc(s["hi_done"], 1)
                for i in range(2):
                    wait(dve, s["hi_done"], 2 * b.number + i + 1)
                    nc.vector.tensor_tensor(split[i][:, 1, :], full[i][:], split[i][:, 0, :].bitcast(F32),
                                            ALU.subtract).then_inc(s["split_done"], 1)

            def stack_k(b):
                wait(dve, s["dist_k"], 16 * 12 * (b.number + 1))
                wait(dve, s["q3_krep"], 4 * (b.number + 1))
                wait(dve, s["p2_ready"], 8 * (b.number - 1))
                for j in range(2):
                    nc.vector.tensor_scalar(kst[b.parity][:, :, j, :], krep[:].bitcast(F32), cst[:, C_SEL + j:C_SEL + j + 1],
                                            None, ALU.mult).then_inc(s["kst_dve"], 1)

            def value_bias(b):
                wait(dve, s["v_psum"], b.number + 1)
                wait(dve, s["vst_ready"], 4 * b.number)
                nc.vector.tensor_tensor(vt[:], misc[:, 0:D].rearrange("p (c n) -> p c n", c=2),
                                        bv_row[:].unsqueeze(1).broadcast_to([P, 2, P]), ALU.add).then_inc(s["vt_ready"], 1)
                nc.vector.tensor_copy(mcb[:], mask_col[:, b.number, :]).then_inc(s["mcb_done"], 1)

            def reduce_max(b, half):
                tc, g, pair = half // (2 * GROUPS), half // 2 % GROUPS, half % 2
                if half == 0:
                    wait(dve, s["mt_ready"], b.number)
                wait(dve, s["p1_ready"], 16 * b.number + half + 1)
                head = GH * g + 2 * pair
                nc.vector.tensor_reduce(mx[:, tc, head:head + 2], p1[pair][:].rearrange("p (h s) -> p h s", h=2),
                                        AX.X, ALU.max).then_inc(s["mx_done"], 1)

            def inverse(b):
                wait(dve, s["evac_done"], 4 * b.number + 4)
                nc.vector.reciprocal(rinv[:], sums[:]).then_inc(s["rin_done"], 1)

            def finish(b):
                nc.vector.scalar_tensor_tensor(tmp[:], outs[:], gates[:, 0:1], maskb[:, b.number, :],
                                               ALU.mult, ALU.mult).then_inc(s["tmp_done"], 1)
                dve.wait_ge(s["rin_done"], b.number + 1)
                dve.wait_ge(s["tmp_done"], 2 * b.number + 1)
                nc.vector.tensor_tensor(tmp[:], tmp[:], rinv[:], ALU.mult).then_inc(s["tmp_done"], 1)
                dve.wait_ge(s["tmp_done"], 2 * b.number + 2)
                nc.vector.tensor_tensor(xres[:, b.number, :], xres[:, b.number, :], tmp[:], ALU.add).then_inc(s["fin_done"], 1)
                dve.wait_ge(s["fin_done"], b.number + 1)
                nc.vector.bn_stats(shared["stats"][:, b.number, :], xres[:, b.number, :])

            normalise(fixed(0))
            dve.wait_ge(s["w_scaled"], 2)
            full_qk(fixed(0))
            split_qk(fixed(0))
            normalise(fixed(1))
            dve.wait_ge(s["consts_in"], 16 * N_CONST_DMAS)
            value_bias(fixed(0))
            full_qk(fixed(1))
            stack_k(fixed(0))
            split_qk(fixed(1))
            for half in range(16):
                reduce_max(fixed(0), half)
            for group in range(1, 4):
                row_statistics(group)
            dve.wait_ge(s["tanh_done"], 1)

            def step(b, one=True, two=True, before=True):
                def reduce(first, last):
                    if one:
                        for half in range(first, last):
                            reduce_max(b.plus(1), half)
                if two:
                    normalise(b.plus(2))
                if one:
                    stack_k(b.plus(1))
                if two:
                    full_qk(b.plus(2))
                    split_qk(b.plus(2))
                reduce(0, 3)
                if one:
                    value_bias(b.plus(1))
                reduce(3, 6)
                if before:
                    inverse(b.plus(-1))
                reduce(6, 9)
                if before:
                    finish(b.plus(-1))
                reduce(9, 16)
            step(fixed(0), before=False)
            step(fixed(1))
            paired_loop(dve, 2, B - 2, step)
            step(fixed(B - 2), two=False)
            step(fixed(B - 1), one=False, two=False)
            nc.vector.memset(ones[:], 1.0).then_inc(s["bit_sums"], 1)
            dve.wait_ge(s["bit_in"], 16)
            for i in range(3):
                nc.vector.tensor_reduce(bit_sum[:, i:i + 1], bit_f[:, i, :], AX.X, ALU.add,
                                        apply_absolute_value=True).then_inc(s["bit_sums"], 1)
            dve.wait_ge(s["bit_mean"], 1)
            nc.vector.tensor_scalar(shared["bit_mean"][:], misc[:, 0:3], 1.0 / (D * FF), Q_EPS,
                                    ALU.mult, ALU.max).then_inc(s["bit_chain"], 1)
            dve.wait_ge(s["bit_chain"], 1)
            nc.vector.reciprocal(bit_scale[:], shared["bit_mean"][:]).then_inc(s["bit_chain"], 1)
            dve.wait_ge(s["bit_chain"], 2)
            for i in range(3):
                nc.vector.tensor_scalar(bit_f[:, i, :], bit_f[:, i, :], bit_scale[:, i:i + 1], 1.0,
                                        ALU.mult, ALU.min).then_inc(s["bit_chain"], 1)
            for i in range(3):
                dve.wait_ge(s["bit_chain"], i + 3)
                nc.vector.tensor_scalar(bit_f[:, i, :], bit_f[:, i, :], -1.0, ROUND,
                                        ALU.max, ALU.add).then_inc(s["bit_chain"], 1)
            for i in range(3):
                dve.wait_ge(s["bit_chain"], i + 6)
                nc.vector.tensor_scalar(shared["bit_w"][i][:], bit_f[:, i, :], ROUND, None, ALU.subtract)
            inverse(fixed(B - 1))
            finish(fixed(B - 1))

        @block.scalar
        def _(act):
            def deviation(group):
                act.wait_ge(s["stats_done"], 2 * group + 2)
                cols = slice(4 * group, 4 * group + 4)
                nc.scalar.activation(rstd[:, cols], mv[:, cols, 1], ACT.Sqrt, bias=eps[:, 0:1]).then_inc(s["rstd_in"], 1)

            def stack_q(b):
                wait(act, s["dist_q"], 16 * 12 * (b.number + 1))
                wait(act, s["q3_qrep"], b.number + 1)
                wait(act, s["p2_ready"], 8 * (b.number - 1))
                nc.scalar.activation(qst[b.parity][:], qrep[:].bitcast(F32), ACT.Copy).then_inc(s["q_stacked"], 1)

            def shift(b):
                wait(act, s["mt_ready"], b.number + 1)
                nc.scalar.activation(qst[b.parity][96:96 + HEADS0, :, :],
                                     misc[0:HEADS0, 0:D].unsqueeze(1).broadcast_to([HEADS0, GROUPS, D]),
                                     ACT.Copy, scale=-1.0).then_inc(s["shift_done"], 1)

            def exps(b, tile):
                wait(act, s["p2_ready"], 8 * b.number + tile + 1)
                wait(act, s["pv_done"], 8 * b.number + tile - 1)
                nc.scalar.activation(probs[tile % 2][:].rearrange("p k c t -> p (k c t)"), p2[tile % 2][:],
                                     ACT.Exp).then_inc(s["exp_done"], 1)

            def evacuate(b):
                wait(act, s["pv_done"], 8 * b.number + 8)
                wait(act, s["fin_done"], b.number)
                for half in range(2):
                    own, other = slice(64 * half, 64 * half + 64), slice(64 - 64 * half, 128 - 64 * half)
                    for dst, rows in ((sums, other), (outs, own)):
                        nc.scalar.activation(dst[own, :], pv[rows, half * D:(half + 1) * D],
                                             ACT.Copy).then_inc(s["evac_done"], 1)

            act.wait_ge(s["small_done"], 1)
            deviation(0)
            stack_q(fixed(0))
            shift(fixed(0))
            for group in range(1, 4):
                deviation(group)
            act.wait_ge(s["consts_in"], 16 * N_CONST_DMAS)
            nc.scalar.activation(gates[:], gates[:], ACT.Tanh).then_inc(s["tanh_done"], 1)

            def step(b, one=True, before=True):
                for tile in range(8):
                    exps(b, tile)
                    if before and tile == 0:
                        evacuate(b.plus(-1))
                    if one and tile == 0:
                        stack_q(b.plus(1))
                if one:
                    shift(b.plus(1))
            step(fixed(0), before=False)
            step(fixed(1))
            paired_loop(act, 2, B - 2, step)
            step(fixed(B - 2))
            step(fixed(B - 1), one=False)
            evacuate(fixed(B - 1))

        @block.gpsimd
        def _(pool):
            def settle():
                pool.nop(nofuse=True)

            def mask_rows(b):
                wait(pool, s[f"mrow_in{b.parity}"], 16 * (b.half + 1))
                wait(pool, s["kst_dve"], 2 * b.number)
                wait(pool, s["kst_pool"], 2 * b.number)
                wait(pool, s["vst_ready"], 4 * b.number)
                settle()
                for g in range(GROUPS):
                    nc.gpsimd.tensor_scalar(krep[96:128, g, :], mrow[b.parity][96:128, :],
                                            cst[96:128, C_KA:C_KA + 1], cst[96:128, C_KB + g:C_KB + g + 1],
                                            ALU.mult, ALU.add).then_inc(s["q3_krep"], 1)
                wait(pool, s["q_stacked"], b.number)
                wait(pool, s["q3_krep"], 4 * (b.number + 1))
                settle()
                nc.gpsimd.tensor_scalar(qrep[96:128, :, :],
                                        mrow[b.parity][96:128, :].unsqueeze(1).broadcast_to([32, GROUPS, D]),
                                        cst[96:128, C_QA:C_QA + 1], cst[96:128, C_QB:C_QB + 1],
                                        ALU.mult, ALU.add).then_inc(s["q3_qrep"], 1)

            def stack_k(b):
                wait(pool, s["dist_k"], 16 * 12 * (b.number + 1))
                wait(pool, s["q3_qrep"], b.number + 1)
                wait(pool, s["p2_ready"], 8 * (b.number - 1))
                settle()
                for j in range(2, 4):
                    nc.gpsimd.tensor_scalar(kst[b.parity][:, :, j, :], krep[:].bitcast(F32), cst[:, C_SEL + j:C_SEL + j + 1],
                                            1.0, ALU.mult, ALU.mult).then_inc(s["kst_pool"], 1)

            def place_v(b):
                wait(pool, s["vt_ready"], b.number + 1)
                wait(pool, s["mcb_done"], b.number + 1)
                wait(pool, s["pv_done"], 8 * (b.number - 1))
                wait(pool, s["kst_pool"], 2 * (b.number + 1))
                settle()
                for c in range(2):
                    for half in range(2):
                        first = vst[b.parity][:, c, 8 * half:8 * half + 8, :]
                        flat = first.rearrange("p h n -> p (h n)")
                        out = bass.AP(flat.tensor, flat.offset + 64 * half, [list(flat.ap[0]), [P + 8, 8], [1, 8]])
                        nc.gpsimd.tensor_scalar(out, vt[:, c, 64 * half:64 * half + 64].rearrange("p (h n) -> p h n", h=8),
                                                mcb[:, c:c + 1],
                                                1.0, ALU.mult, ALU.mult).then_inc(s["vst_ready"], 1)

            pool.wait_ge(s["weights_in"], 16 * N_WEIGHT_DMAS)
            mask_rows(fixed(0))
            pool.wait_ge(s["q3_qrep"], 1)
            for i in range(2):
                nc.gpsimd.memset(vst[i][:], 0.0).then_inc(s["vst_zero"], 1)
            pool.wait_ge(s["vst_zero"], 2)
            for i in range(2):
                for half in range(2):
                    view = vst[i][:, :, 8 * half:8 * half + 8, :]
                    for h in range(8):
                        col = (64 if half == 0 else 0) + 8 * h
                        last = nc.gpsimd.memset(view[:, :, h, col:col + 8], 1.0)
                last.then_inc(s["ones_done"], 1)
            pool.wait_ge(s["ones_done"], 2)
            stack_k(fixed(0))
            place_v(fixed(0))
            mask_rows(fixed(1))

            def step(b):
                stack_k(b.plus(1))
                place_v(b.plus(1))
                mask_rows(b.plus(2))
            for n in range(2):
                step(fixed(n))
            paired_loop(pool, 2, B - 2, step)
            stack_k(fixed(B - 1))
            place_v(fixed(B - 1))


TILES, GROUPS_OF_TILES = 4, 4
TOK = TILES * S
EXPERTS = 8
M_STAGES = 4
CHUNKS = 17
W_COLS = 6 * P
SEL_ROWS = 32


def mixture(nc, mem, shared, weights, router, select, rank):
    xres, ident, gates, stats = shared["x"], shared["ident"], shared["gates"], shared["stats"]

    def sb(name, shape, dt=F32):
        return mem.enter_context(nc.sbuf_tensor("m_" + name, shape, dt))

    def ps(name, cols):
        return mem.enter_context(nc.psum_tensor("m_" + name, [P, cols], F32))

    stage = [shared["stage"][:, W_COLS * i:W_COLS * (i + 1)] for i in range(M_STAGES)]
    staged = shared["mix_staged"]
    w_hi = sb("w_hi", [P, CHUNKS, W_COLS], F32R)
    w_lo = sb("w_lo", [P, CHUNKS, W_COLS], F32R)
    router_sb = sb("router", [P, 2, EXPERTS + 1])
    select_f = sb("select_f", [SEL_ROWS, CHUNKS * P])
    select_r = sb("select_r", [SEL_ROWS, CHUNKS * P], F32R)
    rank_sb = sb("rank", [P, TILES, EXPERTS])
    mv = sb("mv", [P, B, 2])
    rstd = sb("rstd", [P, B])
    eps = sb("eps", [P, 1])
    xn = sb("xn", [P, TILES, D])
    xt = sb("xt", [P, 2, TOK])
    x_hi = sb("x_hi", [P, 2, TOK], F32R)
    x_lo = sb("x_lo", [P, 2, TOK], F32R)
    logit_t = sb("logit_t", [EXPERTS + 1, TOK])
    e = sb("e", [P, TILES, EXPERTS + 1])
    r1 = sb("r1", [P, TILES])
    w1 = sb("w1", [P, TILES, EXPERTS])
    w2 = sb("w2", [P, TILES, EXPERTS])
    comb = sb("comb", [P, TILES, SEL_ROWS])
    comb_hi = sb("comb_hi", [P, TILES, EXPERTS + 1], F32R)
    comb_f = sb("comb_f", [P, TILES, EXPERTS + 1])
    comb_t = sb("comb_t", [SEL_ROWS, TOK], F32R)
    sg = [sb(f"sg{i}", [P, TOK]) for i in range(2)]
    hid = [sb(f"hid{i}", [P, TOK]) for i in range(2)]
    h_hi = [sb(f"h_hi{i}", [P, TOK], F32R) for i in range(3)]
    h_lo = [sb(f"h_lo{i}", [P, TOK], F32R) for i in range(3)]
    yt = sb("yt", [P, 2, TOK])

    g_ps = [ps(f"g{i}", TOK) for i in range(2)]
    u_ps = [ps(f"u{i}", TOK) for i in range(2)]
    c_ps = ps("c", TOK)
    acc = [ps(f"acc{i}", TOK) for i in range(2)]
    misc = ps("misc", TOK)

    names = """in0 eps_done aggr sqrt_done rstd_done sel_done hi_w lo_w
        xn_done tr_ready tr_read split_hi split_lo router_ready logit_read nat_ready 
        route exp_done comb_done combt_ready combt_done comb_chain g_ready u_ready c_ready silu_done
        mul_done hid_done h_hi h_lo down_done yt_done y_ready y_read""".split()
    s = {n: shared["semaphores"].enter_context(nc.semaphore("m_" + n)) for n in names}
    last_chunk = CHUNKS - 1

    with nc.Block() as block:

        @block.sync
        def _(sp):
            for dst, src in ((router_sb[:], router), (select_f[:], select), (rank_sb[:], rank)):
                sp.dma_start(dst, src).then_inc(s["in0"], 16)
            for j in range(M_STAGES, CHUNKS):
                wait(sp, s["hi_w"], j - M_STAGES + 1)
                wait(sp, s["lo_w"], j - M_STAGES + 1)
                sp.dma_start(stage[j % M_STAGES], weights[j]).then_inc(staged[j % M_STAGES], 16)
            sp.wait_ge(s["hi_w"], CHUNKS)
            sp.wait_ge(s["lo_w"], CHUNKS)
            for j in range(C_STAGES):
                sp.dma_start(shared["stage"][:, 1024 * j:1024 * (j + 1)], shared["att_dram"][j]).then_inc(shared["att_staged"][j], 16)

        @block.tensor
        def _(pe):
            def transpose_x(n, kc):
                wait(pe, s["xn_done"], TILES * (n + 1))
                if kc == 0:
                    wait(pe, s["combt_done"], n)
                    wait(pe, s["y_read"], 2 * (n - 1))
                else:
                    wait(pe, s["tr_read"], 2 * n + 1)
                for t in range(TILES):
                    last = nc.tensor.transpose(misc[:, t * S:(t + 1) * S], xn[:, t, kc * P:(kc + 1) * P], ident[:])
                last.then_inc(s["tr_ready"], 1)

            def route_logits(n):
                wait(pe, s["tr_read"], 2 * n + 2)
                for kc in range(2):
                    last = nc.tensor.matmul(misc[0:EXPERTS + 1, :], router_sb[:, kc, :], xt[:, kc, :],
                                            start=kc == 0, stop=kc == 1)
                last.then_inc(s["router_ready"], 1)

            def transpose_logits(n):
                wait(pe, s["logit_read"], n + 1)
                pe.nop(nofuse=True)
                for t in range(TILES):
                    last = nc.tensor.transpose(misc[:, 16 * t:16 * t + EXPERTS + 1], logit_t[:, t * S:(t + 1) * S],
                                               ident[0:EXPERTS + 1, 0:EXPERTS + 1])
                last.then_inc(s["nat_ready"], 1)

            def transpose_comb(n):
                wait(pe, s["comb_done"], 2 * (n + 1))
                for t in range(TILES):
                    last = nc.tensor.transpose(misc[0:SEL_ROWS, t * S:(t + 1) * S], comb[:, t, :], ident[:])
                last.then_inc(s["combt_ready"], 1)

            def three(out, j, col, hi, lo, first, final):
                cols = slice(col, col + P)
                nc.tensor.matmul(out, w_hi[:, j, cols], hi, start=first, stop=False)
                nc.tensor.matmul(out, w_lo[:, j, cols], hi, start=False, stop=False)
                return nc.tensor.matmul(out, w_hi[:, j, cols], lo, start=False, stop=final)

            def up(n, j, group0):
                m = CHUNKS * n + j
                if group0:
                    wait(pe, s["hi_w"], j + 1)
                    wait(pe, s["lo_w"], j + 1)
                if j == 0:
                    wait(pe, s["split_hi"], n + 1)
                    wait(pe, s["split_lo"], n + 1)
                wait(pe, s["silu_done"], m - 1 if j else m)
                for kc in range(2):
                    last = three(g_ps[j % 2][:], j, kc * P, x_hi[:, kc, :], x_lo[:, kc, :], kc == 0, kc == 1)
                last.then_inc(s["g_ready"], 1)
                wait(pe, s["mul_done"], m - 1 if j else m)
                for kc in range(2):
                    last = three(u_ps[j % 2][:], j, (2 + kc) * P, x_hi[:, kc, :], x_lo[:, kc, :], kc == 0, kc == 1)
                last.then_inc(s["u_ready"], 1)
                if j == 0:
                    wait(pe, s["combt_done"], n + 1)
                wait(pe, s["hid_done"], m)
                nc.tensor.matmul(c_ps[:], select_r[:, j * P:(j + 1) * P], comb_t[:],
                                 start=True, stop=True).then_inc(s["c_ready"], 1)

            def down(n, j):
                m = CHUNKS * n + j
                wait(pe, s["h_hi"], m + 1)
                wait(pe, s["h_lo"], m + 1)
                if j == 0:
                    wait(pe, s["yt_done"], 2 * n)
                for fh in range(2):
                    last = three(acc[fh][:], j, (4 + fh) * P, h_hi[j % 3][:], h_lo[j % 3][:], j == 0, j == last_chunk)
                last.then_inc(s["down_done"], 1)

            def transpose_y(n, half, after):
                wait(pe, s["yt_done"], 2 * n + 2)
                if half == 0:
                    wait(pe, s["combt_done"], after)
                else:
                    wait(pe, s["y_read"], 2 * n + 1)
                for t in range(2):
                    for fh in range(2):
                        last = nc.tensor.transpose(misc[:, t * D + fh * P:t * D + (fh + 1) * P],
                                                   yt[:, fh, (2 * half + t) * S:(2 * half + t + 1) * S], ident[:])
                last.then_inc(s["y_ready"], 1)

            def group(n, first, final):
                for j in range(CHUNKS):
                    up(n, j, first)
                    if j < 2:
                        if not first:
                            down(n - 1, CHUNKS - 2 + j)
                    else:
                        down(n, j - 2)
                    if not first and j in (3, 4):
                        transpose_y(n - 1, j - 3, n + 1)
                    if not final:
                        if j in (6, 7):
                            transpose_x(n + 1, j - 6)
                        if j == 8:
                            route_logits(n + 1)
                        if j == 9:
                            transpose_logits(n + 1)
                        if j == 14:
                            transpose_comb(n + 1)

            wait(pe, s["in0"], 48)
            wait(pe, s["sel_done"], 2)
            transpose_x(0, 0)
            transpose_x(0, 1)
            route_logits(0)
            transpose_logits(0)
            transpose_comb(0)
            group(0, True, False)
            with pe.Fori(1, GROUPS_OF_TILES - 1) as n:
                group(n, False, False)
            group(GROUPS_OF_TILES - 1, False, True)
            for j in (CHUNKS - 2, CHUNKS - 1):
                down(GROUPS_OF_TILES - 1, j)
            for half in range(2):
                transpose_y(GROUPS_OF_TILES - 1, half, GROUPS_OF_TILES)

        @block.vector
        def _(dve):
            def normalise(n):
                wait(dve, s["tr_ready"], 2 * n)
                for t in range(TILES):
                    b = TILES * n + t
                    nc.vector.tensor_scalar(xn[:, t, :], xres[:, b, :], mv[:, b, 0:1], rstd[:, bass.ds(b, 1)],
                                            ALU.subtract, ALU.mult).then_inc(s["xn_done"], 1)

            def split_x(n):
                wait(dve, s["u_ready"], CHUNKS * n)
                wait(dve, s["tr_read"], 2 * n + 2)
                nc.vector.tensor_copy(x_hi[:], xt[:]).then_inc(s["split_hi"], 1)
                dve.wait_ge(s["split_hi"], n + 1)
                nc.vector.tensor_tensor(x_lo[:], xt[:], x_hi[:].bitcast(F32), ALU.subtract).then_inc(s["split_lo"], 1)

            def chain(ins, k):
                ins.then_inc(s["route"], 1)
                dve.wait_ge(s["route"], k)

            ROUTE = 15

            def route_a(n):
                base = ROUTE * n
                wait(dve, s["nat_ready"], n + 1)
                logits = misc[:, 0:64].rearrange("p (t c) -> p t c", c=16)
                chain(nc.vector.tensor_reduce(r1[:], logits[:, :, 0:EXPERTS], AX.X, ALU.max), base + 1)
                chain(nc.vector.tensor_tensor(e[:, :, 0:EXPERTS], logits[:, :, 0:EXPERTS],
                                              r1[:].unsqueeze(2).broadcast_to([P, TILES, EXPERTS]), ALU.subtract), base + 2)
                chain(nc.vector.tensor_scalar(e[:, :, EXPERTS:], logits[:, :, EXPERTS:EXPERTS + 1], -1.0, None, ALU.mult), base + 3)

            def pick(base, src, w):
                wide = [P, TILES, EXPERTS]
                chain(nc.vector.tensor_reduce(r1[:], src, AX.X, ALU.max), base + 1)
                chain(nc.vector.tensor_tensor(w[:], src, r1[:].unsqueeze(2).broadcast_to(wide), ALU.is_equal), base + 2)
                chain(nc.vector.tensor_tensor(w[:], w[:], rank_sb[:], ALU.mult), base + 3)
                chain(nc.vector.tensor_reduce(r1[:], w[:], AX.X, ALU.max), base + 4)
                chain(nc.vector.tensor_tensor(w[:], w[:], r1[:].unsqueeze(2).broadcast_to(wide), ALU.is_equal), base + 5)

            def route_b(n):
                base = ROUTE * n
                wait(dve, s["exp_done"], n + 1)
                wait(dve, s["combt_ready"], n)
                probs = e[:, :, 0:EXPERTS]
                pick(base + 3, probs, w1)
                ins = nc.vector.scalar_tensor_tensor(w2[:], w1[:], -4.0, probs, ALU.mult, ALU.add)
                chain(ins, base + 9)
                wide = [P, TILES, EXPERTS]
                chain(nc.vector.tensor_reduce(r1[:], w2[:], AX.X, ALU.max), base + 10)
                chain(nc.vector.tensor_tensor(w2[:], w2[:], r1[:].unsqueeze(2).broadcast_to(wide), ALU.is_equal), base + 11)
                chain(nc.vector.tensor_tensor(w2[:], w2[:], rank_sb[:], ALU.mult), base + 12)
                chain(nc.vector.tensor_reduce(r1[:], w2[:], AX.X, ALU.max), base + 13)
                chain(nc.vector.tensor_tensor(w2[:], w2[:], r1[:].unsqueeze(2).broadcast_to(wide), ALU.is_equal), base + 14)
                chain(nc.vector.tensor_tensor(w1[:], w1[:], w2[:], ALU.add), base + 15)

            COMB = 7

            def chain2(ins, k):
                ins.then_inc(s["comb_chain"], 1)
                dve.wait_ge(s["comb_chain"], k)

            def route_c(n):
                base = COMB * n
                wide = [P, TILES, EXPERTS]
                probs = e[:, :, 0:EXPERTS]
                chain2(nc.vector.tensor_tensor(w1[:], w1[:], probs, ALU.mult), base + 1)
                chain2(nc.vector.tensor_reduce(r1[:], w1[:], AX.X, ALU.add), base + 2)
                chain2(nc.vector.reciprocal(r1[:], r1[:]), base + 3)
                chain2(nc.vector.tensor_tensor(comb_f[:, :, 0:EXPERTS], w1[:],
                                               r1[:].unsqueeze(2).broadcast_to(wide), ALU.mult), base + 4)
                chain2(nc.vector.tensor_scalar(e[:, :, EXPERTS:], e[:, :, EXPERTS:], 1.0, None, ALU.add), base + 5)
                chain2(nc.vector.reciprocal(comb_f[:, :, EXPERTS:], e[:, :, EXPERTS:]), base + 6)
                chain2(nc.vector.tensor_copy(comb_hi[:], comb_f[:]), base + 7)
                nc.vector.tensor_copy(comb[:, :, 0:EXPERTS + 1], comb_hi[:].bitcast(F32)).then_inc(s["comb_done"], 1)
                nc.vector.tensor_tensor(comb[:, :, 16:17 + EXPERTS], comb_f[:], comb_hi[:].bitcast(F32),
                                        ALU.subtract).then_inc(s["comb_done"], 1)

            def split_weights(j):
                wait(dve, s["hi_w"], j + 1)
                nc.vector.tensor_tensor(w_lo[:, j, :], stage[j % M_STAGES], w_hi[:, j, :].bitcast(F32),
                                        ALU.subtract).then_inc(s["lo_w"], 1)

            def hidden(n, j):
                m = CHUNKS * n + j
                wait(dve, s["silu_done"], m + 1)
                wait(dve, s["u_ready"], m + 1)
                wait(dve, s["h_lo"], m - 1 if j else m)
                wait(dve, s["h_hi"], m - 1 if j else m)
                nc.vector.tensor_tensor(sg[j % 2][:], sg[j % 2][:], u_ps[j % 2][:], ALU.mult).then_inc(s["mul_done"], 1)
                wait(dve, s["mul_done"], m + 1)
                wait(dve, s["c_ready"], m + 1)
                nc.vector.tensor_tensor(hid[j % 2][:], sg[j % 2][:], c_ps[:], ALU.mult).then_inc(s["hid_done"], 1)

            def hidden_low(n, j):
                m = CHUNKS * n + j
                wait(dve, s["h_hi"], m + 1)
                nc.vector.tensor_tensor(h_lo[j % 3][:], hid[j % 2][:], h_hi[j % 3][:].bitcast(F32),
                                        ALU.subtract).then_inc(s["h_lo"], 1)

            def add_y(n, half):
                wait(dve, s["y_ready"], 2 * n + half + 1)
                tiles = xres[:, bass.ds(TILES * n + 2 * half, 2), :].rearrange("p t d -> p (t d)")
                nc.vector.scalar_tensor_tensor(tiles, misc[:], gates[:, 2:3], tiles, ALU.mult,
                                               ALU.add).then_inc(s["y_read"], 1)
                wait(dve, s["y_read"], 2 * n + half + 1)
                for t in range(2):
                    at = TILES * n + 2 * half + t
                    nc.vector.bn_stats(stats[:, at, :], xres[:, at, :])

            def group(n, first, final):
                for j in range(CHUNKS):
                    if first and j + 2 < CHUNKS:
                        split_weights(j + 2)
                    if j == 0 and not first:
                        hidden_low(n - 1, last_chunk)
                    hidden(n, j)
                    if j > 0:
                        hidden_low(n, j - 1)
                    if not first and j in (3, 4):
                        add_y(n - 1, j - 3)
                    if not final:
                        if j == 5:
                            normalise(n + 1)
                        if j == 10:
                            route_a(n + 1)
                        if j == 12:
                            route_b(n + 1)
                            route_c(n + 1)
                        if j == last_chunk:
                            split_x(n + 1)

            nc.vector.memset(eps[:], LN_EPS).then_inc(s["eps_done"], 1)
            nc.vector.memset(comb[:], 0.0).then_inc(s["sel_done"], 1)
            for b in range(B):
                last = nc.vector.bn_aggr(mv[:, b, :], stats[:, b, :])
            last.then_inc(s["aggr"], 1)
            dve.wait_ge(s["in0"], 48)
            nc.vector.tensor_copy(select_r[:], select_f[:]).then_inc(s["sel_done"], 1)
            dve.wait_ge(s["sqrt_done"], 1)
            nc.vector.reciprocal(rstd[:], rstd[:]).then_inc(s["rstd_done"], 1)
            dve.wait_ge(s["rstd_done"], 1)
            normalise(0)
            split_x(0)
            route_a(0)
            for j in range(2):
                split_weights(j)
            route_b(0)
            route_c(0)
            group(0, True, False)
            with dve.Fori(1, GROUPS_OF_TILES - 1) as n:
                group(n, False, False)
            group(GROUPS_OF_TILES - 1, False, True)
            hidden_low(GROUPS_OF_TILES - 1, last_chunk)
            for half in range(2):
                add_y(GROUPS_OF_TILES - 1, half)

        @block.scalar
        def _(act):
            def evacuate_x(n):
                for kc in range(2):
                    wait(act, s["tr_ready"], 2 * n + kc + 1)
                    if kc == 0:
                        wait(act, s["split_lo"], n)
                    nc.scalar.activation(xt[:, kc, :], misc[:], ACT.Copy).then_inc(s["tr_read"], 1)

            def evacuate_logits(n):
                wait(act, s["router_ready"], n + 1)
                nc.scalar.activation(logit_t[:], misc[0:EXPERTS + 1, :], ACT.Copy).then_inc(s["logit_read"], 1)

            def exp(n):
                wait(act, s["route"], 15 * n + 3)
                nc.scalar.activation(e[:], e[:], ACT.Exp).then_inc(s["exp_done"], 1)

            def evacuate_comb(n):
                wait(act, s["combt_ready"], n + 1)
                wait(act, s["c_ready"], CHUNKS * n)
                nc.scalar.activation(comb_t[:], misc[0:SEL_ROWS, :], ACT.Copy).then_inc(s["combt_done"], 1)

            def split_weights(j):
                wait(act, staged[j % M_STAGES], 16 * (j // M_STAGES + 1))
                nc.scalar.activation(w_hi[:, j, :], stage[j % M_STAGES], ACT.Copy).then_inc(s["hi_w"], 1)

            def silu(n, j):
                m = CHUNKS * n + j
                wait(act, s["g_ready"], m + 1)
                wait(act, s["hid_done"], m - 1 if j else m)
                nc.scalar.activation(sg[j % 2][:], g_ps[j % 2][:], ACT.Silu).then_inc(s["silu_done"], 1)

            def hidden_high(n, j):
                m = CHUNKS * n + j
                wait(act, s["hid_done"], m + 1)
                wait(act, s["down_done"], m - 1 if j < 2 else m - 2)
                nc.scalar.activation(h_hi[j % 3][:], hid[j % 2][:], ACT.Copy).then_inc(s["h_hi"], 1)

            def evacuate_y(n):
                wait(act, s["down_done"], CHUNKS * (n + 1))
                for fh in range(2):
                    nc.scalar.activation(yt[:, fh, :], acc[fh][:], ACT.Copy).then_inc(s["yt_done"], 1)

            def group(n, first, final):
                for j in range(CHUNKS):
                    silu(n, j)
                    if j > 0:
                        hidden_high(n, j - 1)
                    elif not first:
                        hidden_high(n - 1, last_chunk)
                    if first and j + 3 < CHUNKS:
                        split_weights(j + 3)
                    if not first and j == 2:
                        evacuate_y(n - 1)
                    if not final:
                        if j == 7:
                            evacuate_x(n + 1)
                        if j == 8:
                            evacuate_logits(n + 1)
                        if j == 11:
                            exp(n + 1)
                        if j == last_chunk:
                            evacuate_comb(n + 1)

            act.wait_ge(s["aggr"], 1)
            act.wait_ge(s["eps_done"], 1)
            nc.scalar.activation(rstd[:], mv[:, :, 1], ACT.Sqrt, bias=eps[:, 0:1]).then_inc(s["sqrt_done"], 1)
            evacuate_x(0)
            evacuate_logits(0)
            for j in range(2):
                split_weights(j)
            exp(0)
            evacuate_comb(0)
            split_weights(2)
            group(0, True, False)
            with act.Fori(1, GROUPS_OF_TILES - 1) as n:
                group(n, False, False)
            group(GROUPS_OF_TILES - 1, False, True)
            hidden_high(GROUPS_OF_TILES - 1, last_chunk)
            evacuate_y(GROUPS_OF_TILES - 1)


KV, HPK = 4, 4
HD1 = 128
RMS_EPS = 1e-6
C_STAGES = 3
PIECES = 10


def attention1(nc, mem, shared, weights, norm_w, ctx):
    xres, ident, gates, stats = shared["x"], shared["ident"], shared["gates"], shared["stats"]

    def sb(name, shape, dt=F32):
        return mem.enter_context(nc.sbuf_tensor("c_" + name, shape, dt))

    def ps(name):
        return mem.enter_context(nc.psum_tensor("c_" + name, [P, 512], F32))

    stage = [shared["stage"][:, 1024 * i:1024 * (i + 1)] for i in range(C_STAGES)]
    staged = shared["att_staged"]
    w_hi = sb("w_hi", [P, PIECES, 1024], F32R)
    w_lo = sb("w_lo", [P, PIECES, 1024], F32R)
    norm_sb = sb("norm", [P, 2])
    wqk = sb("wqk", [P, 1])
    mv = sb("mv", [P, B, 2])
    rstd = sb("rstd", [P, B])
    eps = sb("eps", [P, 1])
    half_neg = sb("half_neg", [P, KV])
    cbuf = [sb(f"ctx{i}", [P, D]) for i in range(2)]
    xn = sb("xn", [P, D])
    in_hi = sb("in_hi", [P, 4, P], F32R)
    in_lo = sb("in_lo", [P, 4, P], F32R)
    sq = [sb(f"sq{i}", [P, 512]) for i in range(2)]
    ssq = sb("ssq", [P, 5 * KV])
    ms = sb("ms", [P, 5 * KV])
    rms = sb("rms", [P, 5 * KV])
    kn = sb("kn", [P, 512])
    qn = [sb(f"qn{i}", [P, 512]) for i in range(2)]
    k_t = [sb(f"k_t{i}", [P, KV, P]) for i in range(2)]
    q_t = [sb(f"q_t{i}", [P, KV, 512]) for i in range(2)]
    v_sb = [sb(f"v{i}", [P, KV, HD1]) for i in range(2)]
    probs = [sb(f"probs{i}", [P, 512]) for i in range(4)]
    top = sb("top", [P, 4 * HPK])
    tot = sb("tot", [P, 4 * HPK])
    inv = sb("inv", [P, 4 * HPK])
    p_t = [sb(f"p_t{i}", [P, 512]) for i in range(2)]
    o_hi = [sb(f"o_hi{i}", [P, 512], F32R) for i in range(2)]
    o_lo = [sb(f"o_lo{i}", [P, 512], F32R) for i in range(2)]

    pj = [ps(f"pj{i}") for i in range(2)]
    tr = [ps(f"tr{i}") for i in range(2)]
    sc = [ps(f"sc{i}") for i in range(2)]
    pv = ps("pv")
    out = ps("out")

    names = """in0 hi_w lo_w eps_done aggr sqrt_done rstd_done wqk_done ctx_in0 ctx_in1 xn_done
        x_tr x_hi x_lo pj_ready sq_done ssq_done ms_done rms_done mul_done v_read kt_tr kt_read qt_tr qt_read
        sc_ready max_done sub_done exp_done sum_done inv_done norm_done pt_tr pt_read pv_ready o_hi o_lo
        out_ready x_done""".split()
    s = {n: shared["semaphores"].enter_context(nc.semaphore("c_" + n)) for n in names}

    def heads(ap):
        return ap.rearrange("p (h n) -> p h n", h=4)

    def spread(ap):
        return ap.unsqueeze(2).broadcast_to([P, 4, 128])

    with nc.Block() as block:

        @block.sync
        def _(sp):
            def step(b):
                wait(sp, s["x_tr"], b.number - 1)
                sp.dma_start(cbuf[b.parity][:], ctx[b.number]).then_inc(s[f"ctx_in{b.parity}"], 16)
            sp.dma_start(norm_sb[:], norm_w).then_inc(s["in0"], 16)
            for n in range(2):
                step(fixed(n))
            for j in range(C_STAGES, PIECES):
                wait(sp, s["hi_w"], j - C_STAGES + 1)
                wait(sp, s["lo_w"], j - C_STAGES + 1)
                sp.dma_start(stage[j % C_STAGES], weights[j]).then_inc(staged[j % C_STAGES], 16)
            paired_loop(sp, 2, B, step)

        @block.tensor
        def _(pe):
            def transpose_in(b):
                wait(pe, s["xn_done"], b.number + 1)
                wait(pe, s[f"ctx_in{b.parity}"], 16 * (b.half + 1))
                wait(pe, s["kt_read"], b.number)
                wait(pe, s["pt_read"], 4 * (b.number - 1))
                for src, at in ((xn, 0), (cbuf[b.parity], 2)):
                    for kc in range(2):
                        last = nc.tensor.transpose(tr[0][:, (at + kc) * P:(at + kc + 1) * P],
                                                   src[:, kc * P:(kc + 1) * P], ident[:])
                last.then_inc(s["x_tr"], 1)

            def project(a, c, loading=False):
                n = a.number
                if c == 0:
                    wait(pe, s["x_hi"], n + 1)
                    wait(pe, s["x_lo"], n + 1)
                if loading:
                    wait(pe, s["hi_w"], 2 * (c // 2) + 2)
                    wait(pe, s["lo_w"], 2 * (c // 2) + 2)
                if c == 3:
                    wait(pe, s["v_read"], n + 1)
                else:
                    wait(pe, s["mul_done"], 5 * n + {0: -1, 1: 0, 2: 1, 4: 2, 5: 3}[c])
                for kc in range(2):
                    row = kc + (2 if c < 2 else 0)
                    if c < 2:
                        w = (kc, c * 512)
                    else:
                        w = (c // 2 * 2 + kc, (c % 2) * 512)
                    wh, wl = (t[:, w[0], w[1]:w[1] + 512] for t in (w_hi, w_lo))
                    nc.tensor.matmul(pj[c % 2][:], in_hi[:, row, :], wh, start=kc == 0, stop=False)
                    nc.tensor.matmul(pj[c % 2][:], in_hi[:, row, :], wl, start=False, stop=False)
                    last = nc.tensor.matmul(pj[c % 2][:], in_lo[:, row, :], wh, start=False, stop=kc == 1)
                last.then_inc(s["pj_ready"], 1)

            def transpose_k(a, b_runs):
                if b_runs:
                    wait(pe, s["pt_read"], 4 * (a.number - 1) + 2)
                wait(pe, s["mul_done"], 5 * a.number + 1)
                wait(pe, s["x_lo"], a.number + 1)
                wait(pe, s["x_hi"], a.number + 1)
                for i in range(KV):
                    last = nc.tensor.transpose(tr[0][:, i * P:(i + 1) * P], kn[:, i * P:(i + 1) * P], ident[:])
                last.then_inc(s["kt_tr"], 1)

            def transpose_q(a, i):
                wait(pe, s["mul_done"], 5 * a.number + 2 + i)
                if i == 0:
                    wait(pe, s["pt_read"], 4 * (a.number - 1) + 1)
                else:
                    wait(pe, s["qt_read"], 4 * a.number + i)
                for h in range(HPK):
                    last = nc.tensor.transpose(tr[1][:, h * P:(h + 1) * P], qn[i % 2][:, h * P:(h + 1) * P], ident[:])
                last.then_inc(s["qt_tr"], 1)

            def transpose_p(b, i, a_runs):
                wait(pe, s["norm_done"], 4 * b.number + i + 1)
                if i == 0:
                    wait(pe, s["qt_read"], 4 * (b.number + 1))
                elif i == 1:
                    if a_runs:
                        wait(pe, s["x_hi"], b.number + 2)
                        wait(pe, s["x_lo"], b.number + 2)
                    wait(pe, s["pt_read"], 4 * b.number)
                elif i == 2:
                    wait(pe, s["pt_read"], 4 * b.number + 2)
                    if a_runs:
                        wait(pe, s["kt_read"], b.number + 2)
                else:
                    wait(pe, s["pt_read"], 4 * b.number + i)
                for h in range(HPK):
                    last = nc.tensor.transpose(tr[0 if i else 1][:, h * P:(h + 1) * P],
                                               probs[i][:, h * P:(h + 1) * P], ident[:])
                last.then_inc(s["pt_tr"], 1)

            def score(b, i):
                if i == 0:
                    wait(pe, s["kt_read"], b.number + 1)
                wait(pe, s["qt_read"], 4 * b.number + i + 1)
                wait(pe, s["sub_done"], 4 * b.number + i - 1)
                for h in range(HPK):
                    last = nc.tensor.matmul(sc[i % 2][:, h * P:(h + 1) * P], q_t[b.parity][:, i, h * P:(h + 1) * P],
                                            k_t[b.parity][:, i, :], start=True, stop=True)
                last.then_inc(s["sc_ready"], 1)

            def weigh(b, i):
                if i == 0:
                    wait(pe, s["v_read"], b.number + 1)
                wait(pe, s["pt_read"], 4 * b.number + i + 1)
                wait(pe, s["o_hi"], 4 * b.number + i)
                wait(pe, s["o_lo"], 4 * b.number + i)
                nc.tensor.matmul(pv[:], v_sb[b.parity][:, i, :], p_t[i % 2][:], start=True, stop=True).then_inc(s["pv_ready"], 1)

            def project_out(b, i):
                wait(pe, s["o_hi"], 4 * b.number + i + 1)
                wait(pe, s["o_lo"], 4 * b.number + i + 1)
                if i == 0:
                    wait(pe, s["x_done"], b.number)
                for h in range(HPK):
                    wh, wl = (t[:, 6 + i, h * D:(h + 1) * D] for t in (w_hi, w_lo))
                    oh, ol = (t[i % 2][:, h * P:(h + 1) * P] for t in (o_hi, o_lo))
                    nc.tensor.matmul(out[:, 0:D], oh, wh, start=i == 0 and h == 0, stop=False)
                    nc.tensor.matmul(out[:, 0:D], oh, wl, start=False, stop=False)
                    last = nc.tensor.matmul(out[:, 0:D], ol, wh, start=False, stop=i == 3 and h == 3)
                last.then_inc(s["out_ready"], 1)

            def step(b, do_b=True, do_a=True, do_x=True, before=True, loading=False):
                a = b.plus(1)
                if do_b:
                    score(b, 0)
                if do_a:
                    project(a, 0, loading)
                if do_b and before:
                    project_out(b.plus(-1), 3)
                if do_a:
                    project(a, 1, loading)
                if do_b:
                    score(b, 1)
                if do_a:
                    project(a, 2, loading)
                if do_b:
                    transpose_p(b, 0, do_a)
                    score(b, 2)
                if do_a:
                    project(a, 3, loading)
                if do_b:
                    weigh(b, 0)
                    transpose_p(b, 1, do_a)
                if do_a:
                    transpose_q(a, 0)
                    project(a, 4, loading)
                    transpose_k(a, do_b)
                if do_b:
                    score(b, 3)
                    weigh(b, 1)
                    project_out(b, 0)
                    transpose_p(b, 2, do_a)
                if do_a:
                    transpose_q(a, 1)
                    project(a, 5, loading)
                if do_b:
                    weigh(b, 2)
                    project_out(b, 1)
                    transpose_p(b, 3, do_a)
                if do_a:
                    transpose_q(a, 2)
                if do_b:
                    project_out(b, 2)
                if do_x:
                    transpose_in(b.plus(2))
                if do_b:
                    weigh(b, 3)
                if do_a:
                    transpose_q(a, 3)

            step(fixed(-2), do_b=False, do_a=False)
            step(fixed(-1), do_b=False, loading=True)
            wait(pe, s["hi_w"], PIECES)
            wait(pe, s["lo_w"], PIECES)
            step(fixed(0), before=False)
            step(fixed(1))
            paired_loop(pe, 2, B - 2, step)
            step(fixed(B - 2), do_x=False)
            step(fixed(B - 1), do_a=False, do_x=False)
            project_out(fixed(B - 1), 3)

        @block.vector
        def _(dve):
            def split_weights(first, last):
                for j in range(first, last):
                    wait(dve, s["hi_w"], j + 1)
                    nc.vector.tensor_tensor(w_lo[:, j, :], stage[j % C_STAGES], w_hi[:, j, :].bitcast(F32),
                                            ALU.subtract).then_inc(s["lo_w"], 1)

            def normalise(b):
                wait(dve, s["x_tr"], b.number)
                nc.vector.tensor_scalar(xn[:], xres[:, b.number, :], mv[:, b.number, 0:1], rstd[:, bass.ds(b.number, 1)],
                                        ALU.subtract, ALU.mult).then_inc(s["xn_done"], 1)

            def split_in(b):
                wait(dve, s["x_hi"], b.number + 1)
                wait(dve, s["pj_ready"], 6 * b.number)
                nc.vector.tensor_tensor(in_lo[:].rearrange("p a n -> p (a n)"), tr[0][:],
                                        in_hi[:].bitcast(F32).rearrange("p a n -> p (a n)"), ALU.subtract).then_inc(s["x_lo"], 1)

            def sum_squares(a, k):
                wait(dve, s["sq_done"], 5 * a.number + k + 1)
                nc.vector.tensor_reduce(ssq[:, 4 * k:4 * k + 4], heads(sq[k % 2][:]),
                                        AX.X, ALU.add).then_inc(s["ssq_done"], 1)

            def scale(a, k):
                wait(dve, s["rms_done"], 5 * a.number + k + 1)
                if k == 0:
                    wait(dve, s["kt_tr"], a.number)
                    dst = kn
                else:
                    wait(dve, s["qt_tr"], 4 * a.number + k - 2)
                    dst = qn[(k - 1) % 2]
                bank = 0 if k == 0 else (k + 1) % 2
                nc.vector.tensor_tensor(heads(dst[:]), heads(pj[bank][:]), spread(rms[:, 4 * k:4 * k + 4]),
                                        ALU.mult).then_inc(s["mul_done"], 1)

            def evacuate_k(a):
                wait(dve, s["kt_tr"], a.number + 1)
                wait(dve, s["sc_ready"], 4 * (a.number - 1))
                nc.vector.tensor_scalar(k_t[a.parity][:].rearrange("p a n -> p (a n)"), tr[0][:], wqk[:, 0:1], None,
                                        ALU.mult).then_inc(s["kt_read"], 1)

            def shift(b, i):
                wait(dve, s["sc_ready"], 4 * b.number + i + 1)
                nc.vector.tensor_reduce(top[:, 4 * i:4 * i + 4], heads(sc[i % 2][:]), AX.X, ALU.max).then_inc(s["max_done"], 1)
                wait(dve, s["max_done"], 4 * b.number + i + 1)
                wait(dve, s["pt_tr"], 4 * (b.number - 1) + i + 1)
                nc.vector.tensor_tensor(heads(probs[i][:]), heads(sc[i % 2][:]), spread(top[:, 4 * i:4 * i + 4]),
                                        ALU.subtract).then_inc(s["sub_done"], 1)

            def total(b, i):
                wait(dve, s["exp_done"], 4 * b.number + i + 1)
                nc.vector.tensor_reduce(tot[:, 4 * i:4 * i + 4], heads(probs[i][:]), AX.X, ALU.add).then_inc(s["sum_done"], 1)
                wait(dve, s["sum_done"], 4 * b.number + i + 1)
                nc.vector.reciprocal(inv[:, 4 * i:4 * i + 4], tot[:, 4 * i:4 * i + 4]).then_inc(s["inv_done"], 1)

            def split_out(b, i):
                wait(dve, s["o_hi"], 4 * b.number + i + 1)
                wait(dve, s["out_ready"], 4 * b.number + i - 1)
                nc.vector.tensor_tensor(o_lo[i % 2][:], pv[:], o_hi[i % 2][:].bitcast(F32), ALU.subtract).then_inc(s["o_lo"], 1)

            def add_out(b):
                wait(dve, s["out_ready"], 4 * b.number + 4)
                nc.vector.scalar_tensor_tensor(xres[:, b.number, :], out[:, 0:D], gates[:, 1:2], xres[:, b.number, :],
                                               ALU.mult, ALU.add).then_inc(s["x_done"], 1)
                wait(dve, s["x_done"], b.number + 1)
                nc.vector.bn_stats(stats[:, b.number, :], xres[:, b.number, :])

            def step(b, do_b=True, do_a=True, do_x=True, before=True, loading=False):
                a = b.plus(1)
                if do_b:
                    shift(b, 0)
                if do_a:
                    sum_squares(a, 0)
                if do_b:
                    total(b, 0)
                if do_a:
                    scale(a, 0)
                if loading:
                    split_weights(2, 4)
                if do_b:
                    shift(b, 1)
                if do_a:
                    sum_squares(a, 1)
                if do_b:
                    total(b, 1)
                if do_a:
                    scale(a, 1)
                if loading:
                    split_weights(4, 6)
                if do_b:
                    shift(b, 2)
                if do_a:
                    sum_squares(a, 2)
                if do_b:
                    total(b, 2)
                    split_out(b, 0)
                    if before:
                        add_out(b.plus(-1))
                if do_a:
                    evacuate_k(a)
                    scale(a, 2)
                    sum_squares(a, 3)
                if do_b:
                    shift(b, 3)
                    split_out(b, 1)
                    total(b, 3)
                if do_a:
                    scale(a, 3)
                    sum_squares(a, 4)
                if do_b:
                    split_out(b, 2)
                if do_x:
                    normalise(b.plus(2))
                if do_a:
                    scale(a, 4)
                if do_x:
                    split_in(b.plus(2))
                if do_b:
                    split_out(b, 3)

            nc.vector.memset(eps[:], LN_EPS).then_inc(s["eps_done"], 1)
            nc.vector.memset(half_neg[:], -0.5).then_inc(s["eps_done"], 1)
            for b in range(B):
                last = nc.vector.bn_aggr(mv[:, b, :], stats[:, b, :])
            last.then_inc(s["aggr"], 1)
            dve.wait_ge(s["in0"], 16)
            nc.vector.scalar_tensor_tensor(wqk[:], norm_sb[:, 0:1], HD1 ** -0.5, norm_sb[:, 1:2],
                                           ALU.mult, ALU.mult).then_inc(s["wqk_done"], 1)
            dve.wait_ge(s["sqrt_done"], 1)
            nc.vector.reciprocal(rstd[:], rstd[:]).then_inc(s["rstd_done"], 1)
            dve.wait_ge(s["rstd_done"], 1)
            dve.wait_ge(s["wqk_done"], 1)
            step(fixed(-2), do_b=False, do_a=False)
            split_weights(0, 2)
            step(fixed(-1), do_b=False, loading=True)
            split_weights(6, PIECES)
            step(fixed(0), before=False)
            step(fixed(1))
            paired_loop(dve, 2, B - 2, step)
            step(fixed(B - 2), do_x=False)
            step(fixed(B - 1), do_a=False, do_x=False)
            add_out(fixed(B - 1))

        @block.scalar
        def _(act):
            def copy(dst, src):
                return nc.scalar.activation(dst, src, ACT.Copy)

            def split_weights(first, last):
                for j in range(first, last):
                    wait(act, staged[j % C_STAGES], 16 * (j // C_STAGES + 1))
                    copy(w_hi[:, j, :], stage[j % C_STAGES]).then_inc(s["hi_w"], 1)

            def square(a, k):
                c = 0 if k == 0 else k + 1
                wait(act, s["pj_ready"], 6 * a.number + c + 1)
                wait(act, s["ssq_done"], 5 * a.number + k - (1 if k else 0))
                nc.scalar.activation(sq[k % 2][:], pj[c % 2][:], ACT.Square).then_inc(s["sq_done"], 1)

            def values(a):
                wait(act, s["pj_ready"], 6 * a.number + 2)
                wait(act, s["pv_ready"], 4 * (a.number - 1))
                copy(v_sb[a.parity][:].rearrange("p a n -> p (a n)"), pj[1][:]).then_inc(s["v_read"], 1)

            def exp(b, i):
                wait(act, s["sub_done"], 4 * b.number + i + 1)
                nc.scalar.activation(probs[i][:], probs[i][:], ACT.Exp).then_inc(s["exp_done"], 1)

            def evacuate_p(b, i):
                wait(act, s["pt_tr"], 4 * b.number + i + 1)
                wait(act, s["pv_ready"], 4 * b.number + i - 1)
                copy(p_t[i % 2][:], tr[0 if i else 1][:]).then_inc(s["pt_read"], 1)

            def evacuate_q(a, i):
                wait(act, s["qt_tr"], 4 * a.number + i + 1)
                wait(act, s["sc_ready"], 4 * (a.number - 1))
                copy(q_t[a.parity][:, i, :], tr[1][:]).then_inc(s["qt_read"], 1)

            def split_out(b, i):
                wait(act, s["pv_ready"], 4 * b.number + i + 1)
                wait(act, s["out_ready"], 4 * b.number + i - 1)
                copy(o_hi[i % 2][:], pv[:]).then_inc(s["o_hi"], 1)

            def split_in(b):
                wait(act, s["x_tr"], b.number + 1)
                wait(act, s["pj_ready"], 6 * b.number)
                copy(in_hi[:].rearrange("p a n -> p (a n)"), tr[0][:]).then_inc(s["x_hi"], 1)

            def step(b, do_b=True, do_a=True, do_x=True, loading=False):
                a = b.plus(1)
                if do_a:
                    square(a, 0)
                if do_b:
                    exp(b, 0)
                if do_a:
                    values(a)
                if loading:
                    split_weights(2, 4)
                if do_a:
                    square(a, 1)
                if do_b:
                    exp(b, 1)
                    evacuate_p(b, 0)
                if do_a:
                    square(a, 2)
                if loading:
                    split_weights(4, 6)
                if do_b:
                    exp(b, 2)
                    split_out(b, 0)
                    evacuate_p(b, 1)
                if do_a:
                    evacuate_q(a, 0)
                    square(a, 3)
                if do_b:
                    exp(b, 3)
                    split_out(b, 1)
                    evacuate_p(b, 2)
                if do_a:
                    evacuate_q(a, 1)
                    square(a, 4)
                if do_b:
                    split_out(b, 2)
                    evacuate_p(b, 3)
                if do_a:
                    evacuate_q(a, 2)
                if do_x:
                    split_in(b.plus(2))
                if do_b:
                    split_out(b, 3)
                if do_a:
                    evacuate_q(a, 3)

            act.wait_ge(s["aggr"], 1)
            act.wait_ge(s["eps_done"], 1)
            nc.scalar.activation(rstd[:], mv[:, :, 1], ACT.Sqrt, bias=eps[:, 0:1]).then_inc(s["sqrt_done"], 1)
            step(fixed(-2), do_b=False, do_a=False)
            split_weights(0, 2)
            step(fixed(-1), do_b=False, loading=True)
            split_weights(6, PIECES)
            for n in range(2):
                step(fixed(n))
            paired_loop(act, 2, B - 2, step)
            step(fixed(B - 2), do_x=False)
            step(fixed(B - 1), do_a=False, do_x=False)

        @block.gpsimd
        def _(pool):
            def settle():
                pool.nop(nofuse=True)

            def root(a, k):
                n = 5 * a.number + k
                cols = slice(4 * k, 4 * k + 4)
                wait(pool, s["ssq_done"], n + 1)
                settle()
                nc.gpsimd.tensor_scalar(ms[:, cols], ssq[:, cols], 1.0 / HD1, RMS_EPS, ALU.mult, ALU.add).then_inc(s["ms_done"], 1)
                wait(pool, s["ms_done"], n + 1)
                settle()
                nc.gpsimd.tensor_tensor(rms[:, cols], ms[:, cols], half_neg[:], ALU.pow).then_inc(s["rms_done"], 1)

            def norm(b, i):
                wait(pool, s["inv_done"], 4 * b.number + i + 1)
                settle()
                nc.gpsimd.tensor_tensor(heads(probs[i][:]), heads(probs[i][:]), spread(inv[:, 4 * i:4 * i + 4]),
                                        ALU.mult).then_inc(s["norm_done"], 1)

            def step(b, do_b=True, do_a=True):
                for i in range(4):
                    if do_a:
                        root(b.plus(1), i)
                    if do_b:
                        norm(b, i)
                if do_a:
                    root(b.plus(1), 4)

            pool.wait_ge(s["eps_done"], 2)
            step(fixed(-1), do_b=False)
            for n in range(2):
                step(fixed(n))
            paired_loop(pool, 2, B - 2, step)
            step(fixed(B - 2))
            step(fixed(B - 1), do_a=False)


HCH = FF // P


def bitlinear(nc, mem, shared, out):
    xres, gates, stats = shared["x"], shared["gates"], shared["stats"]
    ident_f = shared["ident"]

    def sb(name, shape, dt=F32):
        return mem.enter_context(nc.sbuf_tensor("d_" + name, shape, dt))

    def ps(name, cols, dt=F32):
        return mem.enter_context(nc.psum_tensor("d_" + name, [P, cols], dt))

    wq = shared["bit_w"]
    wmean = shared["bit_mean"]
    ident = sb("ident", [P, P], BF16)
    eps = sb("eps", [P, 1])
    half_neg = sb("half_neg", [P, B])
    magic = sb("magic", [P, 1])
    mv = sb("mv", [P, B, 2])
    rstd = sb("rstd", [P, B])
    rms = sb("rms", [P, B])
    xn = sb("xn", [P, B, D])
    amax = sb("amax", [P, B])
    qs = sb("qs", [P, B])
    unit = sb("unit", [P, B])
    gate_a = sb("gate_a", [P, B])
    up_a = sb("up_a", [P, B])
    down_a = sb("down_a", [P, B])
    xq = sb("xq", [P, B, D], BF16)
    xq_t = [sb(f"xq_t{i}", [P, 2, P], BF16) for i in range(2)]
    sg = [sb(f"sg{i}", [P, FF]) for i in range(2)]
    h = [sb(f"h{i}", [P, FF]) for i in range(2)]
    hs = sb("hs", [P, FF])
    sq = sb("sq", [P, FF])
    ssq = sb("ssq", [P, 2])
    hms = sb("hms", [P, 2])
    hr = sb("hr", [P, 2])
    hmax = sb("hmax", [P, B])
    hunit = sb("hunit", [P, B])
    hqs = sb("hqs", [P, B])
    hq = [sb(f"hq{i}", [P, FF], BF16) for i in range(2)]
    hq_t = [sb(f"hq_t{i}", [P, FF], BF16) for i in range(2)]

    g_ps = ps("g", FF)
    u_ps = ps("u", FF)
    h_tr = ps("h_tr", FF, BF16)
    x_tr = ps("x_tr", 2 * P, BF16)
    y_ps = ps("y", 512)

    names = """set_done aggr sqrt_done x_chain rms_done xq_done xq_steps rq_done w_chain xt_ready xt_read
        g_ready u_ready silu_done h_done sq_done max_done ms_done pow_done h_chain hs_done hq_done
        ht_ready ht_read y_ready x_done stored""".split()
    s = {n: shared["semaphores"].enter_context(nc.semaphore("d_" + n)) for n in names}

    with nc.Block() as block:

        @block.sync
        def _(sp):
            def store(b):
                wait(sp, s["x_done"], b.number + 1)
                sp.dma_start(out[b.number], xres[:, b.number, :]).then_inc(s["stored"], 16)
            for n in range(2):
                store(fixed(n))
            paired_loop(sp, 2, B, store)
            sp.wait_ge(s["stored"], 16 * B)

        @block.tensor
        def _(pe):
            def transpose_x(b):
                wait(pe, s["xq_done"], b.number + 1)
                wait(pe, s["xt_read"], b.number)
                for kc in range(2):
                    last = nc.tensor.transpose(x_tr[:, kc * P:(kc + 1) * P], xq[:, b.number, kc * P:(kc + 1) * P], ident[:])
                last.then_inc(s["xt_ready"], 1)

            def gate_up(b):
                wait(pe, s["xt_read"], b.number + 1)
                for i, (bank, free, ready) in enumerate(((g_ps, "silu_done", "g_ready"), (u_ps, "h_done", "u_ready"))):
                    wait(pe, s[free], b.number)
                    for half in range(2):
                        for kc in range(2):
                            last = nc.tensor.matmul(bank[:, half * 512:(half + 1) * 512], xq_t[b.parity][:, kc, :],
                                                    wq[i][:, kc * FF + half * 512:kc * FF + (half + 1) * 512],
                                                    start=kc == 0, stop=kc == 1)
                    last.then_inc(s[ready], 1)

            def transpose_h(b):
                wait(pe, s["hq_done"], b.number + 1)
                wait(pe, s["ht_read"], b.number)
                for c in range(HCH):
                    last = nc.tensor.transpose(h_tr[:, c * P:(c + 1) * P], hq[b.parity][:, c * P:(c + 1) * P], ident[:])
                last.then_inc(s["ht_ready"], 1)

            def down(b):
                wait(pe, s["ht_read"], b.number + 1)
                wait(pe, s["x_done"], b.number)
                for c in range(HCH):
                    last = nc.tensor.matmul(y_ps[:, 0:D], hq_t[b.parity][:, c * P:(c + 1) * P], wq[2][:, c * D:(c + 1) * D],
                                            start=c == 0, stop=c == HCH - 1)
                last.then_inc(s["y_ready"], 1)

            def step(b, one=True, two=True, behind=2):
                if one:
                    gate_up(b.plus(1))
                if two:
                    transpose_x(b.plus(2))
                if behind > 1:
                    down(b.plus(-2))
                if behind > 0:
                    transpose_h(b.plus(-1))

            pe.wait_ge(s["set_done"], 4)
            transpose_x(fixed(0))
            gate_up(fixed(0))
            transpose_x(fixed(1))
            for n in range(2):
                step(fixed(n), behind=n)
            paired_loop(pe, 2, B - 2, step)
            step(fixed(B - 2), two=False)
            step(fixed(B - 1), one=False, two=False)
            down(fixed(B - 2))
            transpose_h(fixed(B - 1))
            down(fixed(B - 1))

        @block.vector
        def _(dve):
            col = lambda t, b: t[:, bass.ds(b.number, 1)]

            nc.vector.memset(eps[:], LN_EPS).then_inc(s["set_done"], 1)
            nc.vector.memset(half_neg[:], -0.5).then_inc(s["set_done"], 1)
            nc.vector.memset(magic[:, 0:1], ROUND).then_inc(s["set_done"], 1)
            nc.vector.tensor_copy(ident[:], ident_f[:]).then_inc(s["set_done"], 1)
            for b in range(B):
                last = nc.vector.bn_aggr(mv[:, b, :], stats[:, b, :])
            last.then_inc(s["aggr"], 1)
            dve.wait_ge(s["sqrt_done"], 1)
            nc.vector.reciprocal(rstd[:], rstd[:]).then_inc(s["x_chain"], 1)
            dve.wait_ge(s["x_chain"], 1)
            for b in range(B):
                last = nc.vector.tensor_scalar(xn[:, b, :], xres[:, b, :], mv[:, b, 0:1], rstd[:, b:b + 1],
                                               ALU.subtract, ALU.mult)
            nc.vector.tensor_tensor(rms[:], rstd[:], rstd[:], ALU.mult).then_inc(s["x_chain"], 1)
            dve.wait_ge(s["x_chain"], 2)
            nc.vector.tensor_tensor(rms[:], rms[:], mv[:, :, 1], ALU.mult).then_inc(s["x_chain"], 1)
            dve.wait_ge(s["x_chain"], 3)
            nc.vector.tensor_scalar(rms[:], rms[:], RMS_EPS, None, ALU.add).then_inc(s["x_chain"], 1)
            nc.vector.tensor_reduce(amax[:], xn[:], AX.X, ALU.max, apply_absolute_value=True).then_inc(s["x_chain"], 1)
            dve.wait_ge(s["rms_done"], 1)
            dve.wait_ge(s["x_chain"], 5)
            nc.vector.tensor_tensor(amax[:], amax[:], rms[:], ALU.mult).then_inc(s["x_chain"], 1)
            dve.wait_ge(s["x_chain"], 6)
            nc.vector.tensor_scalar(unit[:], amax[:], Q_EPS, 1.0 / 127, ALU.max, ALU.mult).then_inc(s["x_chain"], 1)
            dve.wait_ge(s["x_chain"], 7)
            nc.vector.reciprocal(qs[:], unit[:]).then_inc(s["x_chain"], 1)
            dve.wait_ge(s["x_chain"], 8)
            nc.vector.tensor_tensor(amax[:], rms[:], qs[:], ALU.mult).then_inc(s["rq_done"], 1)
            nc.vector.tensor_scalar(gate_a[:], unit[:], wmean[:, 0:1], None, ALU.mult).then_inc(s["w_chain"], 1)
            nc.vector.tensor_scalar(up_a[:], unit[:], wmean[:, 1:2], None, ALU.mult).then_inc(s["w_chain"], 1)
            dve.wait_ge(s["w_chain"], 2)

            def product(b):
                wait(dve, s["silu_done"], b.number + 1)
                wait(dve, s["u_ready"], b.number + 1)
                wait(dve, s["sq_done"], b.number - 1)
                nc.vector.scalar_tensor_tensor(h[b.parity][:], u_ps[:], col(up_a, b), sg[b.parity][:],
                                               ALU.mult, ALU.mult).then_inc(s["h_done"], 1)

            def largest(b):
                wait(dve, s["h_done"], b.number + 1)
                nc.vector.tensor_reduce(col(hmax, b), h[b.parity][:], AX.X, ALU.max,
                                        apply_absolute_value=True).then_inc(s["max_done"], 1)

            def scales(b):
                n = b.number
                wait(dve, s["pow_done"], n + 1)
                wait(dve, s["max_done"], n + 1)
                nc.vector.tensor_scalar(col(hmax, b), col(hmax, b), hr[:, b.parity:b.parity + 1], Q_EPS, ALU.mult, ALU.max).then_inc(s["h_chain"], 1)
                wait(dve, s["h_chain"], 4 * n + 1)
                nc.vector.tensor_scalar(col(hunit, b), col(hmax, b), 1.0 / 127, None, ALU.mult).then_inc(s["h_chain"], 1)
                wait(dve, s["h_chain"], 4 * n + 2)
                nc.vector.reciprocal(col(hqs, b), col(hunit, b)).then_inc(s["h_chain"], 1)
                nc.vector.tensor_scalar(col(down_a, b), col(hunit, b), wmean[:, 2:3], gates[:, 3:4],
                                        ALU.mult, ALU.mult).then_inc(s["h_chain"], 1)

            def quantise(b):
                wait(dve, s["h_chain"], 4 * b.number + 4)
                wait(dve, s["hq_done"], b.number)
                nc.vector.tensor_scalar(hs[:], h[b.parity][:], hr[:, b.parity:b.parity + 1], col(hqs, b),
                                        ALU.mult, ALU.mult).then_inc(s["hs_done"], 1)
                wait(dve, s["hs_done"], b.number + 1)
                wait(dve, s["ht_ready"], b.number - 1)
                nc.vector.tensor_scalar(hq[b.parity][:], hs[:], ROUND, ROUND, ALU.add, ALU.subtract).then_inc(s["hq_done"], 1)

            def add_y(b):
                wait(dve, s["y_ready"], b.number + 1)
                nc.vector.scalar_tensor_tensor(xres[:, b.number, :], y_ps[:, 0:D], col(down_a, b), xres[:, b.number, :],
                                               ALU.mult, ALU.add).then_inc(s["x_done"], 1)

            def step(b, one=True, behind=2):
                if one:
                    product(b.plus(1))
                scales(b)
                quantise(b)
                if one:
                    largest(b.plus(1))
                if behind > 1:
                    add_y(b.plus(-2))

            product(fixed(0))
            largest(fixed(0))
            for n in range(2):
                step(fixed(n), behind=n)
            paired_loop(dve, 2, B - 2, step)
            step(fixed(B - 2))
            step(fixed(B - 1), one=False)
            for n in range(B - 2, B):
                add_y(fixed(n))

        @block.scalar
        def _(act):
            def evacuate_x(b):
                wait(act, s["xt_ready"], b.number + 1)
                wait(act, s["u_ready"], b.number - 1)
                nc.scalar.activation(xq_t[b.parity][:].rearrange("p a n -> p (a n)"), x_tr[:],
                                     ACT.Copy).then_inc(s["xt_read"], 1)

            def silu(b):
                wait(act, s["g_ready"], b.number + 1)
                wait(act, s["h_done"], b.number - 1)
                nc.scalar.activation(sg[b.parity][:], g_ps[:], ACT.Silu,
                                     scale=gate_a[:, bass.ds(b.number, 1)]).then_inc(s["silu_done"], 1)

            def square(b):
                wait(act, s["h_done"], b.number + 1)
                wait(act, s["sq_done"], b.number)
                nc.scalar.activation(sq[:], h[b.parity][:], ACT.Square,
                                     accum_out=ssq[:, b.parity:b.parity + 1]).then_inc(s["sq_done"], 1)

            def evacuate_h(b):
                wait(act, s["ht_ready"], b.number + 1)
                wait(act, s["y_ready"], b.number - 1)
                nc.scalar.activation(hq_t[b.parity][:], h_tr[:], ACT.Copy).then_inc(s["ht_read"], 1)

            act.wait_ge(s["aggr"], 1)
            act.wait_ge(s["set_done"], 1)
            nc.scalar.activation(rstd[:], mv[:, :, 1], ACT.Sqrt, bias=eps[:, 0:1]).then_inc(s["sqrt_done"], 1)
            evacuate_x(fixed(0))
            act.wait_ge(s["w_chain"], 1)
            silu(fixed(0))
            evacuate_x(fixed(1))
            square(fixed(0))

            def step(b, one=True, two=True, behind=2):
                if one:
                    silu(b.plus(1))
                if two:
                    evacuate_x(b.plus(2))
                if behind > 0:
                    evacuate_h(b.plus(-1))
                if one:
                    square(b.plus(1))
            for n in range(2):
                step(fixed(n), behind=n)
            paired_loop(act, 2, B - 2, step)
            step(fixed(B - 2), two=False)
            step(fixed(B - 1), one=False, two=False)
            evacuate_h(fixed(B - 1))

        @block.gpsimd
        def _(pool):
            wide = [P, D]

            def settle():
                pool.nop(nofuse=True)

            def round_x(b):
                row = xn[:, b.number, :]
                settle()
                nc.gpsimd.tensor_tensor(row, row, amax[:, bass.ds(b.number, 1)].broadcast_to(wide),
                                        ALU.mult).then_inc(s["xq_steps"], 1)
                wait(pool, s["xq_steps"], 2 * b.number + 1)
                settle()
                nc.gpsimd.tensor_tensor(row, row, magic[:].broadcast_to(wide), ALU.add).then_inc(s["xq_steps"], 1)
                wait(pool, s["xq_steps"], 2 * b.number + 2)
                settle()
                nc.gpsimd.tensor_tensor(xq[:, b.number, :], row, magic[:].broadcast_to(wide),
                                        ALU.subtract).then_inc(s["xq_done"], 1)

            def inverse_root(b):
                wait(pool, s["sq_done"], b.number + 1)
                settle()
                at = slice(b.parity, b.parity + 1)
                nc.gpsimd.tensor_scalar(hms[:, at], ssq[:, at], 1.0 / FF, RMS_EPS, ALU.mult, ALU.add).then_inc(s["ms_done"], 1)
                wait(pool, s["ms_done"], b.number + 1)
                settle()
                nc.gpsimd.tensor_tensor(hr[:, at], hms[:, at], half_neg[:, 0:1], ALU.pow).then_inc(s["pow_done"], 1)

            def step(b):
                inverse_root(b)
                round_x(b.plus(AHEAD))

            AHEAD = 4
            pool.wait_ge(s["set_done"], 4)
            pool.wait_ge(s["x_chain"], 4)
            nc.gpsimd.tensor_tensor(rms[:], rms[:], half_neg[:], ALU.pow).then_inc(s["rms_done"], 1)
            pool.wait_ge(s["rq_done"], 1)
            for n in range(AHEAD):
                round_x(fixed(n))
            paired_loop(pool, 0, B - AHEAD, step)
            for n in range(B - AHEAD, B):
                inverse_root(fixed(n))


def program(nc, x, ctx, mask, mask_col, gates, wq0, wk0, wv0, bq0, bk0, bv0, consts, ident,
            mix_w, router, select, rank, att_w, norm_w, bit_w, out):
    with ExitStack() as kept:
        def sb(name, shape):
            return kept.enter_context(nc.sbuf_tensor(name, shape, F32))

        shared = {"x": sb("x", [S, B, D]),
                  "stats": sb("stats", [S, B, 6]),
                  "ident": sb("ident", [P, P]), "gates": sb("gates", [P, 4]), "ident_dram": ident,
                  "gates_dram": gates, "mask_col_dram": mask_col, "bit_dram": bit_w, "semaphores": kept,
                  "stage": sb("stage", [P, STAGE_COLS]), "mix_dram": mix_w, "att_dram": att_w,
                  "mix_staged": [kept.enter_context(nc.semaphore(f"mix_staged{i}")) for i in range(M_STAGES)],
                  "att_staged": [kept.enter_context(nc.semaphore(f"att_staged{i}")) for i in range(C_STAGES)],
                  "bit_mean": sb("bit_mean", [P, 3]),
                  "bit_w": [kept.enter_context(nc.sbuf_tensor(f"bit_w{i}", [P, 2 * FF], BF16)) for i in range(3)]}
        with ExitStack() as mem:
            attention0(nc, mem, shared, x, ctx, mask, wq0, wk0, wv0, bq0, bk0, bv0, consts)
        with ExitStack() as mem:
            mixture(nc, mem, shared, mix_w, router, select, rank)
        with ExitStack() as mem:
            attention1(nc, mem, shared, att_w, norm_w, ctx)
        with ExitStack() as mem:
            bitlinear(nc, mem, shared, out)


def attention0_consts():
    c = np.zeros((P, CONST_COLS), np.float32)
    for head in range(GH):
        for quadrant in range(3):
            c[32 * quadrant + HD0 * head:32 * quadrant + HD0 * (head + 1), head] = 1
        c[96 + head:96 + HEADS0:GH, head] = 1
        c[112:116, head] = 1
    c[112:114, 4], c[112:116, 5] = -1, 1
    c[114, 6], c[115, 6] = NEG_HI, NEG_LO
    for group in range(GROUPS):
        c[96 + GH * group:96 + GH * (group + 1), 7 + group] = 1
        c[[112, 114], 7 + group], c[[113, 115], 7 + group] = -NEG_HI, -NEG_LO
    return c


def expert_rows(expert, shared_expert):
    rows = np.zeros((CHUNKS * P, D), np.float32)
    n = expert.shape[0] * expert.shape[1]
    rows[:n] = expert.reshape(n, D)
    rows[n:n + shared_expert.shape[0]] = shared_expert
    return rows


def pack_mixture(gate_up, down, sh_gate, sh_up, sh_down):
    inner = gate_up.shape[1] // 2
    parts = []
    for expert, one in ((gate_up[:, :inner], sh_gate), (gate_up[:, inner:], sh_up)):
        rows = expert_rows(expert, one)
        parts.append(rows.reshape(CHUNKS, P, 2, P).transpose(0, 3, 2, 1).reshape(CHUNKS, P, D))
    parts.append(expert_rows(down.transpose(0, 2, 1), sh_down.T).reshape(CHUNKS, P, D))
    return np.concatenate(parts, axis=2)


def select_matrix(inner, shared_inner):
    owner = np.concatenate([np.repeat(np.arange(EXPERTS), inner), np.full(shared_inner, EXPERTS)])
    select = np.zeros((SEL_ROWS, CHUNKS * P), np.float32)
    rows = np.arange(owner.size)
    select[owner, rows] = 1
    select[SEL_ROWS // 2 + owner, rows] = 1
    return select


def pack_attention1(wk, wv, wq, wo):
    halves = slice(0, P), slice(P, D)
    pieces = [np.concatenate([wk[h], wv[h]], axis=1) for h in halves]
    pieces += [wq[h][:, c * 1024:(c + 1) * 1024] for c in range(2) for h in halves]
    pieces += list(wo.reshape(KV, HPK, HD1, D).transpose(0, 2, 1, 3).reshape(KV, HD1, HPK * D))
    return np.stack(pieces)


def pack_bitlinear(*weights):
    return np.stack([w.T.reshape(w.shape[1] // P, P, w.shape[0]).transpose(1, 0, 2).reshape(P, -1) for w in weights])


def kernel(**inputs):
    import concourse.bacc as bacc
    from concourse.bass_utils import run_bass_kernel_spmd

    a = {name: np.asarray(value) for name, value in inputs.items()}
    mask = a["mask_Bx1x2048_fk1"]
    l0 = {n: a["L0_ffn_" + n] for n in ("gate_up_proj", "down_proj", "sh_gate_w", "sh_up_w", "sh_down_w")}
    router = np.concatenate([a["L0_ffn_router_weight"], a["L0_ffn_shared_gate_w"]])
    layout = {
        "x": a["x"], "ctx": a["ctx_2048"], "mask": mask,
        "mask_col": mask.reshape(B, 2, P).transpose(2, 0, 1),
        "gates": np.concatenate([a["g_xattn"], a["g_ffn"]]).reshape(1, 4),
        "wq0": a["L0_xattn_Wq"].T, "wk0": a["L0_xattn_Wk"].T, "wv0": a["L0_xattn_Wv"].T,
        "bq0": a["L0_xattn_bq"].reshape(P, 1), "bk0": a["L0_xattn_bk"].reshape(P, 1),
        "bv0": a["L0_xattn_bv"].reshape(1, P),
        "consts": attention0_consts(), "ident": np.eye(P, dtype=np.float32),
        "mix_w": pack_mixture(*l0.values()),
        "router": router.T.reshape(2, P, EXPERTS + 1).transpose(1, 0, 2),
        "select": select_matrix(l0["gate_up_proj"].shape[1] // 2, l0["sh_gate_w"].shape[0]),
        "rank": np.tile(np.arange(EXPERTS, 0, -1, dtype=np.float32), (P, TILES, 1)),
        "att_w": pack_attention1(*(a["L1_xattn_" + n] for n in ("Wk", "Wv", "Wq", "Wo"))),
        "norm_w": np.stack([a["L1_xattn_q_norm_w"], a["L1_xattn_k_norm_w"]], axis=1),
        "bit_w": pack_bitlinear(*(a["L1_ffn_" + n] for n in ("w_gate", "w_up", "w_down"))),
    }
    nc = bacc.Bacc("TRN2", target_bir_lowering=False, num_devices=1)
    arrays, args = {}, []
    for name, value in layout.items():
        value = np.ascontiguousarray(value)
        arrays[f"in_{name}_dram"] = value
        args.append(nc.dram_tensor(f"in_{name}_dram", value.shape, mybir.dt.from_np(value.dtype),
                                   kind="ExternalInput").ap())
    args.append(nc.dram_tensor("out_0_dram", (B, S, D), F32, kind="ExternalOutput").ap())
    program(nc, *args)
    r = run_bass_kernel_spmd(nc, [arrays], core_ids=[0])
    return r.results[0]["out_0_dram"]
```

```python
import itertools
from contextlib import ExitStack

import numpy as np

import concourse.bass as bass
from concourse import mybir

F32 = mybir.dt.float32
F32R = mybir.dt.float32r
BF16 = mybir.dt.bfloat16
ALU = mybir.AluOpType
ACT = mybir.ActivationFunctionType
AX = mybir.AxisListType

B, S, D = 16, 128, 256
P = 128
HEADS0, HD0 = 16, 8
GROUPS, GH = 4, 4
NEG_HI, NEG_LO = 999936.0, 64.0
LN_EPS = 1e-5
CONST_COLS = 11
N_WEIGHT_DMAS, N_CONST_DMAS = 6, 5
FIRST_PASS = 3, 2, 2, 3, 3, 3
K_PARTS, Q_PARTS = (0, 1, 0), (0, 0, 1)
STAGE_COLS = 3072
FF = 1024
Q_EPS = 1e-5
ROUND = 12582912.0


class Batch:

    def __init__(self, number, half, parity):
        self.number, self.half, self.parity = number, half, parity

    def is_number(self, n):
        return isinstance(self.number, int) and self.number == n

    def plus(self, n):
        parity = self.parity + n
        return Batch(self.number + n, self.half + parity // 2, parity % 2)


def fixed(n):
    return Batch(n, n // 2, n % 2)


def wait(engine, semaphore, value):
    if isinstance(value, int) and value <= 0:
        return
    engine.wait_ge(semaphore, value)


def paired_loop(engine, first, last, step):
    with engine.Fori(first // 2, last // 2) as half:
        for parity in range(2):
            step(Batch(half * 2 + parity, half, parity))


def attention0(nc, ctx_mem, shared, x, ctx, mask, wq, wk, wv, bq, bk, bv, consts):
    xres, ident, gates = shared["x"], shared["ident"], shared["gates"]

    def sb(name, shape, dt=F32):
        return ctx_mem.enter_context(nc.sbuf_tensor(name, shape, dt))

    def sem(name):
        return shared["semaphores"].enter_context(nc.semaphore(name))

    def ps(name, cols):
        return ctx_mem.enter_context(nc.psum_tensor(name, [P, cols], F32))

    w_sb = sb("a_w", [P, 3, P])
    bias = sb("a_bias", [P, 2])
    bv_row = sb("a_bv_row", [P, P])
    cst = sb("a_consts", [P, CONST_COLS])
    maskb = sb("a_maskb", [P, B, D])
    mask_col = sb("a_mask_col", [P, B, 2])
    stats = sb("a_stats", [P, B, 6])
    mv = sb("a_mv", [P, B, 2])
    rstd = sb("a_rstd", [P, B])
    eps = sb("a_eps", [P, 1])
    cbuf = [sb(f"a_ctx{i}", [P, D]) for i in range(2)]
    mrow = [sb(f"a_mrow{i}", [P, D]) for i in range(2)]
    xn = sb("a_xn", [P, D])
    full = [sb(f"a_full{i}", [P, D]) for i in range(2)]
    split = [sb(f"a_split{i}", [P, 2, D], F32R) for i in range(2)]
    qst = [sb(f"a_qst{i}", [P, GROUPS, D], F32R) for i in range(2)]
    krep = [sb(f"a_krep{i}", [P, GROUPS, D], F32R) for i in range(2)]
    qrep = [sb(f"a_qrep{i}", [P, GROUPS, D], F32R) for i in range(2)]
    kst = [sb(f"a_kst{i}", [P, GROUPS, GH, D], F32R) for i in range(2)]
    vt = sb("a_vt", [P, 2, P])
    mcb = sb("a_mcb", [P, 2])
    vst = [sb(f"a_vst{i}", [P, 2, HEADS0, 32]) for i in range(2)]
    sum_cols = sb("a_sum_cols", [P, GH, 32])
    mx = sb("a_mx", [P, 2, HEADS0])
    probs = [sb(f"a_probs{i}", [P, 2, 2, D]) for i in range(2)]
    sums = sb("a_sums", [P, D])
    outs = sb("a_outs", [P, D])
    rinv = sb("a_rinv", [P, D])
    tmp = sb("a_tmp", [P, D])

    bit_f = sb("a_bit_f", [P, 3, 2 * FF])
    bit_sum = sb("a_bit_sum", [P, 3])
    bit_abs = sb("a_bit_abs", [P, 2 * FF], BF16)
    ones = sb("a_ones", [P, P])
    bit_scale = sb("a_bit_scale", [P, 3])

    p1 = [ps(f"a_p1{i}", 512) for i in range(2)]
    p2 = [ps(f"a_p2{i}", 1024) for i in range(2)]
    pv = ps("a_pv", 512)
    misc = ps("a_misc", 512)

    def group_and_place(tile, k):
        return 2 * (tile // 4) + k, tile % 4

    names = """
        weights_in consts_in vst_zero ones_done stats_done rstd_in rstd_done w_scaled zeroed ctx_in0 ctx_in1
        mrow_in0 mrow_in1 first_k first_q xn_ready qk_psum full_done hi_done split_done dist_q0 dist_q1
        dist_k0 dist_k1 q3_krep q3_qrep q_stacked kst_dve kst_pool v_psum vt_ready vst_ready p1_ready
        mx_done mt_ready shift_done p2_ready exp_done pv_done evac_done fin_done rin_done bit_in bit_sums
        bit_mean bit_chain tmp_done""".split()
    s = {n: sem("a_" + n) for n in names}
    x_in = [sem(f"a_x_in{i}") for i in range(4)]

    C_SEL, C_QA, C_QB, C_KA, C_KB = 0, 4, 5, 6, 7

    with nc.Block() as block:

        @block.sync
        def _(sp):
            def load_x(i):
                sp.dma_start(xres[:, 4 * i:4 * i + 4, :],
                             x[4 * i:4 * i + 4].rearrange("b s d -> s b d")).then_inc(x_in[i], 16)

            def load(b):
                wait(sp, s["v_psum"], b.number - 1)
                wait(sp, s["qk_psum"], b.number - 1)
                sp.dma_start(cbuf[b.parity][:], ctx[b.number]).then_inc(s[f"ctx_in{b.parity}"], 16)
                wait(sp, s["q3_krep"], 4 * (b.number - 1))
                wait(sp, s["q3_qrep"], b.number - 1)
                sp.dma_start(mrow[b.parity][96:128, :].unsqueeze(1),
                             mask[b.number].partition_broadcast(32)).then_inc(s[f"mrow_in{b.parity}"], 16)

            def distribute_k(b):
                wait(sp, s["split_done"], 2 * b.number + 2)
                wait(sp, s["kst_dve"], 2 * (b.number - 1))
                wait(sp, s["kst_pool"], 2 * (b.number - 1))
                for quadrant, part in enumerate(K_PARTS):
                    for g in range(GROUPS):
                        sp.dma_start(krep[b.parity][32 * quadrant:32 * quadrant + 32, g, :].bitcast(F32),
                                     split[1][32 * g:32 * g + 32, part, :].bitcast(F32)).then_inc(s[f"dist_k{b.parity}"], 16)

            def distribute_q(b):
                wait(sp, s["q_stacked"], b.number - 1)
                for quadrant, part in enumerate(Q_PARTS):
                    for g in range(GROUPS):
                        sp.dma_start(qrep[b.parity][32 * quadrant:32 * quadrant + 32, g, :].bitcast(F32),
                                     split[0][32 * g:32 * g + 32, part, :].bitcast(F32)).then_inc(s[f"dist_q{b.parity}"], 16)

            load_x(0)
            for dst, src in ((w_sb[:, 0, :], wq), (w_sb[:, 1, :], wk), (bias[:, 0:1], bq), (bias[:, 1:2], bk),
                             (maskb[:], mask.rearrange("b o t -> (b o) t").partition_broadcast(P)),
                             (cst[:], consts)):
                sp.dma_start(dst, src).then_inc(s["weights_in"], 16)
            load(fixed(0))
            for dst, src in ((w_sb[:, 2, :], wv), (ident[:], shared["ident_dram"]),
                             (bv_row[:].unsqueeze(1), bv.partition_broadcast(P)),
                             (gates[:].unsqueeze(1), shared["gates_dram"].partition_broadcast(P)),
                             (mask_col[:], shared["mask_col_dram"])):
                sp.dma_start(dst, src).then_inc(s["consts_in"], 16)
            load(fixed(1))
            for i in range(1, 4):
                load_x(i)
            load(fixed(2))
            sp.dma_start(bit_f[:], shared["bit_dram"].rearrange("i p n -> p i n")).then_inc(s["bit_in"], 16)
            distribute_k(fixed(1))
            distribute_q(fixed(1))

            def step(b):
                distribute_k(b)
                load(b.plus(1))
                distribute_q(b)
            paired_loop(sp, 2, B - 2, step)
            step(fixed(B - 2))
            distribute_k(fixed(B - 1))
            distribute_q(fixed(B - 1))
            for j in range(M_STAGES):
                sp.dma_start(shared["stage"][:, W_COLS * j:W_COLS * (j + 1)], shared["mix_dram"][j]).then_inc(shared["mix_staged"][j], 16)

        @block.tensor
        def _(pe):
            def project_qk(b):
                wait(pe, s[f"ctx_in{b.parity}"], 16 * (b.half + 1))
                wait(pe, s["xn_ready"], b.number + 1)
                wait(pe, s["vt_ready"], b.number - 1)
                nc.tensor.matmul(misc[:, 0:D], w_sb[:, 0, :], xn[:], start=True, stop=True)
                nc.tensor.matmul(misc[:, D:2 * D], w_sb[:, 1, :], cbuf[b.parity][:],
                                 start=True, stop=True).then_inc(s["qk_psum"], 1)

            def project_v(b, ahead):
                wait(pe, s["full_done"], 2 * (b.number + ahead) + 2)
                for c in range(2):
                    last = nc.tensor.matmul(misc[:, c * P:(c + 1) * P], cbuf[b.parity][:, c * P:(c + 1) * P],
                                            w_sb[:, 2, :], start=True, stop=True)
                last.then_inc(s["v_psum"], 1)

            def pass1(b, half):
                tc, g, pair = half // (2 * GROUPS), half // 2 % GROUPS, half % 2
                if half == 0:
                    wait(pe, s["q_stacked"], b.number + 1)
                    wait(pe, s["kst_dve"], 2 * b.number + 2)
                    wait(pe, s["kst_pool"], 2 * b.number + 2)
                wait(pe, s["mx_done"], 16 * b.number + half - 1)
                nc.tensor.matmul(p1[pair][:], qst[b.parity][:, g, tc * P:(tc + 1) * P],
                                 kst[b.parity][:, g, 2 * pair:2 * pair + 2, :],
                                 start=True, stop=True).then_inc(s["p1_ready"], 1)

            def transpose_max(b):
                wait(pe, s["mx_done"], 16 * b.number + 16)
                for tc in range(2):
                    last = nc.tensor.transpose(p1[0][0:HEADS0, tc * P:(tc + 1) * P], mx[:, tc, :], ident[:])
                last.then_inc(s["mt_ready"], 1)

            def pass2(b, tile):
                if tile == 0:
                    wait(pe, s["shift_done"], b.number + 1)
                wait(pe, s["exp_done"], 8 * b.number + tile - 1)
                for k in range(2):
                    g, j = group_and_place(tile, k)
                    for c in range(2):
                        last = nc.tensor.matmul(p2[tile % 2][:, (2 * k + c) * D:(2 * k + c + 1) * D],
                                                kst[b.parity][:, g, j, c * P:(c + 1) * P],
                                                qst[b.parity][:, g, :], start=True, stop=True)
                last.then_inc(s["p2_ready"], 1)

            def weigh(b, tile, c):
                if c == 0:
                    if tile == 0:
                        wait(pe, s["vst_ready"], 2 * b.number + 2)
                        wait(pe, s["evac_done"], 3 * b.number)
                    wait(pe, s["exp_done"], 8 * b.number + tile + 1)
                flags = dict(start=tile % 4 == 0 and c == 0, stop=tile % 4 == 3 and c == 1)
                for k in range(2):
                    g, j = group_and_place(tile, k)
                    nc.tensor.matmul(pv[32 * g:32 * g + 32, 0:D], vst[b.parity][:, c, GH * g + j, :],
                                     probs[tile % 2][:, k, c, :], **flags)
                for k in range(2):
                    g, j = group_and_place(tile, k)
                    row = 32 * ((g + 2) % GROUPS)
                    last = nc.tensor.matmul(pv[row:row + 32, D:2 * D], sum_cols[:, j, :],
                                            probs[tile % 2][:, k, c, :], **flags)
                if c == 1:
                    last.then_inc(s["pv_done"], 1)

            wait(pe, s["w_scaled"], 2)
            wait(pe, s["weights_in"], 16 * N_WEIGHT_DMAS)
            project_qk(fixed(0))
            wait(pe, s["consts_in"], 16 * N_CONST_DMAS)
            project_v(fixed(0), 0)
            wait(pe, s["vt_ready"], 1)
            project_qk(fixed(1))
            wait(pe, s["zeroed"], 2)
            for half in range(16):
                pass1(fixed(0), half)
            transpose_max(fixed(0))
            pass2(fixed(0), 0)
            wait(pe, s["full_done"], 4)
            project_qk(fixed(2))
            wait(pe, s["ones_done"], 1)

            def step(b, one=True, two=True, three=True):
                done = 0
                for tile, halves in zip(range(1, 7), FIRST_PASS):
                    turn = [(halves + 2) // 3, (halves + 1) // 3, halves // 3] if one else [0] * 3
                    if one and tile == 1:
                        turn = [halves, 0, 0]
                    pass2(b, tile)
                    if three and tile == 6:
                        project_qk(b.plus(3))
                    if two and not three and tile == 5:
                        wait(pe, s["bit_sums"], 3)
                        wait(pe, s["vt_ready"], b.number + 2)
                        nc.tensor.matmul(misc[:, 0:3], ones[:], bit_sum[:], start=True, stop=True).then_inc(s["bit_mean"], 1)
                    if one and tile == 2:
                        project_v(b.plus(1), int(two))
                    for part in range(3):
                        for _ in range(turn[part]):
                            pass1(b.plus(1), done)
                            done += 1
                        if part < 2:
                            weigh(b, tile - 1, part)
                pass2(b, 7)
                for k in range(2):
                    weigh(b, 6, k)
                    if one and k == 0:
                        transpose_max(b.plus(1))
                if one:
                    pass2(b.plus(1), 0)
                for k in range(2):
                    weigh(b, 7, k)
            for n in range(2):
                step(fixed(n))
            paired_loop(pe, 2, B - 4, step)
            for n in range(B - 4, B):
                step(fixed(n), n + 1 < B, n + 2 < B, n + 3 < B)

        @block.vector
        def _(dve):
            def row_statistics(group):
                n, cols = group, slice(4 * group, 4 * group + 4)
                dve.wait_ge(x_in[group], 16)
                for b in range(4 * group, 4 * group + 4):
                    last = nc.vector.bn_stats(stats[:, b, :], xres[:, b, :])
                last.then_inc(s["stats_done"], 1)
                dve.wait_ge(s["stats_done"], 2 * n + 1)
                for b in range(4 * group, 4 * group + 4):
                    last = nc.vector.bn_aggr(mv[:, b, :], stats[:, b, :])
                last.then_inc(s["stats_done"], 1)
                dve.wait_ge(s["rstd_in"], n + 1)
                nc.vector.reciprocal(rstd[:, cols], rstd[:, cols]).then_inc(s["rstd_done"], 1)
                dve.wait_ge(s["rstd_done"], n + 1)

            nc.vector.memset(eps[:], LN_EPS).then_inc(s["zeroed"], 1)
            nc.vector.memset(ones[:], 1.0)
            nc.vector.memset(mx[:], 0.0).then_inc(s["zeroed"], 1)
            row_statistics(0)
            dve.wait_ge(s["weights_in"], 16 * N_WEIGHT_DMAS)
            nc.vector.tensor_scalar(w_sb[:, 0, :], w_sb[:, 0, :], HD0 ** -0.5, None, ALU.mult).then_inc(s["w_scaled"], 1)
            nc.vector.tensor_scalar(bias[:, 0:1], bias[:, 0:1], HD0 ** -0.5, None, ALU.mult).then_inc(s["w_scaled"], 1)

            def normalise(b):
                wait(dve, s["qk_psum"], b.number)
                nc.vector.tensor_scalar(xn[:], xres[:, b.number, :], mv[:, b.number, 0:1],
                                        rstd[:, bass.ds(b.number, 1)],
                                        ALU.subtract, ALU.mult).then_inc(s["xn_ready"], 1)

            def full_qk(b):
                wait(dve, s["qk_psum"], b.number + 1)
                wait(dve, s["split_done"], 2 * b.number)
                for i in range(2):
                    nc.vector.scalar_tensor_tensor(full[i][:], misc[:, i * D:(i + 1) * D], bias[:, i:i + 1],
                                                   maskb[:, b.number, :], ALU.add, ALU.mult).then_inc(s["full_done"], 1)

            def split_qk(b):
                if b.is_number(1):
                    dve.wait_ge(s["first_k"], 12)
                wait(dve, s[f"dist_k{1 - b.parity}"], 16 * 12 * b.half)
                wait(dve, s[f"dist_q{1 - b.parity}"], 16 * 12 * b.half)
                for i in range(2):
                    wait(dve, s["full_done"], 2 * b.number + i + 1)
                    nc.vector.tensor_copy(split[i][:, 0, :], full[i][:]).then_inc(s["hi_done"], 1)
                for i in range(2):
                    wait(dve, s["hi_done"], 2 * b.number + i + 1)
                    nc.vector.tensor_tensor(split[i][:, 1, :], full[i][:], split[i][:, 0, :].bitcast(F32),
                                            ALU.subtract).then_inc(s["split_done"], 1)

            def stack_k(b):
                if b.is_number(0):
                    dve.wait_ge(s["first_k"], 12)
                wait(dve, s[f"dist_k{b.parity}"], 16 * 12 * (b.half + b.parity))
                wait(dve, s["q3_krep"], 4 * (b.number + 1))
                wait(dve, s["p2_ready"], 8 * (b.number - 1))
                for j in range(2):
                    nc.vector.tensor_scalar(kst[b.parity][:, :, j, :], krep[b.parity][:].bitcast(F32), cst[:, C_SEL + j:C_SEL + j + 1],
                                            None, ALU.mult).then_inc(s["kst_dve"], 1)

            def value_bias(b):
                wait(dve, s["v_psum"], b.number + 1)
                wait(dve, s["vst_ready"], 2 * b.number)
                nc.vector.tensor_copy(mcb[:], mask_col[:, b.number, :])
                nc.vector.tensor_tensor(vt[:], misc[:, 0:D].rearrange("p (c n) -> p c n", c=2),
                                        bv_row[:].unsqueeze(1).broadcast_to([P, 2, P]), ALU.add).then_inc(s["vt_ready"], 1)

            def reduce_max(b, half):
                tc, g, pair = half // (2 * GROUPS), half // 2 % GROUPS, half % 2
                if half == 0:
                    wait(dve, s["mt_ready"], b.number)
                wait(dve, s["p1_ready"], 16 * b.number + half + 1)
                head = GH * g + 2 * pair
                nc.vector.tensor_reduce(mx[:, tc, head:head + 2], p1[pair][:].rearrange("p (h s) -> p h s", h=2),
                                        AX.X, ALU.max).then_inc(s["mx_done"], 1)

            def inverse(b):
                wait(dve, s["evac_done"], 3 * b.number + 3)
                nc.vector.reciprocal(rinv[:], sums[:]).then_inc(s["rin_done"], 1)

            def bit_scales():
                dve.wait_ge(s["bit_mean"], 1)
                nc.vector.tensor_scalar(shared["bit_mean"][:], misc[:, 0:3], 1.0 / (D * FF), Q_EPS,
                                        ALU.mult, ALU.max).then_inc(s["bit_chain"], 1)
                dve.wait_ge(s["bit_chain"], 1)
                nc.vector.reciprocal(bit_scale[:], shared["bit_mean"][:]).then_inc(s["bit_chain"], 1)
                dve.wait_ge(s["bit_chain"], 2)

            def round_bit_weights(i):
                w = bit_f[:, i, :]
                nc.vector.tensor_scalar(w, w, bit_scale[:, i:i + 1], 1.0, ALU.mult, ALU.min).then_inc(s["bit_chain"], 1)
                dve.wait_ge(s["bit_chain"], 2 * i + 3)
                nc.vector.tensor_scalar(w, w, -1.0, ROUND, ALU.max, ALU.add).then_inc(s["bit_chain"], 1)
                dve.wait_ge(s["bit_chain"], 2 * i + 4)
                nc.vector.tensor_scalar(shared["bit_w"][i][:], w, ROUND, None, ALU.subtract)

            def finish(b, between=lambda: None):
                nc.vector.scalar_tensor_tensor(tmp[:], outs[:], gates[:, 0:1], maskb[:, b.number, :],
                                               ALU.mult, ALU.mult).then_inc(s["tmp_done"], 1)
                between()
                dve.wait_ge(s["rin_done"], b.number + 1)
                dve.wait_ge(s["tmp_done"], 2 * b.number + 1)
                nc.vector.tensor_tensor(tmp[:], tmp[:], rinv[:], ALU.mult).then_inc(s["tmp_done"], 1)
                between()
                dve.wait_ge(s["tmp_done"], 2 * b.number + 2)
                nc.vector.tensor_tensor(xres[:, b.number, :], xres[:, b.number, :], tmp[:], ALU.add).then_inc(s["fin_done"], 1)
                between()
                dve.wait_ge(s["fin_done"], b.number + 1)
                nc.vector.bn_stats(shared["stats"][:, b.number, :], xres[:, b.number, :])

            normalise(fixed(0))
            dve.wait_ge(s["w_scaled"], 2)
            full_qk(fixed(0))
            split_qk(fixed(0))
            dve.wait_ge(s["split_done"], 1)
            for quadrant, part in enumerate(Q_PARTS):
                for g in range(GROUPS):
                    nc.vector.tensor_copy(qrep[0][32 * quadrant:32 * quadrant + 32, g, :],
                                          split[0][32 * g:32 * g + 32, part, :].bitcast(F32)).then_inc(s["first_q"], 1)
            normalise(fixed(1))
            dve.wait_ge(s["consts_in"], 16 * N_CONST_DMAS)
            value_bias(fixed(0))
            full_qk(fixed(1))
            stack_k(fixed(0))
            split_qk(fixed(1))
            normalise(fixed(2))
            for half in range(16):
                reduce_max(fixed(0), half)
            for group in range(1, 4):
                row_statistics(group)
            full_qk(fixed(2))
            split_qk(fixed(2))
            dve.wait_ge(s["rstd_in"], 5)

            def step(b, one=True, three=True, before=True):
                halves = iter(range(16 if one else 0))

                def reduce(count):
                    for half in itertools.islice(halves, count):
                        reduce_max(b.plus(1), half)
                if one:
                    stack_k(b.plus(1))
                reduce(3)
                if one:
                    value_bias(b.plus(1))
                reduce(2)
                if before:
                    inverse(b.plus(-1))
                reduce(3)
                if before:
                    finish(b.plus(-1), lambda: reduce(1))
                if three:
                    normalise(b.plus(3))
                reduce(16)
                if three:
                    full_qk(b.plus(3))
                    split_qk(b.plus(3))
            step(fixed(0), before=False)
            step(fixed(1))
            paired_loop(dve, 2, B - 4, step)
            for n in range(B - 4, B):
                step(fixed(n), n + 1 < B, n + 3 < B)
                if n == B - 3:
                    bit_scales()
                if n >= B - 3:
                    round_bit_weights(n - (B - 3))
            inverse(fixed(B - 1))
            finish(fixed(B - 1))

        @block.scalar
        def _(act):
            def deviation(group):
                act.wait_ge(s["stats_done"], 2 * group + 2)
                cols = slice(4 * group, 4 * group + 4)
                nc.scalar.activation(rstd[:, cols], mv[:, cols, 1], ACT.Sqrt, bias=eps[:, 0:1]).then_inc(s["rstd_in"], 1)

            def sum_bit_weights():
                act.wait_ge(s["bit_in"], 16)
                for i in range(3):
                    nc.scalar.activation(bit_abs[:], bit_f[:, i, :], ACT.Abs,
                                         accum_out=bit_sum[:, i:i + 1]).then_inc(s["bit_sums"], 1)
                    act.wait_ge(s["bit_sums"], i + 1)

            def stack_q(b):
                if b.is_number(0):
                    act.wait_ge(s["first_q"], 12)
                wait(act, s[f"dist_q{b.parity}"], 16 * 12 * (b.half + b.parity))
                wait(act, s["q3_qrep"], b.number + 1)
                wait(act, s["p2_ready"], 8 * (b.number - 1))
                nc.scalar.activation(qst[b.parity][:], qrep[b.parity][:].bitcast(F32), ACT.Copy).then_inc(s["q_stacked"], 1)

            def shift(b):
                wait(act, s["mt_ready"], b.number + 1)
                nc.scalar.activation(qst[b.parity][96:96 + HEADS0, :, :],
                                     p1[0][0:HEADS0, 0:D].unsqueeze(1).broadcast_to([HEADS0, GROUPS, D]),
                                     ACT.Copy, scale=-1.0).then_inc(s["shift_done"], 1)

            def exps(b, tile):
                wait(act, s["p2_ready"], 8 * b.number + tile + 1)
                wait(act, s["pv_done"], 8 * b.number + tile - 1)
                nc.scalar.activation(probs[tile % 2][:].rearrange("p k c t -> p (k c t)"), p2[tile % 2][:],
                                     ACT.Exp).then_inc(s["exp_done"], 1)

            def evacuate(b):
                wait(act, s["pv_done"], 8 * b.number + 8)
                wait(act, s["fin_done"], b.number)
                for dst, src in ((sums[0:64, :], pv[64:128, D:]), (sums[64:128, :], pv[0:64, D:]), (outs[:], pv[:, 0:D])):
                    nc.scalar.activation(dst, src, ACT.Copy).then_inc(s["evac_done"], 1)

            act.wait_ge(s["zeroed"], 2)
            deviation(0)
            act.wait_ge(s["split_done"], 2)
            for quadrant, part in enumerate(K_PARTS):
                for g in range(GROUPS):
                    nc.scalar.activation(krep[0][32 * quadrant:32 * quadrant + 32, g, :],
                                         split[1][32 * g:32 * g + 32, part, :].bitcast(F32), ACT.Copy).then_inc(s["first_k"], 1)
            stack_q(fixed(0))
            sum_bit_weights()
            shift(fixed(0))
            for group in range(1, 4):
                deviation(group)
            act.wait_ge(s["consts_in"], 16 * N_CONST_DMAS)
            nc.scalar.activation(gates[:], gates[:], ACT.Tanh).then_inc(s["rstd_in"], 1)

            def step(b, one=True, before=True):
                if one:
                    stack_q(b.plus(1))
                for tile in range(8):
                    exps(b, tile)
                    if before and tile == 0:
                        evacuate(b.plus(-1))
                if one:
                    shift(b.plus(1))
            step(fixed(0), before=False)
            step(fixed(1))
            paired_loop(act, 2, B - 2, step)
            step(fixed(B - 2))
            step(fixed(B - 1), one=False)
            evacuate(fixed(B - 1))

        @block.gpsimd
        def _(pool):
            def settle():
                pool.nop(nofuse=True)

            def mask_rows(b):
                wait(pool, s[f"mrow_in{b.parity}"], 16 * (b.half + 1))
                wait(pool, s["kst_dve"], 2 * (b.number - 1))
                wait(pool, s["kst_pool"], 2 * (b.number - 1))
                wait(pool, s["vst_ready"], 2 * b.number)
                settle()
                for g in range(GROUPS):
                    nc.gpsimd.tensor_scalar(krep[b.parity][96:128, g, :], mrow[b.parity][96:128, :],
                                            cst[96:128, C_KA:C_KA + 1], cst[96:128, C_KB + g:C_KB + g + 1],
                                            ALU.mult, ALU.add).then_inc(s["q3_krep"], 1)
                wait(pool, s["q_stacked"], b.number - 1)
                wait(pool, s["q3_krep"], 4 * (b.number + 1))
                settle()
                nc.gpsimd.tensor_scalar(qrep[b.parity][96:128, :, :],
                                        mrow[b.parity][96:128, :].unsqueeze(1).broadcast_to([32, GROUPS, D]),
                                        cst[96:128, C_QA:C_QA + 1], cst[96:128, C_QB:C_QB + 1],
                                        ALU.mult, ALU.add).then_inc(s["q3_qrep"], 1)

            def stack_k(b):
                if b.is_number(0):
                    pool.wait_ge(s["first_k"], 12)
                wait(pool, s[f"dist_k{b.parity}"], 16 * 12 * (b.half + b.parity))
                wait(pool, s["q3_qrep"], b.number + 1)
                wait(pool, s["p2_ready"], 8 * (b.number - 1))
                settle()
                for j in range(2, 4):
                    nc.gpsimd.tensor_scalar(kst[b.parity][:, :, j, :], krep[b.parity][:].bitcast(F32), cst[:, C_SEL + j:C_SEL + j + 1],
                                            1.0, ALU.mult, ALU.mult).then_inc(s["kst_pool"], 1)

            def place_v(b):
                wait(pool, s["vt_ready"], b.number + 1)
                wait(pool, s["pv_done"], 8 * (b.number - 1))
                wait(pool, s["kst_pool"], 2 * (b.number + 1))
                settle()
                for c in range(2):
                    block = vst[b.parity][:, c, :, :].rearrange("p h n -> p (h n)")
                    out = bass.AP(block.tensor, block.offset, [list(block.ap[0]), [GH * 32, GROUPS], [32 + HD0, GH], [1, HD0]])
                    nc.gpsimd.tensor_scalar(out, vt[:, c, :].rearrange("p (g j n) -> p g j n", g=GROUPS, j=GH),
                                            mcb[:, c:c + 1], 1.0, ALU.mult, ALU.mult).then_inc(s["vst_ready"], 1)

            pool.wait_ge(s["weights_in"], 16 * N_WEIGHT_DMAS)
            mask_rows(fixed(0))
            pool.wait_ge(s["q3_qrep"], 1)
            for view in (vst[0], vst[1], sum_cols):
                nc.gpsimd.memset(view[:], 0.0).then_inc(s["vst_zero"], 1)
            pool.wait_ge(s["vst_zero"], 3)
            for j in range(GH):
                last = nc.gpsimd.memset(sum_cols[:, j, HD0 * j:HD0 * (j + 1)], 1.0)
            last.then_inc(s["ones_done"], 1)
            pool.wait_ge(s["ones_done"], 1)
            stack_k(fixed(0))
            place_v(fixed(0))
            mask_rows(fixed(1))

            def step(b):
                stack_k(b.plus(1))
                place_v(b.plus(1))
                mask_rows(b.plus(2))
            for n in range(2):
                step(fixed(n))
            paired_loop(pool, 2, B - 2, step)
            stack_k(fixed(B - 1))
            place_v(fixed(B - 1))


TILES, GROUPS_OF_TILES = 4, 4
TOK = TILES * S
EXPERTS = 8
M_STAGES = 4
CHUNKS = 17
W_COLS = 6 * P
SEL_ROWS = 32


def mixture(nc, mem, shared, weights, router, select, rank):
    xres, ident, gates, stats = shared["x"], shared["ident"], shared["gates"], shared["stats"]

    def sb(name, shape, dt=F32):
        return mem.enter_context(nc.sbuf_tensor("m_" + name, shape, dt))

    def ps(name, cols):
        return mem.enter_context(nc.psum_tensor("m_" + name, [P, cols], F32))

    stage = [shared["stage"][:, W_COLS * i:W_COLS * (i + 1)] for i in range(M_STAGES)]
    staged = shared["mix_staged"]
    w_hi = sb("w_hi", [P, CHUNKS, W_COLS], F32R)
    w_lo = sb("w_lo", [P, CHUNKS, W_COLS], F32R)
    router_sb = sb("router", [P, 2, EXPERTS + 1])
    select_f = sb("select_f", [SEL_ROWS, CHUNKS * P])
    select_r = sb("select_r", [SEL_ROWS, CHUNKS * P], F32R)
    rank_sb = sb("rank", [P, TILES, EXPERTS])
    mv = sb("mv", [P, B, 2])
    rstd = sb("rstd", [P, B])
    eps = sb("eps", [P, 1])
    xn = sb("xn", [P, TILES, D])
    xt = sb("xt", [P, 2, TOK])
    x_hi = sb("x_hi", [P, 2, TOK], F32R)
    x_lo = sb("x_lo", [P, 2, TOK], F32R)
    logit_t = sb("logit_t", [EXPERTS + 1, TOK])
    e = sb("e", [P, TILES, EXPERTS + 1])
    r1 = sb("r1", [P, TILES])
    w1 = sb("w1", [P, TILES, EXPERTS])
    w2 = sb("w2", [P, TILES, EXPERTS])
    comb = sb("comb", [P, TILES, SEL_ROWS])
    comb_hi = sb("comb_hi", [P, TILES, EXPERTS + 1], F32R)
    comb_f = sb("comb_f", [P, TILES, EXPERTS + 1])
    comb_t = sb("comb_t", [SEL_ROWS, TOK], F32R)
    sg = [sb(f"sg{i}", [P, TOK]) for i in range(2)]
    hid = [sb(f"hid{i}", [P, TOK]) for i in range(2)]
    h_hi = [sb(f"h_hi{i}", [P, TOK], F32R) for i in range(3)]
    h_lo = [sb(f"h_lo{i}", [P, TOK], F32R) for i in range(3)]
    yt = sb("yt", [P, 2, TOK])

    g_ps = [ps(f"g{i}", TOK) for i in range(2)]
    u_ps = [ps(f"u{i}", TOK) for i in range(2)]
    c_ps = ps("c", TOK)
    acc = [ps(f"acc{i}", TOK) for i in range(2)]
    misc = ps("misc", TOK)

    names = """in0 eps_done aggr sqrt_done rstd_done sel_done hi_w lo_w
        xn_done tr_ready tr_read split_hi split_lo router_ready logit_read nat_ready 
        route exp_done comb_done combt_ready combt_done comb_chain g_ready u_ready c_ready silu_done
        mul_done hid_done h_hi h_lo down_done yt_done y_ready y_read""".split()
    s = {n: shared["semaphores"].enter_context(nc.semaphore("m_" + n)) for n in names}
    last_chunk = CHUNKS - 1

    with nc.Block() as block:

        @block.sync
        def _(sp):
            for dst, src in ((router_sb[:], router), (select_f[:], select), (rank_sb[:], rank)):
                sp.dma_start(dst, src).then_inc(s["in0"], 16)
            for j in range(M_STAGES, CHUNKS):
                wait(sp, s["hi_w"], j - M_STAGES + 1)
                wait(sp, s["lo_w"], j - M_STAGES + 1)
                sp.dma_start(stage[j % M_STAGES], weights[j]).then_inc(staged[j % M_STAGES], 16)
            sp.wait_ge(s["hi_w"], CHUNKS)
            sp.wait_ge(s["lo_w"], CHUNKS)
            for j in range(C_STAGES):
                sp.dma_start(shared["stage"][:, 1024 * j:1024 * (j + 1)], shared["att_dram"][j]).then_inc(shared["att_staged"][j], 16)

        @block.tensor
        def _(pe):
            def transpose_x(n, kc):
                wait(pe, s["xn_done"], TILES * (n + 1))
                if kc == 0:
                    wait(pe, s["combt_done"], n)
                    wait(pe, s["y_read"], 2 * (n - 1))
                else:
                    wait(pe, s["tr_read"], 2 * n + 1)
                for t in range(TILES):
                    last = nc.tensor.transpose(misc[:, t * S:(t + 1) * S], xn[:, t, kc * P:(kc + 1) * P], ident[:])
                last.then_inc(s["tr_ready"], 1)

            def route_logits(n):
                wait(pe, s["tr_read"], 2 * n + 2)
                for kc in range(2):
                    last = nc.tensor.matmul(misc[0:EXPERTS + 1, :], router_sb[:, kc, :], xt[:, kc, :],
                                            start=kc == 0, stop=kc == 1)
                last.then_inc(s["router_ready"], 1)

            def transpose_logits(n):
                wait(pe, s["logit_read"], n + 1)
                pe.nop(nofuse=True)
                for t in range(TILES):
                    last = nc.tensor.transpose(misc[:, 16 * t:16 * t + EXPERTS + 1], logit_t[:, t * S:(t + 1) * S],
                                               ident[0:EXPERTS + 1, 0:EXPERTS + 1])
                last.then_inc(s["nat_ready"], 1)

            def transpose_comb(n):
                wait(pe, s["comb_done"], 2 * (n + 1))
                for t in range(TILES):
                    last = nc.tensor.transpose(misc[0:SEL_ROWS, t * S:(t + 1) * S], comb[:, t, :], ident[:])
                last.then_inc(s["combt_ready"], 1)

            def three(out, j, col, hi, lo, first, final):
                cols = slice(col, col + P)
                nc.tensor.matmul(out, w_hi[:, j, cols], hi, start=first, stop=False)
                nc.tensor.matmul(out, w_lo[:, j, cols], hi, start=False, stop=False)
                return nc.tensor.matmul(out, w_hi[:, j, cols], lo, start=False, stop=final)

            def up(n, j, group0):
                m = CHUNKS * n + j
                if group0:
                    wait(pe, s["hi_w"], j + 1)
                    wait(pe, s["lo_w"], j + 1)
                if j == 0:
                    wait(pe, s["split_hi"], n + 1)
                    wait(pe, s["split_lo"], n + 1)
                wait(pe, s["silu_done"], m - 1 if j else m)
                for kc in range(2):
                    last = three(g_ps[j % 2][:], j, kc * P, x_hi[:, kc, :], x_lo[:, kc, :], kc == 0, kc == 1)
                last.then_inc(s["g_ready"], 1)
                wait(pe, s["mul_done"], m - 1 if j else m)
                for kc in range(2):
                    last = three(u_ps[j % 2][:], j, (2 + kc) * P, x_hi[:, kc, :], x_lo[:, kc, :], kc == 0, kc == 1)
                last.then_inc(s["u_ready"], 1)

            def spread(n, j):
                m = CHUNKS * n + j
                if j == 0:
                    wait(pe, s["combt_done"], n + 1)
                wait(pe, s["hid_done"], m)
                nc.tensor.matmul(c_ps[:], select_r[:, j * P:(j + 1) * P], comb_t[:],
                                 start=True, stop=True).then_inc(s["c_ready"], 1)

            def down(n, j):
                m = CHUNKS * n + j
                wait(pe, s["h_hi"], m + 1)
                wait(pe, s["h_lo"], m + 1)
                if j == 0:
                    wait(pe, s["yt_done"], 2 * n)
                for fh in range(2):
                    last = three(acc[fh][:], j, (4 + fh) * P, h_hi[j % 3][:], h_lo[j % 3][:], j == 0, j == last_chunk)
                last.then_inc(s["down_done"], 1)

            def transpose_y(n, half, after):
                wait(pe, s["yt_done"], 2 * n + 2)
                if half == 0:
                    wait(pe, s["combt_done"], after)
                else:
                    wait(pe, s["y_read"], 2 * n + 1)
                for t in range(2):
                    for fh in range(2):
                        last = nc.tensor.transpose(misc[:, t * D + fh * P:t * D + (fh + 1) * P],
                                                   yt[:, fh, (2 * half + t) * S:(2 * half + t + 1) * S], ident[:])
                last.then_inc(s["y_ready"], 1)

            def group(n, first, final):
                for j in range(CHUNKS):
                    if not first:
                        up(n, j, first)
                    elif j == 0:
                        up(n, 0, first)
                        up(n, 1, first)
                        transpose_comb(n)
                    elif j > 1:
                        up(n, j, first)
                    spread(n, j)
                    if j > 1:
                        down(n, j - 2)
                    elif j == 1 and not first:
                        down(n - 1, last_chunk)
                    if j == last_chunk:
                        down(n, last_chunk - 1)
                    if not first and j in (3, 4):
                        transpose_y(n - 1, j - 3, n + 1)
                    if not final:
                        if j in (6, 7):
                            transpose_x(n + 1, j - 6)
                        if j == 8:
                            route_logits(n + 1)
                        if j == 9:
                            transpose_logits(n + 1)
                        if j == 14:
                            transpose_comb(n + 1)

            transpose_x(0, 0)
            transpose_x(0, 1)
            wait(pe, s["in0"], 48)
            wait(pe, s["sel_done"], 2)
            route_logits(0)
            transpose_logits(0)
            group(0, True, False)
            with pe.Fori(1, GROUPS_OF_TILES - 1) as n:
                group(n, False, False)
            group(GROUPS_OF_TILES - 1, False, True)
            down(GROUPS_OF_TILES - 1, last_chunk)
            for half in range(2):
                transpose_y(GROUPS_OF_TILES - 1, half, GROUPS_OF_TILES)

        @block.vector
        def _(dve):
            def normalise(n):
                wait(dve, s["tr_ready"], 2 * n)
                for t in range(TILES):
                    b = TILES * n + t
                    nc.vector.tensor_scalar(xn[:, t, :], xres[:, b, :], mv[:, b, 0:1], rstd[:, bass.ds(b, 1)],
                                            ALU.subtract, ALU.mult).then_inc(s["xn_done"], 1)

            def split_x(n):
                wait(dve, s["u_ready"], CHUNKS * n)
                wait(dve, s["tr_read"], 2 * n + 2)
                nc.vector.tensor_copy(x_hi[:], xt[:]).then_inc(s["split_hi"], 1)
                dve.wait_ge(s["split_hi"], n + 1)
                nc.vector.tensor_tensor(x_lo[:], xt[:], x_hi[:].bitcast(F32), ALU.subtract).then_inc(s["split_lo"], 1)

            def chain(ins, k):
                ins.then_inc(s["route"], 1)
                dve.wait_ge(s["route"], k)

            ROUTE = 15

            def route_a(n):
                base = ROUTE * n
                wait(dve, s["nat_ready"], n + 1)
                logits = misc[:, 0:64].rearrange("p (t c) -> p t c", c=16)
                chain(nc.vector.tensor_reduce(r1[:], logits[:, :, 0:EXPERTS], AX.X, ALU.max), base + 1)
                chain(nc.vector.tensor_tensor(e[:, :, 0:EXPERTS], logits[:, :, 0:EXPERTS],
                                              r1[:].unsqueeze(2).broadcast_to([P, TILES, EXPERTS]), ALU.subtract), base + 2)
                chain(nc.vector.tensor_scalar(e[:, :, EXPERTS:], logits[:, :, EXPERTS:EXPERTS + 1], -1.0, None, ALU.mult), base + 3)

            def pick(base, src, w):
                wide = [P, TILES, EXPERTS]
                chain(nc.vector.tensor_reduce(r1[:], src, AX.X, ALU.max), base + 1)
                chain(nc.vector.tensor_tensor(w[:], src, r1[:].unsqueeze(2).broadcast_to(wide), ALU.is_equal), base + 2)
                chain(nc.vector.tensor_tensor(w[:], w[:], rank_sb[:], ALU.mult), base + 3)
                chain(nc.vector.tensor_reduce(r1[:], w[:], AX.X, ALU.max), base + 4)
                chain(nc.vector.tensor_tensor(w[:], w[:], r1[:].unsqueeze(2).broadcast_to(wide), ALU.is_equal), base + 5)

            def route_b(n):
                base = ROUTE * n
                wait(dve, s["exp_done"], n + 1)
                wait(dve, s["combt_ready"], n)
                probs = e[:, :, 0:EXPERTS]
                pick(base + 3, probs, w1)
                ins = nc.vector.scalar_tensor_tensor(w2[:], w1[:], -4.0, probs, ALU.mult, ALU.add)
                chain(ins, base + 9)
                wide = [P, TILES, EXPERTS]
                chain(nc.vector.tensor_reduce(r1[:], w2[:], AX.X, ALU.max), base + 10)
                chain(nc.vector.tensor_tensor(w2[:], w2[:], r1[:].unsqueeze(2).broadcast_to(wide), ALU.is_equal), base + 11)
                chain(nc.vector.tensor_tensor(w2[:], w2[:], rank_sb[:], ALU.mult), base + 12)
                chain(nc.vector.tensor_reduce(r1[:], w2[:], AX.X, ALU.max), base + 13)
                chain(nc.vector.tensor_tensor(w2[:], w2[:], r1[:].unsqueeze(2).broadcast_to(wide), ALU.is_equal), base + 14)
                chain(nc.vector.tensor_tensor(w1[:], w1[:], w2[:], ALU.add), base + 15)

            COMB = 7

            def chain2(ins, k):
                ins.then_inc(s["comb_chain"], 1)
                dve.wait_ge(s["comb_chain"], k)

            def route_c(n):
                base = COMB * n
                wide = [P, TILES, EXPERTS]
                probs = e[:, :, 0:EXPERTS]
                chain2(nc.vector.tensor_tensor(w1[:], w1[:], probs, ALU.mult), base + 1)
                chain2(nc.vector.tensor_reduce(r1[:], w1[:], AX.X, ALU.add), base + 2)
                chain2(nc.vector.reciprocal(r1[:], r1[:]), base + 3)
                chain2(nc.vector.tensor_tensor(comb_f[:, :, 0:EXPERTS], w1[:],
                                               r1[:].unsqueeze(2).broadcast_to(wide), ALU.mult), base + 4)
                chain2(nc.vector.tensor_scalar(e[:, :, EXPERTS:], e[:, :, EXPERTS:], 1.0, None, ALU.add), base + 5)
                chain2(nc.vector.reciprocal(comb_f[:, :, EXPERTS:], e[:, :, EXPERTS:]), base + 6)
                chain2(nc.vector.tensor_copy(comb_hi[:], comb_f[:]), base + 7)
                nc.vector.tensor_copy(comb[:, :, 0:EXPERTS + 1], comb_hi[:].bitcast(F32)).then_inc(s["comb_done"], 1)
                nc.vector.tensor_tensor(comb[:, :, 16:17 + EXPERTS], comb_f[:], comb_hi[:].bitcast(F32),
                                        ALU.subtract).then_inc(s["comb_done"], 1)

            def split_weights(j):
                wait(dve, s["hi_w"], j + 1)
                nc.vector.tensor_tensor(w_lo[:, j, :], stage[j % M_STAGES], w_hi[:, j, :].bitcast(F32),
                                        ALU.subtract).then_inc(s["lo_w"], 1)

            def hidden(n, j):
                m = CHUNKS * n + j
                wait(dve, s["silu_done"], m + 1)
                wait(dve, s["u_ready"], m + 1)
                wait(dve, s["h_lo"], m - 1 if j else m)
                wait(dve, s["h_hi"], m - 1 if j else m)
                nc.vector.tensor_tensor(sg[j % 2][:], sg[j % 2][:], u_ps[j % 2][:], ALU.mult).then_inc(s["mul_done"], 1)
                wait(dve, s["mul_done"], m + 1)
                wait(dve, s["c_ready"], m + 1)
                nc.vector.tensor_tensor(hid[j % 2][:], sg[j % 2][:], c_ps[:], ALU.mult).then_inc(s["hid_done"], 1)

            def hidden_low(n, j):
                m = CHUNKS * n + j
                wait(dve, s["h_hi"], m + 1)
                nc.vector.tensor_tensor(h_lo[j % 3][:], hid[j % 2][:], h_hi[j % 3][:].bitcast(F32),
                                        ALU.subtract).then_inc(s["h_lo"], 1)

            def add_y(n, half):
                wait(dve, s["y_ready"], 2 * n + half + 1)
                tiles = xres[:, bass.ds(TILES * n + 2 * half, 2), :].rearrange("p t d -> p (t d)")
                nc.vector.scalar_tensor_tensor(tiles, misc[:], gates[:, 2:3], tiles, ALU.mult,
                                               ALU.add).then_inc(s["y_read"], 1)
                wait(dve, s["y_read"], 2 * n + half + 1)
                for t in range(2):
                    at = TILES * n + 2 * half + t
                    nc.vector.bn_stats(stats[:, at, :], xres[:, at, :])

            def group(n, first, final):
                for j in range(CHUNKS):
                    if first and j + 2 < CHUNKS:
                        split_weights(j + 2)
                    if j == 0 and not first:
                        hidden_low(n - 1, last_chunk)
                    hidden(n, j)
                    if j > 0:
                        hidden_low(n, j - 1)
                    if not first and j in (3, 4):
                        add_y(n - 1, j - 3)
                    if not final:
                        if j == 5:
                            normalise(n + 1)
                        if j == 10:
                            route_a(n + 1)
                        if j == 12:
                            route_b(n + 1)
                            route_c(n + 1)
                        if j == last_chunk:
                            split_x(n + 1)

            nc.vector.memset(eps[:], LN_EPS).then_inc(s["eps_done"], 1)
            nc.vector.memset(comb[:], 0.0).then_inc(s["sel_done"], 1)
            for b in range(B):
                last = nc.vector.bn_aggr(mv[:, b, :], stats[:, b, :])
            last.then_inc(s["aggr"], 1)
            dve.wait_ge(s["sqrt_done"], 1)
            nc.vector.reciprocal(rstd[:], rstd[:]).then_inc(s["rstd_done"], 1)
            dve.wait_ge(s["rstd_done"], 1)
            normalise(0)
            dve.wait_ge(s["in0"], 48)
            nc.vector.tensor_copy(select_r[:], select_f[:]).then_inc(s["sel_done"], 1)
            split_x(0)
            route_a(0)
            for j in range(2):
                split_weights(j)
            route_b(0)
            route_c(0)
            group(0, True, False)
            with dve.Fori(1, GROUPS_OF_TILES - 1) as n:
                group(n, False, False)
            group(GROUPS_OF_TILES - 1, False, True)
            hidden_low(GROUPS_OF_TILES - 1, last_chunk)
            for half in range(2):
                add_y(GROUPS_OF_TILES - 1, half)

        @block.scalar
        def _(act):
            def evacuate_x(n):
                for kc in range(2):
                    wait(act, s["tr_ready"], 2 * n + kc + 1)
                    if kc == 0:
                        wait(act, s["split_lo"], n)
                    nc.scalar.activation(xt[:, kc, :], misc[:], ACT.Copy).then_inc(s["tr_read"], 1)

            def evacuate_logits(n):
                wait(act, s["router_ready"], n + 1)
                nc.scalar.activation(logit_t[:], misc[0:EXPERTS + 1, :], ACT.Copy).then_inc(s["logit_read"], 1)

            def exp(n):
                wait(act, s["route"], 15 * n + 3)
                nc.scalar.activation(e[:], e[:], ACT.Exp).then_inc(s["exp_done"], 1)

            def evacuate_comb(n):
                wait(act, s["combt_ready"], n + 1)
                wait(act, s["c_ready"], CHUNKS * n)
                nc.scalar.activation(comb_t[:], misc[0:SEL_ROWS, :], ACT.Copy).then_inc(s["combt_done"], 1)

            def split_weights(j):
                wait(act, staged[j % M_STAGES], 16 * (j // M_STAGES + 1))
                nc.scalar.activation(w_hi[:, j, :], stage[j % M_STAGES], ACT.Copy).then_inc(s["hi_w"], 1)

            def silu(n, j):
                m = CHUNKS * n + j
                wait(act, s["g_ready"], m + 1)
                wait(act, s["hid_done"], m - 1 if j else m)
                nc.scalar.activation(sg[j % 2][:], g_ps[j % 2][:], ACT.Silu).then_inc(s["silu_done"], 1)

            def hidden_high(n, j):
                m = CHUNKS * n + j
                wait(act, s["hid_done"], m + 1)
                wait(act, s["down_done"], m - 1 if j < 2 else m - 2)
                nc.scalar.activation(h_hi[j % 3][:], hid[j % 2][:], ACT.Copy).then_inc(s["h_hi"], 1)

            def evacuate_y(n):
                wait(act, s["down_done"], CHUNKS * (n + 1))
                for fh in range(2):
                    nc.scalar.activation(yt[:, fh, :], acc[fh][:], ACT.Copy).then_inc(s["yt_done"], 1)

            def group(n, first, final):
                for j in range(CHUNKS):
                    silu(n, j)
                    if j > 0:
                        hidden_high(n, j - 1)
                    elif not first:
                        hidden_high(n - 1, last_chunk)
                    if first and j + 3 < CHUNKS:
                        split_weights(j + 3)
                    if not first and j == 2:
                        evacuate_y(n - 1)
                    if not final:
                        if j == 7:
                            evacuate_x(n + 1)
                        if j == 8:
                            evacuate_logits(n + 1)
                        if j == 11:
                            exp(n + 1)
                        if j == last_chunk:
                            evacuate_comb(n + 1)

            act.wait_ge(s["aggr"], 1)
            act.wait_ge(s["eps_done"], 1)
            nc.scalar.activation(rstd[:], mv[:, :, 1], ACT.Sqrt, bias=eps[:, 0:1]).then_inc(s["sqrt_done"], 1)
            evacuate_x(0)
            evacuate_logits(0)
            for j in range(2):
                split_weights(j)
            exp(0)
            evacuate_comb(0)
            split_weights(2)
            group(0, True, False)
            with act.Fori(1, GROUPS_OF_TILES - 1) as n:
                group(n, False, False)
            group(GROUPS_OF_TILES - 1, False, True)
            hidden_high(GROUPS_OF_TILES - 1, last_chunk)
            evacuate_y(GROUPS_OF_TILES - 1)


KV, HPK = 4, 4
HD1 = 128
RMS_EPS = 1e-6
C_STAGES = 3
PIECES = 10


def attention1(nc, mem, shared, weights, norm_w, ctx):
    xres, ident, gates, stats = shared["x"], shared["ident"], shared["gates"], shared["stats"]

    def sb(name, shape, dt=F32):
        return mem.enter_context(nc.sbuf_tensor("c_" + name, shape, dt))

    def ps(name):
        return mem.enter_context(nc.psum_tensor("c_" + name, [P, 512], F32))

    stage = [shared["stage"][:, 1024 * i:1024 * (i + 1)] for i in range(C_STAGES)]
    staged = shared["att_staged"]
    w_hi = sb("w_hi", [P, PIECES, 1024], F32R)
    w_lo = sb("w_lo", [P, PIECES, 1024], F32R)
    norm_sb = sb("norm", [P, 2])
    wqk = sb("wqk", [P, 1])
    mv = sb("mv", [P, B, 2])
    rstd = sb("rstd", [P, B])
    eps = sb("eps", [P, 1])
    half_neg = sb("half_neg", [P, KV])
    cbuf = [sb(f"ctx{i}", [P, D]) for i in range(2)]
    xn = sb("xn", [P, D])
    in_hi = sb("in_hi", [P, 4, P], F32R)
    in_lo = sb("in_lo", [P, 4, P], F32R)
    sq = [sb(f"sq{i}", [P, 512]) for i in range(2)]
    ssq = sb("ssq", [P, 5 * KV])
    ms = sb("ms", [P, 5 * KV])
    rms = sb("rms", [P, 5 * KV])
    kn = sb("kn", [P, 512])
    qn = [sb(f"qn{i}", [P, 512]) for i in range(2)]
    k_t = [sb(f"k_t{i}", [P, KV, P]) for i in range(2)]
    q_t = [sb(f"q_t{i}", [P, KV, 512]) for i in range(2)]
    v_sb = [sb(f"v{i}", [P, KV, HD1]) for i in range(2)]
    probs = [sb(f"probs{i}", [P, 512]) for i in range(4)]
    top = sb("top", [P, 4 * HPK])
    tot = sb("tot", [P, 4 * HPK])
    inv = sb("inv", [P, 4 * HPK])
    p_t = [sb(f"p_t{i}", [P, 512]) for i in range(2)]
    o_hi = [sb(f"o_hi{i}", [P, 512], F32R) for i in range(2)]
    o_lo = [sb(f"o_lo{i}", [P, 512], F32R) for i in range(2)]

    pj = [ps(f"pj{i}") for i in range(2)]
    tr = [ps(f"tr{i}") for i in range(2)]
    sc = [ps(f"sc{i}") for i in range(2)]
    pv = ps("pv")
    out = ps("out")

    names = """in0 hi_w lo_w eps_done aggr sqrt_done rstd_done ctx_in0 ctx_in1 xn_done
        x_tr x_hi x_lo pj_ready sq_done ssq_done ms_done rms_done mul_done v_read kt_tr kt_read qt_tr qt_read
        sc_ready max_done sub_done exp_done sum_done inv_done norm_done pt_tr pt_read pv_ready o_hi o_lo
        out_ready x_done""".split()
    s = {n: shared["semaphores"].enter_context(nc.semaphore("c_" + n)) for n in names}

    def heads(ap):
        return ap.rearrange("p (h n) -> p h n", h=4)

    def spread(ap):
        return ap.unsqueeze(2).broadcast_to([P, 4, 128])

    with nc.Block() as block:

        @block.sync
        def _(sp):
            def step(b):
                wait(sp, s["x_tr"], b.number - 1)
                sp.dma_start(cbuf[b.parity][:], ctx[b.number]).then_inc(s[f"ctx_in{b.parity}"], 16)
            sp.dma_start(norm_sb[:], norm_w).then_inc(s["in0"], 16)
            for n in range(2):
                step(fixed(n))
            for j in range(C_STAGES, PIECES):
                wait(sp, s["hi_w"], j - C_STAGES + 1)
                wait(sp, s["lo_w"], j - C_STAGES + 1)
                sp.dma_start(stage[j % C_STAGES], weights[j]).then_inc(staged[j % C_STAGES], 16)
            paired_loop(sp, 2, B, step)

        @block.tensor
        def _(pe):
            def transpose_in(b):
                wait(pe, s["xn_done"], b.number + 1)
                wait(pe, s[f"ctx_in{b.parity}"], 16 * (b.half + 1))
                wait(pe, s["kt_read"], b.number)
                wait(pe, s["pt_read"], 4 * (b.number - 1))
                for src, at in ((xn, 0), (cbuf[b.parity], 2)):
                    for kc in range(2):
                        last = nc.tensor.transpose(tr[0][:, (at + kc) * P:(at + kc + 1) * P],
                                                   src[:, kc * P:(kc + 1) * P], ident[:])
                last.then_inc(s["x_tr"], 1)

            def project(a, c, loading=False):
                n = a.number
                if c == 0:
                    wait(pe, s["x_hi"], n + 1)
                    wait(pe, s["x_lo"], n + 1)
                if loading:
                    wait(pe, s["hi_w"], 2 * (c // 2) + 2)
                    wait(pe, s["lo_w"], 2 * (c // 2) + 2)
                if c == 3:
                    wait(pe, s["v_read"], n + 1)
                else:
                    wait(pe, s["mul_done"], 5 * n + {0: -1, 1: 0, 2: 1, 4: 2, 5: 3}[c])
                for kc in range(2):
                    row = kc + (2 if c < 2 else 0)
                    if c < 2:
                        w = (kc, c * 512)
                    else:
                        w = (c // 2 * 2 + kc, (c % 2) * 512)
                    wh, wl = (t[:, w[0], w[1]:w[1] + 512] for t in (w_hi, w_lo))
                    nc.tensor.matmul(pj[c % 2][:], in_hi[:, row, :], wh, start=kc == 0, stop=False)
                    nc.tensor.matmul(pj[c % 2][:], in_hi[:, row, :], wl, start=False, stop=False)
                    last = nc.tensor.matmul(pj[c % 2][:], in_lo[:, row, :], wh, start=False, stop=kc == 1)
                last.then_inc(s["pj_ready"], 1)

            def transpose_k(a, b_runs):
                if b_runs:
                    wait(pe, s["pt_read"], 4 * (a.number - 1) + 2)
                wait(pe, s["mul_done"], 5 * a.number + 1)
                wait(pe, s["x_lo"], a.number + 1)
                wait(pe, s["x_hi"], a.number + 1)
                for i in range(KV):
                    last = nc.tensor.transpose(tr[0][:, i * P:(i + 1) * P], kn[:, i * P:(i + 1) * P], ident[:])
                last.then_inc(s["kt_tr"], 1)

            def transpose_q(a, i):
                wait(pe, s["mul_done"], 5 * a.number + 2 + i)
                if i == 0:
                    wait(pe, s["pt_read"], 4 * (a.number - 1) + 1)
                else:
                    wait(pe, s["qt_read"], 4 * a.number + i)
                for h in range(HPK):
                    last = nc.tensor.transpose(tr[1][:, h * P:(h + 1) * P], qn[i % 2][:, h * P:(h + 1) * P], ident[:])
                last.then_inc(s["qt_tr"], 1)

            def transpose_p(b, i, a_runs):
                wait(pe, s["norm_done"], 4 * b.number + i + 1)
                if i == 0:
                    wait(pe, s["qt_read"], 4 * (b.number + 1))
                elif i == 1:
                    if a_runs:
                        wait(pe, s["x_hi"], b.number + 2)
                        wait(pe, s["x_lo"], b.number + 2)
                    wait(pe, s["pt_read"], 4 * b.number)
                elif i == 2:
                    wait(pe, s["pt_read"], 4 * b.number + 2)
                    if a_runs:
                        wait(pe, s["kt_read"], b.number + 2)
                else:
                    wait(pe, s["pt_read"], 4 * b.number + i)
                for h in range(HPK):
                    last = nc.tensor.transpose(tr[0 if i else 1][:, h * P:(h + 1) * P],
                                               probs[i][:, h * P:(h + 1) * P], ident[:])
                last.then_inc(s["pt_tr"], 1)

            def score(b, i):
                if i == 0:
                    wait(pe, s["kt_read"], b.number + 1)
                wait(pe, s["qt_read"], 4 * b.number + i + 1)
                wait(pe, s["sub_done"], 4 * b.number + i - 1)
                for h in range(HPK):
                    last = nc.tensor.matmul(sc[i % 2][:, h * P:(h + 1) * P], q_t[b.parity][:, i, h * P:(h + 1) * P],
                                            k_t[b.parity][:, i, :], start=True, stop=True)
                last.then_inc(s["sc_ready"], 1)

            def weigh(b, i):
                if i == 0:
                    wait(pe, s["v_read"], b.number + 1)
                wait(pe, s["pt_read"], 4 * b.number + i + 1)
                wait(pe, s["o_hi"], 4 * b.number + i)
                wait(pe, s["o_lo"], 4 * b.number + i)
                nc.tensor.matmul(pv[:], v_sb[b.parity][:, i, :], p_t[i % 2][:], start=True, stop=True).then_inc(s["pv_ready"], 1)

            def project_out(b, i):
                wait(pe, s["o_hi"], 4 * b.number + i + 1)
                wait(pe, s["o_lo"], 4 * b.number + i + 1)
                if i == 0:
                    wait(pe, s["x_done"], b.number)
                for h in range(HPK):
                    wh, wl = (t[:, 6 + i, h * D:(h + 1) * D] for t in (w_hi, w_lo))
                    oh, ol = (t[i % 2][:, h * P:(h + 1) * P] for t in (o_hi, o_lo))
                    nc.tensor.matmul(out[:, 0:D], oh, wh, start=i == 0 and h == 0, stop=False)
                    nc.tensor.matmul(out[:, 0:D], oh, wl, start=False, stop=False)
                    last = nc.tensor.matmul(out[:, 0:D], ol, wh, start=False, stop=i == 3 and h == 3)
                last.then_inc(s["out_ready"], 1)

            def step(b, do_b=True, do_a=True, do_x=True, before=True, loading=False):
                a = b.plus(1)
                if do_b:
                    score(b, 0)
                if do_a:
                    project(a, 0, loading)
                if do_b and before:
                    project_out(b.plus(-1), 3)
                if do_a:
                    project(a, 1, loading)
                if do_b:
                    score(b, 1)
                if do_a:
                    project(a, 2, loading)
                if do_b:
                    transpose_p(b, 0, do_a)
                    score(b, 2)
                if do_a:
                    project(a, 3, loading)
                if do_b:
                    weigh(b, 0)
                    transpose_p(b, 1, do_a)
                if do_a:
                    transpose_q(a, 0)
                    project(a, 4, loading)
                    transpose_k(a, do_b)
                if do_b:
                    score(b, 3)
                    weigh(b, 1)
                    project_out(b, 0)
                    transpose_p(b, 2, do_a)
                if do_a:
                    transpose_q(a, 1)
                    project(a, 5, loading)
                if do_b:
                    weigh(b, 2)
                    project_out(b, 1)
                    transpose_p(b, 3, do_a)
                if do_a:
                    transpose_q(a, 2)
                if do_b:
                    project_out(b, 2)
                if do_x:
                    transpose_in(b.plus(2))
                if do_b:
                    weigh(b, 3)
                if do_a:
                    transpose_q(a, 3)

            step(fixed(-2), do_b=False, do_a=False)
            step(fixed(-1), do_b=False, loading=True)
            wait(pe, s["hi_w"], PIECES)
            wait(pe, s["lo_w"], PIECES)
            step(fixed(0), before=False)
            step(fixed(1))
            paired_loop(pe, 2, B - 2, step)
            step(fixed(B - 2), do_x=False)
            step(fixed(B - 1), do_a=False, do_x=False)
            project_out(fixed(B - 1), 3)

        @block.vector
        def _(dve):
            def split_weights(first, last):
                for j in range(first, last):
                    wait(dve, s["hi_w"], j + 1)
                    nc.vector.tensor_tensor(w_lo[:, j, :], stage[j % C_STAGES], w_hi[:, j, :].bitcast(F32),
                                            ALU.subtract).then_inc(s["lo_w"], 1)

            def normalise(b):
                wait(dve, s["x_tr"], b.number)
                nc.vector.tensor_scalar(xn[:], xres[:, b.number, :], mv[:, b.number, 0:1], rstd[:, bass.ds(b.number, 1)],
                                        ALU.subtract, ALU.mult).then_inc(s["xn_done"], 1)

            def split_in(b):
                wait(dve, s["x_hi"], b.number + 1)
                wait(dve, s["pj_ready"], 6 * b.number)
                nc.vector.tensor_tensor(in_lo[:].rearrange("p a n -> p (a n)"), tr[0][:],
                                        in_hi[:].bitcast(F32).rearrange("p a n -> p (a n)"), ALU.subtract).then_inc(s["x_lo"], 1)

            def sum_squares(a, k):
                wait(dve, s["sq_done"], 5 * a.number + k + 1)
                nc.vector.tensor_reduce(ssq[:, 4 * k:4 * k + 4], heads(sq[k % 2][:]),
                                        AX.X, ALU.add).then_inc(s["ssq_done"], 1)

            def scale(a, k):
                wait(dve, s["rms_done"], 5 * a.number + k + 1)
                if k == 0:
                    wait(dve, s["kt_tr"], a.number)
                    dst = kn
                else:
                    wait(dve, s["qt_tr"], 4 * a.number + k - 2)
                    dst = qn[(k - 1) % 2]
                bank = 0 if k == 0 else (k + 1) % 2
                nc.vector.tensor_tensor(heads(dst[:]), heads(pj[bank][:]), spread(rms[:, 4 * k:4 * k + 4]),
                                        ALU.mult).then_inc(s["mul_done"], 1)

            def evacuate_k(a):
                wait(dve, s["kt_tr"], a.number + 1)
                wait(dve, s["sc_ready"], 4 * (a.number - 1))
                nc.vector.tensor_scalar(k_t[a.parity][:].rearrange("p a n -> p (a n)"), tr[0][:], wqk[:, 0:1], None,
                                        ALU.mult).then_inc(s["kt_read"], 1)

            def shift(b, i):
                wait(dve, s["sc_ready"], 4 * b.number + i + 1)
                nc.vector.tensor_reduce(top[:, 4 * i:4 * i + 4], heads(sc[i % 2][:]), AX.X, ALU.max).then_inc(s["max_done"], 1)
                wait(dve, s["max_done"], 4 * b.number + i + 1)
                wait(dve, s["pt_tr"], 4 * (b.number - 1) + i + 1)
                nc.vector.tensor_tensor(heads(probs[i][:]), heads(sc[i % 2][:]), spread(top[:, 4 * i:4 * i + 4]),
                                        ALU.subtract).then_inc(s["sub_done"], 1)

            def total(b, i):
                wait(dve, s["exp_done"], 4 * b.number + i + 1)
                nc.vector.tensor_reduce(tot[:, 4 * i:4 * i + 4], heads(probs[i][:]), AX.X, ALU.add).then_inc(s["sum_done"], 1)
                wait(dve, s["sum_done"], 4 * b.number + i + 1)
                nc.vector.reciprocal(inv[:, 4 * i:4 * i + 4], tot[:, 4 * i:4 * i + 4]).then_inc(s["inv_done"], 1)

            def split_out(b, i):
                wait(dve, s["o_hi"], 4 * b.number + i + 1)
                wait(dve, s["out_ready"], 4 * b.number + i - 1)
                nc.vector.tensor_tensor(o_lo[i % 2][:], pv[:], o_hi[i % 2][:].bitcast(F32), ALU.subtract).then_inc(s["o_lo"], 1)

            def add_out(b):
                wait(dve, s["out_ready"], 4 * b.number + 4)
                nc.vector.scalar_tensor_tensor(xres[:, b.number, :], out[:, 0:D], gates[:, 1:2], xres[:, b.number, :],
                                               ALU.mult, ALU.add).then_inc(s["x_done"], 1)

            def row_statistics(b):
                wait(dve, s["x_done"], b.number + 1)
                nc.vector.bn_stats(stats[:, b.number, :], xres[:, b.number, :])
                for extreme, op in ((shared["row_max"], ALU.max), (shared["row_min"], ALU.min)):
                    nc.vector.tensor_reduce(extreme[:, bass.ds(b.number, 1)], xres[:, b.number, :], AX.X, op)

            def step(b, do_b=True, do_a=True, do_x=True, before=True, loading=False):
                a = b.plus(1)
                if do_b:
                    shift(b, 0)
                if do_a:
                    sum_squares(a, 0)
                if do_b:
                    total(b, 0)
                if do_a:
                    scale(a, 0)
                if loading:
                    split_weights(3, 5)
                if do_b:
                    shift(b, 1)
                if do_a:
                    sum_squares(a, 1)
                if do_b:
                    total(b, 1)
                if do_a:
                    scale(a, 1)
                if loading:
                    split_weights(5, 6)
                if do_b:
                    shift(b, 2)
                if do_a:
                    sum_squares(a, 2)
                if do_b:
                    total(b, 2)
                    split_out(b, 0)
                    if before:
                        add_out(b.plus(-1))
                if do_a:
                    evacuate_k(a)
                    scale(a, 2)
                    sum_squares(a, 3)
                if loading:
                    split_weights(6, 8)
                if do_b:
                    shift(b, 3)
                    split_out(b, 1)
                    total(b, 3)
                if do_a:
                    scale(a, 3)
                    sum_squares(a, 4)
                if do_b:
                    split_out(b, 2)
                    if before:
                        row_statistics(b.plus(-1))
                if do_x:
                    normalise(b.plus(2))
                if do_a:
                    scale(a, 4)
                if do_x:
                    split_in(b.plus(2))
                if do_b:
                    split_out(b, 3)

            nc.vector.memset(eps[:], LN_EPS).then_inc(s["eps_done"], 1)
            nc.vector.memset(half_neg[:], -0.5).then_inc(s["eps_done"], 1)
            for b in range(B):
                last = nc.vector.bn_aggr(mv[:, b, :], stats[:, b, :])
            last.then_inc(s["aggr"], 1)
            dve.wait_ge(s["in0"], 16)
            nc.vector.scalar_tensor_tensor(wqk[:], norm_sb[:, 0:1], HD1 ** -0.5, norm_sb[:, 1:2],
                                           ALU.mult, ALU.mult).then_inc(s["rstd_done"], 1)
            dve.wait_ge(s["sqrt_done"], 1)
            nc.vector.reciprocal(rstd[:], rstd[:]).then_inc(s["rstd_done"], 1)
            dve.wait_ge(s["rstd_done"], 2)
            step(fixed(-2), do_b=False, do_a=False)
            split_weights(0, 3)
            step(fixed(-1), do_b=False, loading=True)
            split_weights(8, PIECES)
            step(fixed(0), before=False)
            step(fixed(1))
            paired_loop(dve, 2, B - 2, step)
            step(fixed(B - 2), do_x=False)
            step(fixed(B - 1), do_a=False, do_x=False)
            add_out(fixed(B - 1))
            row_statistics(fixed(B - 1))

        @block.scalar
        def _(act):
            def copy(dst, src):
                return nc.scalar.activation(dst, src, ACT.Copy)

            def split_weights(first, last):
                for j in range(first, last):
                    wait(act, staged[j % C_STAGES], 16 * (j // C_STAGES + 1))
                    copy(w_hi[:, j, :], stage[j % C_STAGES]).then_inc(s["hi_w"], 1)

            def square(a, k):
                c = 0 if k == 0 else k + 1
                wait(act, s["pj_ready"], 6 * a.number + c + 1)
                wait(act, s["ssq_done"], 5 * a.number + k - (1 if k else 0))
                nc.scalar.activation(sq[k % 2][:], pj[c % 2][:], ACT.Square).then_inc(s["sq_done"], 1)

            def values(a):
                wait(act, s["pj_ready"], 6 * a.number + 2)
                wait(act, s["pv_ready"], 4 * (a.number - 1))
                copy(v_sb[a.parity][:].rearrange("p a n -> p (a n)"), pj[1][:]).then_inc(s["v_read"], 1)

            def exp(b, i):
                wait(act, s["sub_done"], 4 * b.number + i + 1)
                nc.scalar.activation(probs[i][:], probs[i][:], ACT.Exp).then_inc(s["exp_done"], 1)

            def evacuate_p(b, i):
                wait(act, s["pt_tr"], 4 * b.number + i + 1)
                wait(act, s["pv_ready"], 4 * b.number + i - 1)
                copy(p_t[i % 2][:], tr[0 if i else 1][:]).then_inc(s["pt_read"], 1)

            def evacuate_q(a, i):
                wait(act, s["qt_tr"], 4 * a.number + i + 1)
                wait(act, s["sc_ready"], 4 * (a.number - 1))
                copy(q_t[a.parity][:, i, :], tr[1][:]).then_inc(s["qt_read"], 1)

            def split_out(b, i):
                wait(act, s["pv_ready"], 4 * b.number + i + 1)
                wait(act, s["out_ready"], 4 * b.number + i - 1)
                copy(o_hi[i % 2][:], pv[:]).then_inc(s["o_hi"], 1)

            def split_in(b):
                wait(act, s["x_tr"], b.number + 1)
                wait(act, s["pj_ready"], 6 * b.number)
                copy(in_hi[:].rearrange("p a n -> p (a n)"), tr[0][:]).then_inc(s["x_hi"], 1)

            def step(b, do_b=True, do_a=True, do_x=True, loading=False):
                a = b.plus(1)
                if do_a:
                    square(a, 0)
                if do_b:
                    exp(b, 0)
                if do_a:
                    values(a)
                if loading:
                    split_weights(3, 5)
                if do_a:
                    square(a, 1)
                if do_b:
                    exp(b, 1)
                    evacuate_p(b, 0)
                if do_a:
                    square(a, 2)
                if loading:
                    split_weights(5, 6)
                if do_b:
                    split_out(b, 0)
                    evacuate_p(b, 1)
                    exp(b, 2)
                if do_a:
                    evacuate_q(a, 0)
                    square(a, 3)
                if loading:
                    split_weights(6, 8)
                if do_b:
                    split_out(b, 1)
                    evacuate_p(b, 2)
                    exp(b, 3)
                if do_a:
                    evacuate_q(a, 1)
                    square(a, 4)
                if do_b:
                    split_out(b, 2)
                    evacuate_p(b, 3)
                if do_a:
                    evacuate_q(a, 2)
                if do_x:
                    split_in(b.plus(2))
                if do_b:
                    split_out(b, 3)
                if do_a:
                    evacuate_q(a, 3)

            act.wait_ge(s["aggr"], 1)
            act.wait_ge(s["eps_done"], 1)
            nc.scalar.activation(rstd[:], mv[:, :, 1], ACT.Sqrt, bias=eps[:, 0:1]).then_inc(s["sqrt_done"], 1)
            step(fixed(-2), do_b=False, do_a=False)
            split_weights(0, 3)
            step(fixed(-1), do_b=False, loading=True)
            split_weights(8, PIECES)
            for n in range(2):
                step(fixed(n))
            paired_loop(act, 2, B - 2, step)
            step(fixed(B - 2), do_x=False)
            step(fixed(B - 1), do_a=False, do_x=False)

        @block.gpsimd
        def _(pool):
            def settle():
                pool.nop(nofuse=True)

            def root(a, k):
                n = 5 * a.number + k
                cols = slice(4 * k, 4 * k + 4)
                wait(pool, s["ssq_done"], n + 1)
                settle()
                nc.gpsimd.tensor_scalar(ms[:, cols], ssq[:, cols], 1.0 / HD1, RMS_EPS, ALU.mult, ALU.add).then_inc(s["ms_done"], 1)
                wait(pool, s["ms_done"], n + 1)
                settle()
                nc.gpsimd.tensor_tensor(rms[:, cols], ms[:, cols], half_neg[:], ALU.pow).then_inc(s["rms_done"], 1)

            def norm(b, i):
                wait(pool, s["inv_done"], 4 * b.number + i + 1)
                settle()
                nc.gpsimd.tensor_tensor(heads(probs[i][:]), heads(probs[i][:]), spread(inv[:, 4 * i:4 * i + 4]),
                                        ALU.mult).then_inc(s["norm_done"], 1)

            def step(b, do_b=True, do_a=True):
                for i in range(4):
                    if do_a:
                        root(b.plus(1), i)
                    if do_b:
                        norm(b, i)
                if do_a:
                    root(b.plus(1), 4)

            pool.wait_ge(s["eps_done"], 2)
            step(fixed(-1), do_b=False)
            for n in range(2):
                step(fixed(n))
            paired_loop(pool, 2, B - 2, step)
            step(fixed(B - 2))
            step(fixed(B - 1), do_a=False)


HCH = FF // P


def bitlinear(nc, mem, shared, out):
    xres, gates, stats = shared["x"], shared["gates"], shared["stats"]
    ident_f = shared["ident"]

    def sb(name, shape, dt=F32):
        return mem.enter_context(nc.sbuf_tensor("d_" + name, shape, dt))

    def ps(name, cols, dt=F32):
        return mem.enter_context(nc.psum_tensor("d_" + name, [P, cols], dt))

    wq = shared["bit_w"]
    wmean = shared["bit_mean"]
    ident = sb("ident", [P, P], BF16)
    eps = sb("eps", [P, 2])
    half_neg = sb("half_neg", [P, 1])
    magic = sb("magic", [P, 1])
    mv = sb("mv", [P, B, 2])
    rstd = sb("rstd", [P, B])
    rms = sb("rms", [P, B])
    mean = sb("mean", [P, B])
    xs = sb("xs", [P, D])
    amax = sb("amax", [P, B])
    qs = sb("qs", [P, B])
    unit = sb("unit", [P, B])
    gate_a = sb("gate_a", [P, B])
    up_a = sb("up_a", [P, B])
    down_a = sb("down_a", [P, B])
    xq = sb("xq", [P, B, D], BF16)
    xq_t = [sb(f"xq_t{i}", [P, 2, P], BF16) for i in range(2)]
    sg = [sb(f"sg{i}", [P, FF]) for i in range(2)]
    h = [sb(f"h{i}", [P, FF]) for i in range(2)]
    hs = sb("hs", [P, FF])
    sq = sb("sq", [P, FF])
    ssq = sb("ssq", [P, 2])
    hms = sb("hms", [P, 2])
    hr = sb("hr", [P, 2])
    hmax = sb("hmax", [P, B])
    hunit = sb("hunit", [P, B])
    hqs = sb("hqs", [P, B])
    hq = [sb(f"hq{i}", [P, FF], BF16) for i in range(2)]
    hq_t = [sb(f"hq_t{i}", [P, FF], BF16) for i in range(2)]

    g_ps = ps("g", FF)
    u_ps = ps("u", FF)
    h_tr = ps("h_tr", FF, BF16)
    x_tr = ps("x_tr", 2 * P, BF16)
    y_ps = ps("y", 512)

    DVE_ROUNDS, ROUND_STEPS = 2, 3

    names = """set_done aggr sqrt_done x_chain square_done xq_done xq_steps rq_done w_chain xt_ready xt_read
        g_ready u_ready silu_done h_done sq_done max_done ms_done pow_done h_chain hs_done hq_done
        ht_ready ht_read y_ready x_done stored""".split()
    s = {n: shared["semaphores"].enter_context(nc.semaphore("d_" + n)) for n in names}

    with nc.Block() as block:

        @block.sync
        def _(sp):
            def store(b):
                wait(sp, s["x_done"], b.number + 1)
                sp.dma_start(out[b.number], xres[:, b.number, :]).then_inc(s["stored"], 16)
            for n in range(2):
                store(fixed(n))
            paired_loop(sp, 2, B, store)
            sp.wait_ge(s["stored"], 16 * B)

        @block.tensor
        def _(pe):
            def transpose_x(b):
                wait(pe, s["xq_done"], b.number + 1)
                wait(pe, s["xt_read"], b.number)
                for kc in range(2):
                    last = nc.tensor.transpose(x_tr[:, kc * P:(kc + 1) * P], xq[:, b.number, kc * P:(kc + 1) * P], ident[:])
                last.then_inc(s["xt_ready"], 1)

            def gate_up(b):
                wait(pe, s["xt_read"], b.number + 1)
                for half in range(2):
                    for i, (bank, free, ready) in enumerate(((g_ps, "silu_done", "g_ready"), (u_ps, "h_done", "u_ready"))):
                        wait(pe, s[free], 2 * b.number + half - 1)
                        for kc in range(2):
                            last = nc.tensor.matmul(bank[:, half * 512:(half + 1) * 512], xq_t[b.parity][:, kc, :],
                                                    wq[i][:, kc * FF + half * 512:kc * FF + (half + 1) * 512],
                                                    start=kc == 0, stop=kc == 1)
                        last.then_inc(s[ready], 1)

            def transpose_h(b):
                wait(pe, s["hq_done"], b.number + 1)
                wait(pe, s["ht_read"], b.number)
                for c in range(HCH):
                    last = nc.tensor.transpose(h_tr[:, c * P:(c + 1) * P], hq[b.parity][:, c * P:(c + 1) * P], ident[:])
                last.then_inc(s["ht_ready"], 1)

            def down(b):
                wait(pe, s["ht_read"], b.number + 1)
                wait(pe, s["x_done"], b.number)
                for c in range(HCH):
                    last = nc.tensor.matmul(y_ps[:, 0:D], hq_t[b.parity][:, c * P:(c + 1) * P], wq[2][:, c * D:(c + 1) * D],
                                            start=c == 0, stop=c == HCH - 1)
                last.then_inc(s["y_ready"], 1)

            def step(b, one=True, two=True, behind=2):
                if one:
                    gate_up(b.plus(1))
                if two:
                    transpose_x(b.plus(2))
                if behind > 1:
                    down(b.plus(-2))
                if behind > 0:
                    transpose_h(b.plus(-1))

            pe.wait_ge(s["set_done"], 5)
            transpose_x(fixed(0))
            gate_up(fixed(0))
            transpose_x(fixed(1))
            for n in range(4):
                step(fixed(n), behind=n)
            paired_loop(pe, 4, B - 2, step)
            step(fixed(B - 2), two=False)
            step(fixed(B - 1), one=False, two=False)
            down(fixed(B - 2))
            transpose_h(fixed(B - 1))
            down(fixed(B - 1))

        @block.vector
        def _(dve):
            col = lambda t, b: t[:, bass.ds(b.number, 1)]

            nc.vector.memset(eps[:, 0:1], LN_EPS).then_inc(s["set_done"], 1)
            nc.vector.memset(eps[:, 1:2], RMS_EPS).then_inc(s["set_done"], 1)
            nc.vector.memset(half_neg[:], -0.5).then_inc(s["set_done"], 1)
            nc.vector.memset(magic[:, 0:1], ROUND).then_inc(s["set_done"], 1)
            nc.vector.tensor_copy(ident[:], ident_f[:]).then_inc(s["set_done"], 1)
            for b in range(B):
                last = nc.vector.bn_aggr(mv[:, b, :], stats[:, b, :])
            last.then_inc(s["aggr"], 1)
            steps = 0

            def chain(instruction):
                nonlocal steps
                steps += 1
                instruction.then_inc(s["x_chain"], 1)
                dve.wait_ge(s["x_chain"], steps)

            tt, ts = nc.vector.tensor_tensor, nc.vector.tensor_scalar
            dve.wait_ge(s["aggr"], 1)
            chain(ts(mean[:], mv[:, :, 0], 1.0, None, ALU.mult))
            chain(tt(amax[:], shared["row_max"][:], mean[:], ALU.subtract))
            chain(tt(unit[:], mean[:], shared["row_min"][:], ALU.subtract))
            chain(tt(amax[:], amax[:], unit[:], ALU.max))
            dve.wait_ge(s["sqrt_done"], 1)
            chain(nc.vector.reciprocal(rstd[:], rstd[:]))
            chain(tt(rms[:], rstd[:], rstd[:], ALU.mult))
            tt(rms[:], rms[:], mv[:, :, 1], ALU.mult).then_inc(s["square_done"], 1)
            chain(tt(amax[:], amax[:], rstd[:], ALU.mult))
            dve.wait_ge(s["sqrt_done"], 2)
            chain(nc.vector.reciprocal(rms[:], rms[:]))
            chain(tt(amax[:], amax[:], rms[:], ALU.mult))
            chain(ts(unit[:], amax[:], Q_EPS, 1.0 / 127, ALU.max, ALU.mult))
            chain(nc.vector.reciprocal(qs[:], unit[:]))
            chain(tt(amax[:], rms[:], rstd[:], ALU.mult))
            tt(amax[:], amax[:], qs[:], ALU.mult).then_inc(s["rq_done"], 1)
            dve.wait_ge(s["rq_done"], 1)
            for b in range(DVE_ROUNDS):
                part = hs[:, b * D:(b + 1) * D]
                ts(part, xres[:, b, :], mean[:, b:b + 1], amax[:, b:b + 1],
                   ALU.subtract, ALU.mult).then_inc(s["xq_steps"], ROUND_STEPS)
                dve.wait_ge(s["xq_steps"], ROUND_STEPS * (b + 1))
                ts(xq[:, b, :], part, ROUND, ROUND, ALU.add, ALU.subtract).then_inc(s["xq_done"], 1)
            nc.vector.tensor_scalar(gate_a[:], unit[:], wmean[:, 0:1], None, ALU.mult).then_inc(s["w_chain"], 1)
            nc.vector.tensor_scalar(up_a[:], unit[:], wmean[:, 1:2], None, ALU.mult).then_inc(s["w_chain"], 1)
            dve.wait_ge(s["w_chain"], 2)

            def product(b):
                wait(dve, s["sq_done"], b.number - 1)
                for half in range(2):
                    cols = slice(half * 512, (half + 1) * 512)
                    wait(dve, s["silu_done"], 2 * b.number + half + 1)
                    wait(dve, s["u_ready"], 2 * b.number + half + 1)
                    nc.vector.scalar_tensor_tensor(h[b.parity][:, cols], u_ps[:, cols], col(up_a, b), sg[b.parity][:, cols],
                                                   ALU.mult, ALU.mult).then_inc(s["h_done"], 1)

            def largest(b):
                wait(dve, s["h_done"], 2 * b.number + 2)
                nc.vector.tensor_reduce(col(hmax, b), h[b.parity][:], AX.X, ALU.max,
                                        apply_absolute_value=True).then_inc(s["max_done"], 1)

            def scales(b):
                n = b.number
                wait(dve, s["pow_done"], n + 1)
                wait(dve, s["max_done"], n + 1)
                nc.vector.tensor_scalar(col(hmax, b), col(hmax, b), hr[:, b.parity:b.parity + 1], Q_EPS, ALU.mult, ALU.max).then_inc(s["h_chain"], 1)
                wait(dve, s["h_chain"], 4 * n + 1)
                nc.vector.tensor_scalar(col(hunit, b), col(hmax, b), 1.0 / 127, None, ALU.mult).then_inc(s["h_chain"], 1)
                wait(dve, s["h_chain"], 4 * n + 2)
                nc.vector.reciprocal(col(hqs, b), col(hunit, b)).then_inc(s["h_chain"], 1)
                nc.vector.tensor_scalar(col(down_a, b), col(hunit, b), wmean[:, 2:3], gates[:, 3:4],
                                        ALU.mult, ALU.mult).then_inc(s["h_chain"], 1)

            def quantise(b):
                wait(dve, s["h_chain"], 4 * b.number + 4)
                wait(dve, s["hq_done"], b.number)
                nc.vector.tensor_scalar(hs[:], h[b.parity][:], hr[:, b.parity:b.parity + 1], col(hqs, b),
                                        ALU.mult, ALU.mult).then_inc(s["hs_done"], 1)
                wait(dve, s["hs_done"], b.number + 1)
                wait(dve, s["ht_ready"], b.number - 1)
                nc.vector.tensor_scalar(hq[b.parity][:], hs[:], ROUND, ROUND, ALU.add, ALU.subtract).then_inc(s["hq_done"], 1)

            def add_y(b):
                wait(dve, s["y_ready"], b.number + 1)
                nc.vector.scalar_tensor_tensor(xres[:, b.number, :], y_ps[:, 0:D], col(down_a, b), xres[:, b.number, :],
                                               ALU.mult, ALU.add).then_inc(s["x_done"], 1)

            def step(b, one=True, behind=2):
                if one:
                    product(b.plus(1))
                scales(b)
                quantise(b)
                if one:
                    largest(b.plus(1))
                if behind > 1:
                    add_y(b.plus(-2))

            product(fixed(0))
            largest(fixed(0))
            for n in range(2):
                step(fixed(n), behind=n)
            paired_loop(dve, 2, B - 2, step)
            step(fixed(B - 2))
            step(fixed(B - 1), one=False)
            for n in range(B - 2, B):
                add_y(fixed(n))

        @block.scalar
        def _(act):
            def evacuate_x(b):
                wait(act, s["xt_ready"], b.number + 1)
                wait(act, s["u_ready"], 2 * (b.number - 1))
                nc.scalar.activation(xq_t[b.parity][:].rearrange("p a n -> p (a n)"), x_tr[:],
                                     ACT.Copy).then_inc(s["xt_read"], 1)

            def silu(b):
                wait(act, s["h_done"], 2 * (b.number - 1))
                for half in range(2):
                    cols = slice(half * 512, (half + 1) * 512)
                    wait(act, s["g_ready"], 2 * b.number + half + 1)
                    act.nop(nofuse=True)
                    nc.scalar.activation(sg[b.parity][:, cols], g_ps[:, cols], ACT.Silu,
                                         scale=gate_a[:, bass.ds(b.number, 1)]).then_inc(s["silu_done"], 1)

            def square(b):
                wait(act, s["h_done"], 2 * b.number + 2)
                wait(act, s["sq_done"], b.number)
                nc.scalar.activation(sq[:], h[b.parity][:], ACT.Square,
                                     accum_out=ssq[:, b.parity:b.parity + 1]).then_inc(s["sq_done"], 1)

            def evacuate_h(b):
                wait(act, s["ht_ready"], b.number + 1)
                wait(act, s["y_ready"], b.number - 1)
                nc.scalar.activation(hq_t[b.parity][:], h_tr[:], ACT.Copy).then_inc(s["ht_read"], 1)

            act.wait_ge(s["aggr"], 1)
            act.wait_ge(s["set_done"], 2)
            nc.scalar.activation(rstd[:], mv[:, :, 1], ACT.Sqrt, bias=eps[:, 0:1]).then_inc(s["sqrt_done"], 1)
            act.wait_ge(s["square_done"], 1)
            nc.scalar.activation(rms[:], rms[:], ACT.Sqrt, bias=eps[:, 1:2]).then_inc(s["sqrt_done"], 1)
            evacuate_x(fixed(0))
            act.wait_ge(s["w_chain"], 1)
            silu(fixed(0))
            evacuate_x(fixed(1))
            square(fixed(0))

            def step(b, one=True, two=True, behind=2):
                if one:
                    silu(b.plus(1))
                if two:
                    evacuate_x(b.plus(2))
                if behind > 0:
                    evacuate_h(b.plus(-1))
                if one:
                    square(b.plus(1))
            for n in range(4):
                step(fixed(n), behind=n)
            paired_loop(act, 4, B - 2, step)
            step(fixed(B - 2), two=False)
            step(fixed(B - 1), one=False, two=False)
            evacuate_h(fixed(B - 1))

        @block.gpsimd
        def _(pool):
            wide = [P, D]

            def settle():
                pool.nop(nofuse=True)

            def round_x(b):
                column = bass.ds(b.number, 1)
                row = xs[:]
                wait(pool, s["xq_done"], b.number)
                settle()
                nc.gpsimd.tensor_tensor(row, xres[:, b.number, :], mean[:, column].broadcast_to(wide),
                                        ALU.subtract).then_inc(s["xq_steps"], 1)
                wait(pool, s["xq_steps"], ROUND_STEPS * b.number + 1)
                settle()
                nc.gpsimd.tensor_tensor(row, row, amax[:, bass.ds(b.number, 1)].broadcast_to(wide),
                                        ALU.mult).then_inc(s["xq_steps"], 1)
                wait(pool, s["xq_steps"], ROUND_STEPS * b.number + 2)
                settle()
                nc.gpsimd.tensor_tensor(row, row, magic[:].broadcast_to(wide), ALU.add).then_inc(s["xq_steps"], 1)
                wait(pool, s["xq_steps"], ROUND_STEPS * b.number + 3)
                settle()
                nc.gpsimd.tensor_tensor(xq[:, b.number, :], row, magic[:].broadcast_to(wide),
                                        ALU.subtract).then_inc(s["xq_done"], 1)

            def inverse_root(b):
                wait(pool, s["sq_done"], b.number + 1)
                settle()
                at = slice(b.parity, b.parity + 1)
                nc.gpsimd.tensor_scalar(hms[:, at], ssq[:, at], 1.0 / FF, RMS_EPS, ALU.mult, ALU.add).then_inc(s["ms_done"], 1)
                wait(pool, s["ms_done"], b.number + 1)
                settle()
                nc.gpsimd.tensor_tensor(hr[:, at], hms[:, at], half_neg[:, 0:1], ALU.pow).then_inc(s["pow_done"], 1)

            def step(b):
                inverse_root(b)
                round_x(b.plus(AHEAD))

            AHEAD = 4
            pool.wait_ge(s["set_done"], 5)
            pool.wait_ge(s["rq_done"], 1)
            for n in range(DVE_ROUNDS, AHEAD):
                round_x(fixed(n))
            paired_loop(pool, 0, B - AHEAD, step)
            for n in range(B - AHEAD, B):
                inverse_root(fixed(n))


def program(nc, x, ctx, mask, mask_col, gates, wq0, wk0, wv0, bq0, bk0, bv0, consts, ident,
            mix_w, router, select, rank, att_w, norm_w, bit_w, out):
    with ExitStack() as kept:
        def sb(name, shape):
            return kept.enter_context(nc.sbuf_tensor(name, shape, F32))

        shared = {"x": sb("x", [S, B, D]),
                  "stats": sb("stats", [S, B, 6]),
                  "row_max": sb("row_max", [S, B]), "row_min": sb("row_min", [S, B]),
                  "ident": sb("ident", [P, P]), "gates": sb("gates", [P, 4]), "ident_dram": ident,
                  "gates_dram": gates, "mask_col_dram": mask_col, "bit_dram": bit_w, "semaphores": kept,
                  "stage": sb("stage", [P, STAGE_COLS]), "mix_dram": mix_w, "att_dram": att_w,
                  "mix_staged": [kept.enter_context(nc.semaphore(f"mix_staged{i}")) for i in range(M_STAGES)],
                  "att_staged": [kept.enter_context(nc.semaphore(f"att_staged{i}")) for i in range(C_STAGES)],
                  "bit_mean": sb("bit_mean", [P, 3]),
                  "bit_w": [kept.enter_context(nc.sbuf_tensor(f"bit_w{i}", [P, 2 * FF], BF16)) for i in range(3)]}
        with ExitStack() as mem:
            attention0(nc, mem, shared, x, ctx, mask, wq0, wk0, wv0, bq0, bk0, bv0, consts)
        with ExitStack() as mem:
            mixture(nc, mem, shared, mix_w, router, select, rank)
        with ExitStack() as mem:
            attention1(nc, mem, shared, att_w, norm_w, ctx)
        with ExitStack() as mem:
            bitlinear(nc, mem, shared, out)


def attention0_consts():
    c = np.zeros((P, CONST_COLS), np.float32)
    for head in range(GH):
        for quadrant in range(3):
            c[32 * quadrant + HD0 * head:32 * quadrant + HD0 * (head + 1), head] = 1
        c[96 + head:96 + HEADS0:GH, head] = 1
        c[112:116, head] = 1
    c[112:114, 4], c[112:116, 5] = -1, 1
    c[114, 6], c[115, 6] = NEG_HI, NEG_LO
    for group in range(GROUPS):
        c[96 + GH * group:96 + GH * (group + 1), 7 + group] = 1
        c[[112, 114], 7 + group], c[[113, 115], 7 + group] = -NEG_HI, -NEG_LO
    return c


def expert_rows(expert, shared_expert):
    rows = np.zeros((CHUNKS * P, D), np.float32)
    n = expert.shape[0] * expert.shape[1]
    rows[:n] = expert.reshape(n, D)
    rows[n:n + shared_expert.shape[0]] = shared_expert
    return rows


def pack_mixture(gate_up, down, sh_gate, sh_up, sh_down):
    inner = gate_up.shape[1] // 2
    parts = []
    for expert, one in ((gate_up[:, :inner], sh_gate), (gate_up[:, inner:], sh_up)):
        rows = expert_rows(expert, one)
        parts.append(rows.reshape(CHUNKS, P, 2, P).transpose(0, 3, 2, 1).reshape(CHUNKS, P, D))
    parts.append(expert_rows(down.transpose(0, 2, 1), sh_down.T).reshape(CHUNKS, P, D))
    return np.concatenate(parts, axis=2)


def select_matrix(inner, shared_inner):
    owner = np.concatenate([np.repeat(np.arange(EXPERTS), inner), np.full(shared_inner, EXPERTS)])
    select = np.zeros((SEL_ROWS, CHUNKS * P), np.float32)
    rows = np.arange(owner.size)
    select[owner, rows] = 1
    select[SEL_ROWS // 2 + owner, rows] = 1
    return select


def pack_attention1(wk, wv, wq, wo):
    halves = slice(0, P), slice(P, D)
    pieces = [np.concatenate([wk[h], wv[h]], axis=1) for h in halves]
    pieces += [wq[h][:, c * 1024:(c + 1) * 1024] for c in range(2) for h in halves]
    pieces += list(wo.reshape(KV, HPK, HD1, D).transpose(0, 2, 1, 3).reshape(KV, HD1, HPK * D))
    return np.stack(pieces)


def pack_bitlinear(*weights):
    return np.stack([w.T.reshape(w.shape[1] // P, P, w.shape[0]).transpose(1, 0, 2).reshape(P, -1) for w in weights])


def kernel(**inputs):
    import concourse.bacc as bacc
    from concourse.bass_utils import run_bass_kernel_spmd

    a = {name: np.asarray(value) for name, value in inputs.items()}
    mask = a["mask_Bx1x2048_fk1"]
    l0 = {n: a["L0_ffn_" + n] for n in ("gate_up_proj", "down_proj", "sh_gate_w", "sh_up_w", "sh_down_w")}
    router = np.concatenate([a["L0_ffn_router_weight"], a["L0_ffn_shared_gate_w"]])
    layout = {
        "x": a["x"], "ctx": a["ctx_2048"], "mask": mask,
        "mask_col": mask.reshape(B, 2, P).transpose(2, 0, 1),
        "gates": np.concatenate([a["g_xattn"], a["g_ffn"]]).reshape(1, 4),
        "wq0": a["L0_xattn_Wq"].T, "wk0": a["L0_xattn_Wk"].T, "wv0": a["L0_xattn_Wv"].T,
        "bq0": a["L0_xattn_bq"].reshape(P, 1), "bk0": a["L0_xattn_bk"].reshape(P, 1),
        "bv0": a["L0_xattn_bv"].reshape(1, P),
        "consts": attention0_consts(), "ident": np.eye(P, dtype=np.float32),
        "mix_w": pack_mixture(*l0.values()),
        "router": router.T.reshape(2, P, EXPERTS + 1).transpose(1, 0, 2),
        "select": select_matrix(l0["gate_up_proj"].shape[1] // 2, l0["sh_gate_w"].shape[0]),
        "rank": np.tile(np.arange(EXPERTS, 0, -1, dtype=np.float32), (P, TILES, 1)),
        "att_w": pack_attention1(*(a["L1_xattn_" + n] for n in ("Wk", "Wv", "Wq", "Wo"))),
        "norm_w": np.stack([a["L1_xattn_q_norm_w"], a["L1_xattn_k_norm_w"]], axis=1),
        "bit_w": pack_bitlinear(*(a["L1_ffn_" + n] for n in ("w_gate", "w_up", "w_down"))),
    }
    nc = bacc.Bacc("TRN2", target_bir_lowering=False, num_devices=1)
    arrays, args = {}, []
    for name, value in layout.items():
        value = np.ascontiguousarray(value)
        arrays[f"in_{name}_dram"] = value
        args.append(nc.dram_tensor(f"in_{name}_dram", value.shape, mybir.dt.from_np(value.dtype),
                                   kind="ExternalInput").ap())
    args.append(nc.dram_tensor("out_0_dram", (B, S, D), F32, kind="ExternalOutput").ap())
    program(nc, *args)
    r = run_bass_kernel_spmd(nc, [arrays], core_ids=[0])
    return r.results[0]["out_0_dram"]
```
